# Optimizing a Trainium2 kernel written in Bass

```python
import numpy as np
import jax
import jax.numpy as jnp

def _softmax(x, axis=-1):
    return jax.nn.softmax(x, axis=axis)

def _gelu(x):
    return jax.nn.gelu(x, approximate=True)

def _silu(x):
    return jax.nn.silu(x)

def _sigmoid(x):
    return jax.nn.sigmoid(x)

def _layernorm(x, axis=-1, eps=1e-05):
    m = jnp.mean(x, axis=axis, keepdims=True)
    v = jnp.var(x, axis=axis, keepdims=True)
    return (x - m) / jnp.sqrt(v + eps)

def _scatter_add(tgt, idx, src, axis=0):
    return tgt.at[idx].add(src)

def _segment_sum(src, seg, n):
    return jax.ops.segment_sum(src, seg, n)
kernel_name = 'mk_gps_d2_gnn_r32_e0647e'

def setup_inputs(seed: int=0):
    np.random.seed(seed)
    _w = jnp.asarray

    def _rec_inputs():
        import jax
        import jax.numpy as jnp
        _gk = jax.random.key(seed)
        x = -0.000364 + 1 * jax.random.normal(jax.random.fold_in(_gk, 1), (625, 768), jnp.float32)
        _s = jax.random.randint(jax.random.fold_in(_gk, 2), (10000,), 0, 625, jnp.int32)
        _d = jax.random.randint(jax.random.fold_in(_gk, 3), (10000,), 0, 625, jnp.int32)
        _loop = jnp.arange(625, dtype=jnp.int32)
        src = jnp.concatenate([_s, _d, _loop])
        dst = jnp.concatenate([_d, _s, _loop])
        _o = jnp.argsort(dst, stable=True)
        src = src[_o]
        dst = dst[_o]
        return (x, src, dst)
    x, src, dst = _rec_inputs()

    def _L0_gnn_setup():
        import jax, jax.numpy as jnp
        import numpy as np
        N = 625
        E = 10000
        D = 768
        H = 4
        C = D // H
        NEG_SLOPE = 0.2

        def gat_layer(x, src, dst, W, a_src, a_dst, b):
            h = (x @ W).reshape(-1, H, C)
            as_ = jnp.sum(h * a_src, axis=-1)
            ad_ = jnp.sum(h * a_dst, axis=-1)
            e = jax.nn.leaky_relu(as_[src] + ad_[dst], NEG_SLOPE)
            m = jax.ops.segment_max(e, dst, num_segments=N)
            e = jnp.exp(e - m[dst])
            s = jax.ops.segment_sum(e, dst, num_segments=N)
            alpha = e / s[dst]
            msg = h[src] * alpha[:, :, None]
            out = jax.ops.segment_sum(msg, dst, num_segments=N)
            return out.reshape(-1, H * C) + b
        key = jax.random.key(seed)
        ks = jax.random.split(key, 10)
        x = jax.random.normal(ks[0], (N, D), dtype=jnp.float32)
        edge_index = jax.random.randint(ks[1], (2, E), 0, N, dtype=jnp.int64)
        sc = 0.05
        W1 = jax.random.normal(ks[2], (D, H * C), dtype=jnp.float32) * sc
        a_src1 = jax.random.normal(ks[3], (H, C), dtype=jnp.float32) * sc
        a_dst1 = jax.random.normal(ks[4], (H, C), dtype=jnp.float32) * sc
        b1 = jnp.zeros((H * C,), dtype=jnp.float32)
        W2 = jax.random.normal(ks[5], (H * C, H * C), dtype=jnp.float32) * sc
        a_src2 = jax.random.normal(ks[6], (H, C), dtype=jnp.float32) * sc
        a_dst2 = jax.random.normal(ks[7], (H, C), dtype=jnp.float32) * sc
        b2 = jnp.zeros((H * C,), dtype=jnp.float32)
        return {'x': x, 'edge_index': edge_index, 'W1': W1, 'a_src1': a_src1, 'a_dst1': a_dst1, 'b1': b1, 'W2': W2, 'a_src2': a_src2, 'a_dst2': a_dst2, 'b2': b2}
    _L0_gnn_all = _L0_gnn_setup()
    _L0_gnn_in = {k: v for k, v in _L0_gnn_all.items() if k in ('W1', 'a_src1', 'a_dst1', 'b1', 'W2', 'a_src2', 'a_dst2', 'b2')}
    del _L0_gnn_all

    def _L0_mix_setup():
        import jax, jax.numpy as jnp
        import numpy as np
        EPS = 1e-06
        H = 12

        def _phi(x):
            return jax.nn.elu(x) + 1.0
        key = jax.random.key(seed)
        k1, k2, k3 = jax.random.split(key, 3)
        B, N, D = (32, 1024, 768)
        x = jax.random.normal(k1, (B, N, D), dtype=jnp.float32)
        W_qkv = jax.random.normal(k2, (D, 3 * D), dtype=jnp.float32) * D ** (-0.5)
        W_out = jax.random.normal(k3, (D, D), dtype=jnp.float32) * D ** (-0.5)
        b_out = jnp.zeros((D,), dtype=jnp.float32)
        return {'x': x, 'W_qkv': W_qkv, 'W_out': W_out, 'b_out': b_out}
    _L0_mix_all = _L0_mix_setup()
    _L0_mix_in = {k: v for k, v in _L0_mix_all.items() if k in ('W_qkv', 'W_out', 'b_out')}
    del _L0_mix_all

    def _L0_ffn_setup():
        import jax, jax.numpy as jnp
        import numpy as np
        N_EMBD = 768
        EXPERT_SIZES = [(8, 512), (8, 1024)]
        TOP_K = 8
        NORM_TOPK_PROB = True
        EXPERT_WIDTHS = []
        for cnt, w in EXPERT_SIZES:
            EXPERT_WIDTHS += [w] * cnt
        EXPERT_OFFSETS = np.concatenate([[0], np.cumsum(EXPERT_WIDTHS)]).astype(np.int64)
        NUM_EXPERTS = len(EXPERT_WIDTHS)
        TOTAL_WIDTH = int(EXPERT_OFFSETS[-1])
        key = jax.random.key(seed)
        k1, k2, k3, k4 = jax.random.split(key, 4)
        x = jax.random.normal(k1, (1, 64, N_EMBD), dtype=jnp.float32)
        router_w = jax.random.normal(k2, (NUM_EXPERTS, N_EMBD), dtype=jnp.float32) * 0.02
        w1 = jnp.clip(jax.random.normal(k3, (N_EMBD, TOTAL_WIDTH), dtype=jnp.float32) * 0.02, -0.06, 0.06)
        w2 = jnp.clip(jax.random.normal(k4, (TOTAL_WIDTH, N_EMBD), dtype=jnp.float32) * 0.02, -0.06, 0.06)
        return {'x': x, 'router_w': router_w, 'w1': w1, 'w2': w2}
    _L0_ffn_all = _L0_ffn_setup()
    _L0_ffn_in = {k: v for k, v in _L0_ffn_all.items() if k in ('router_w', 'w1', 'w2')}
    del _L0_ffn_all

    def _L1_gnn_setup():
        import jax, jax.numpy as jnp
        import numpy as np
        N = 625
        DEG = 16
        E = N * DEG
        H = 12
        DIN = 64
        DOUT = 64
        NEG_SLOPE = 0.2
        key = jax.random.key(seed)
        k_h, k_src, k_w, k_al, k_ar, k_wr = jax.random.split(key, 6)
        std = 1.414 * np.sqrt(2.0 / (DIN + DOUT))
        h = jax.random.normal(k_h, (N, H * DIN), dtype=jnp.float32)
        src = jax.random.randint(k_src, (E,), 0, N, dtype=jnp.int64)
        dst = jnp.repeat(jnp.arange(N, dtype=jnp.int64), DEG)
        W = jax.random.normal(k_w, (DOUT, DIN), dtype=jnp.float32) * std
        attn_l = jax.random.normal(k_al, (1, H, DOUT), dtype=jnp.float32) * std
        attn_r = jax.random.normal(k_ar, (1, H, DOUT), dtype=jnp.float32) * std
        W_res = jax.random.normal(k_wr, (DOUT, DIN), dtype=jnp.float32) * std
        return {'h': h, 'src': src, 'dst': dst, 'W': W, 'attn_l': attn_l, 'attn_r': attn_r, 'W_res': W_res}
    _L1_gnn_all = _L1_gnn_setup()
    _L1_gnn_in = {k: v for k, v in _L1_gnn_all.items() if k in ('W', 'attn_l', 'attn_r', 'W_res')}
    del _L1_gnn_all

    def _L1_mix_setup():
        import jax, jax.numpy as jnp
        import numpy as np
        DIM = 768
        HEADS = 12
        DH = DIM // HEADS
        M = 256
        EPS = 0.0001

        def softmax_kernel(data, proj, is_query):
            data_normalizer = data.shape[-1] ** (-0.25)
            ratio = proj.shape[0] ** (-0.5)
            data_dash = jnp.einsum('bhsd,md->bhsm', data_normalizer * data, proj)
            diag = 0.5 * data_normalizer ** 2 * jnp.sum(data * data, axis=-1, keepdims=True)
            if is_query:
                stab = jnp.max(data_dash, axis=-1, keepdims=True)
            else:
                stab = jnp.max(data_dash, axis=(-2, -1), keepdims=True)
            stab = jax.lax.stop_gradient(stab)
            return ratio * (jnp.exp(data_dash - diag - stab) + EPS)
        key = jax.random.key(seed)
        kx, kq, kk, kv, ko, kp = jax.random.split(key, 6)
        B, S = (8, 128)
        w_scale = DIM ** (-0.5)
        return {'x': jax.random.normal(kx, (B, S, DIM), jnp.float32), 'Wq': jax.random.normal(kq, (DIM, DIM), jnp.float32) * w_scale, 'Wk': jax.random.normal(kk, (DIM, DIM), jnp.float32) * w_scale, 'Wv': jax.random.normal(kv, (DIM, DIM), jnp.float32) * w_scale, 'Wo': jax.random.normal(ko, (DIM, DIM), jnp.float32) * w_scale, 'proj': jax.random.normal(kp, (M, DH), jnp.float32)}
    _L1_mix_all = _L1_mix_setup()
    _L1_mix_in = {k: v for k, v in _L1_mix_all.items() if k in ('Wq', 'Wk', 'Wv', 'Wo', 'proj')}
    del _L1_mix_all

    def _L1_ffn_setup():
        import jax, jax.numpy as jnp
        import numpy as np
        from jax import lax
        H = 768
        I = 64
        E = 8
        K = 2
        key = jax.random.key(seed)
        k1, k2, k3, k4 = jax.random.split(key, 4)
        x = jax.random.normal(k1, (1, 1024, H), dtype=jnp.float32)
        router_w = jax.random.normal(k2, (E, H), dtype=jnp.float32) * (1.0 / np.sqrt(H))
        w1 = jax.random.normal(k3, (E, H, I), dtype=jnp.float32) * (1.0 / np.sqrt(H))
        w2 = jax.random.normal(k4, (E, I, H), dtype=jnp.float32) * (1.0 / np.sqrt(I))
        return {'x': x, 'router_w': router_w, 'w1': w1, 'w2': w2}
    _L1_ffn_all = _L1_ffn_setup()
    _L1_ffn_in = {k: v for k, v in _L1_ffn_all.items() if k in ('router_w', 'w1', 'w2')}
    del _L1_ffn_all
    return {'x': x, 'src': src, 'dst': dst, 'L0_gnn_W1': _L0_gnn_in['W1'], 'L0_gnn_a_src1': _L0_gnn_in['a_src1'], 'L0_gnn_a_dst1': _L0_gnn_in['a_dst1'], 'L0_gnn_b1': _L0_gnn_in['b1'], 'L0_gnn_W2': _L0_gnn_in['W2'], 'L0_gnn_a_src2': _L0_gnn_in['a_src2'], 'L0_gnn_a_dst2': _L0_gnn_in['a_dst2'], 'L0_gnn_b2': _L0_gnn_in['b2'], 'L0_mix_W_qkv': _L0_mix_in['W_qkv'], 'L0_mix_W_out': _L0_mix_in['W_out'], 'L0_mix_b_out': _L0_mix_in['b_out'], 'L0_ffn_router_w': _L0_ffn_in['router_w'], 'L0_ffn_w1': _L0_ffn_in['w1'], 'L0_ffn_w2': _L0_ffn_in['w2'], 'L1_gnn_W': _L1_gnn_in['W'], 'L1_gnn_attn_l': _L1_gnn_in['attn_l'], 'L1_gnn_attn_r': _L1_gnn_in['attn_r'], 'L1_gnn_W_res': _L1_gnn_in['W_res'], 'L1_mix_Wq': _L1_mix_in['Wq'], 'L1_mix_Wk': _L1_mix_in['Wk'], 'L1_mix_Wv': _L1_mix_in['Wv'], 'L1_mix_Wo': _L1_mix_in['Wo'], 'L1_mix_proj': _L1_mix_in['proj'], 'L1_ffn_router_w': _L1_ffn_in['router_w'], 'L1_ffn_w1': _L1_ffn_in['w1'], 'L1_ffn_w2': _L1_ffn_in['w2']}

def reference(x, src, dst, L0_gnn_W1, L0_gnn_a_src1, L0_gnn_a_dst1, L0_gnn_b1, L0_gnn_W2, L0_gnn_a_src2, L0_gnn_a_dst2, L0_gnn_b2, L0_mix_W_qkv, L0_mix_W_out, L0_mix_b_out, L0_ffn_router_w, L0_ffn_w1, L0_ffn_w2, L1_gnn_W, L1_gnn_attn_l, L1_gnn_attn_r, L1_gnn_W_res, L1_mix_Wq, L1_mix_Wk, L1_mix_Wv, L1_mix_Wo, L1_mix_proj, L1_ffn_router_w, L1_ffn_w1, L1_ffn_w2):
    import jax
    import jax.numpy as jnp

    def _L0_gnn_ref(x, edge_index, W1, a_src1, a_dst1, b1, W2, a_src2, a_dst2, b2):
        import jax, jax.numpy as jnp
        import numpy as np
        N = 625
        E = 10000
        D = 768
        H = 4
        C = D // H
        NEG_SLOPE = 0.2

        def gat_layer(x, src, dst, W, a_src, a_dst, b):
            h = (x @ W).reshape(-1, H, C)
            as_ = jnp.sum(h * a_src, axis=-1)
            ad_ = jnp.sum(h * a_dst, axis=-1)
            e = jax.nn.leaky_relu(as_[src] + ad_[dst], NEG_SLOPE)
            m = jax.ops.segment_max(e, dst, num_segments=N)
            e = jnp.exp(e - m[dst])
            s = jax.ops.segment_sum(e, dst, num_segments=N)
            alpha = e / s[dst]
            msg = h[src] * alpha[:, :, None]
            out = jax.ops.segment_sum(msg, dst, num_segments=N)
            return out.reshape(-1, H * C) + b
        loop = jnp.arange(N, dtype=edge_index.dtype)
        src = jnp.concatenate([edge_index[0], loop])
        dst = jnp.concatenate([edge_index[1], loop])
        h = gat_layer(x, src, dst, W1, a_src1, a_dst1, b1)
        h = jax.nn.relu(h)
        out = gat_layer(h, src, dst, W2, a_src2, a_dst2, b2)
        return out

    def _L0_mix_ref(x, W_qkv, W_out, b_out):
        import jax, jax.numpy as jnp
        import numpy as np
        EPS = 1e-06
        H = 12

        def _phi(x):
            return jax.nn.elu(x) + 1.0
        B, N, D = x.shape
        d = D // H
        x_ = jnp.pad(x, ((0, 0), (0, 1), (0, 0)))
        qkv = x_ @ W_qkv
        q, k, v = jnp.split(qkv, 3, axis=-1)
        q = q.reshape(B, N + 1, H, d)
        k = k.reshape(B, N + 1, H, d)
        v = v.reshape(B, N + 1, H, d)
        q = _phi(q)
        k = _phi(k)
        kv = jnp.einsum('bshd,bshm->bhdm', k, v)
        z = 1.0 / (jnp.einsum('blhd,bhd->blh', q, k.sum(axis=1)) + EPS)
        out = jnp.einsum('blhd,bhdm,blh->blhm', q, kv, z)
        out = out.reshape(B, N + 1, D)
        out = out @ W_out + b_out
        return out[:, :-1, :]

    def _L0_ffn_ref(x, router_w, w1, w2):
        import jax, jax.numpy as jnp
        import numpy as np
        N_EMBD = 768
        EXPERT_SIZES = [(8, 512), (8, 1024)]
        TOP_K = 8
        NORM_TOPK_PROB = True
        EXPERT_WIDTHS = []
        for cnt, w in EXPERT_SIZES:
            EXPERT_WIDTHS += [w] * cnt
        EXPERT_OFFSETS = np.concatenate([[0], np.cumsum(EXPERT_WIDTHS)]).astype(np.int64)
        NUM_EXPERTS = len(EXPERT_WIDTHS)
        TOTAL_WIDTH = int(EXPERT_OFFSETS[-1])
        B, S, D = x.shape
        xt = x.reshape(-1, D)
        T = xt.shape[0]
        logits = jnp.einsum('td,ed->te', xt, router_w)
        probs = jax.nn.softmax(logits, axis=-1)
        topk_w, topk_idx = jax.lax.top_k(probs, TOP_K)
        if NORM_TOPK_PROB:
            topk_w = topk_w / jnp.sum(topk_w, axis=-1, keepdims=True)
        comb = jnp.zeros((T, NUM_EXPERTS), dtype=xt.dtype)
        comb = comb.at[jnp.arange(T)[:, None], topk_idx].add(topk_w)
        out = jnp.zeros_like(xt)
        for e in range(NUM_EXPERTS):
            off = int(EXPERT_OFFSETS[e])
            wd = EXPERT_WIDTHS[e]
            h = jax.nn.gelu(xt @ w1[:, off:off + wd])
            out = out + comb[:, e:e + 1] * (h @ w2[off:off + wd, :])
        return out.reshape(B, S, D)

    def _L1_gnn_ref(h, src, dst, W, attn_l, attn_r, W_res):
        import jax, jax.numpy as jnp
        import numpy as np
        N = 625
        DEG = 16
        E = N * DEG
        H = 12
        DIN = 64
        DOUT = 64
        NEG_SLOPE = 0.2
        n = h.shape[0]
        hv = h.reshape(n, H, DIN)
        ft = jnp.einsum('nhd,od->nho', hv, W)
        a1 = jnp.sum(ft * attn_l, axis=-1)
        a2 = jnp.sum(ft * attn_r, axis=-1)
        e = jax.nn.leaky_relu(a1[src] + a2[dst], negative_slope=NEG_SLOPE)
        m = jax.ops.segment_max(e, dst, num_segments=n)
        m = jnp.where(jnp.isfinite(m), m, 0.0)
        w = jnp.exp(e - m[dst])
        denom = jax.ops.segment_sum(w, dst, num_segments=n)
        alpha = w / jnp.maximum(denom[dst], 1e-16)
        msg = alpha[:, :, None] * ft[src]
        agg = jax.ops.segment_sum(msg, dst, num_segments=n)
        res = jnp.einsum('nhd,od->nho', hv, W_res)
        out = jax.nn.relu((agg + res).reshape(n, H * DOUT))
        return out

    def _L1_mix_ref(x, Wq, Wk, Wv, Wo, proj):
        import jax, jax.numpy as jnp
        import numpy as np
        DIM = 768
        HEADS = 12
        DH = DIM // HEADS
        M = 256
        EPS = 0.0001

        def softmax_kernel(data, proj, is_query):
            data_normalizer = data.shape[-1] ** (-0.25)
            ratio = proj.shape[0] ** (-0.5)
            data_dash = jnp.einsum('bhsd,md->bhsm', data_normalizer * data, proj)
            diag = 0.5 * data_normalizer ** 2 * jnp.sum(data * data, axis=-1, keepdims=True)
            if is_query:
                stab = jnp.max(data_dash, axis=-1, keepdims=True)
            else:
                stab = jnp.max(data_dash, axis=(-2, -1), keepdims=True)
            stab = jax.lax.stop_gradient(stab)
            return ratio * (jnp.exp(data_dash - diag - stab) + EPS)
        B, S, _ = x.shape

        def split_heads(t):
            return t.reshape(B, S, HEADS, DH).transpose(0, 2, 1, 3)
        q = split_heads(x @ Wq)
        k = split_heads(x @ Wk)
        v = split_heads(x @ Wv)
        qp = softmax_kernel(q, proj, is_query=True)
        kp = softmax_kernel(k, proj, is_query=False)
        k_sum = jnp.sum(kp, axis=2)
        d_inv = 1.0 / jnp.einsum('bhsm,bhm->bhs', qp, k_sum)
        ctx = jnp.einsum('bhsm,bhsd->bhmd', kp, v)
        out = jnp.einsum('bhsm,bhmd,bhs->bhsd', qp, ctx, d_inv)
        out = out.transpose(0, 2, 1, 3).reshape(B, S, DIM)
        return out @ Wo

    def _L1_ffn_ref(x, router_w, w1, w2):
        import jax, jax.numpy as jnp
        import numpy as np
        from jax import lax
        H = 768
        I = 64
        E = 8
        K = 2
        B, S, _ = x.shape
        xt = x.reshape(-1, H)
        logits = xt @ router_w.T
        probs = jax.nn.softmax(logits, axis=-1)
        top_w, top_i = lax.top_k(probs, K)
        top_w = top_w / jnp.sum(top_w, axis=-1, keepdims=True)
        e_sel = jnp.max(top_i, axis=-1)

        def step(out, inp):
            idx, W1e, W2e = inp
            y = jax.nn.silu(xt @ W1e) @ W2e
            mask = (e_sel == idx)[:, None]
            return (jnp.where(mask, y, out), None)
        out0 = jnp.zeros_like(xt)
        out, _ = lax.scan(step, out0, (jnp.arange(E), w1, w2))
        return out.reshape(B, S, H)
    edge_index = jnp.stack([src, dst])
    xn = _layernorm(x, axis=-1)
    x = x + _L0_gnn_ref(xn, edge_index, L0_gnn_W1, L0_gnn_a_src1, L0_gnn_a_dst1, L0_gnn_b1, L0_gnn_W2, L0_gnn_a_src2, L0_gnn_a_dst2, L0_gnn_b2) + _L0_mix_ref(xn[None], L0_mix_W_qkv, L0_mix_W_out, L0_mix_b_out)[0]
    x = x + _L0_ffn_ref(_layernorm(x, axis=-1)[None], L0_ffn_router_w, L0_ffn_w1, L0_ffn_w2)[0]
    xn = _layernorm(x, axis=-1)
    x = x + _L1_gnn_ref(xn, src, dst, L1_gnn_W, L1_gnn_attn_l, L1_gnn_attn_r, L1_gnn_W_res) + _L1_mix_ref(xn[None], L1_mix_Wq, L1_mix_Wk, L1_mix_Wv, L1_mix_Wo, L1_mix_proj)[0]
    x = x + _L1_ffn_ref(_layernorm(x, axis=-1)[None], L1_ffn_router_w, L1_ffn_w1, L1_ffn_w2)[0]
    return x

_drawn_inputs = setup_inputs


def setup_inputs(seed=0):
    import zlib

    import numpy as np

    out = dict(_drawn_inputs(seed))
    spreads = {'L0_gnn_b1': (0.0, 0.1), 'L0_gnn_b2': (0.0, 0.1), 'L0_mix_b_out': (0.0, 0.1)}
    factors = {}
    for name, (base, spread) in spreads.items():
        noise = np.random.default_rng([zlib.crc32(name.encode()), seed]).standard_normal(out[name].shape)
        drawn = base * np.exp(spread * noise) if base else spread * noise
        out[name] = jnp.asarray(drawn.astype(out[name].dtype))
    for name, factor in factors.items():
        out[name] = (out[name] * factor).astype(out[name].dtype)
    return out
```

```python
import numpy as np
import concourse.bass as bass
from concourse import mybir

FP32 = mybir.dt.float32
FP32R = mybir.dt.float32r
FP16 = mybir.dt.float16
BF16 = mybir.dt.bfloat16
I32 = mybir.dt.int32
ALU = mybir.AluOpType
ACT = mybir.ActivationFunctionType
AX = mybir.AxisListType

N = 625
D = 768
P = 125
T = N // P
KT = D // 128
NP = 628
HALF = NP // 2
DH = D // 2
E = 20625
EC = E // P
G_EDGE = 7
CPG = 24
ECP = G_EDGE * CPG
SLOT = 4
NSLOT = 3
SPG = CPG // SLOT
PACK = 4096.0
FAR = -1.0e30
LN_EPS = 1e-5
SLOPE = 0.2
H0 = 4
C0 = D // H0
AUG0 = C0 + 1
MIX_EPS = 1e-6
NEXP0 = 16
TOPK0 = 8
WIDTHS = [512] * 8 + [1024] * 8
CH = 256
NCH = sum(WIDTHS) // CH
H1 = 12
C1 = D // H1
AUG1 = C1 + 1
M1 = 256
K_EPS = 1e-4
E1 = 8
I1 = 64
RPAD = 32

assert CPG * P < PACK and ECP >= EC and SPG % NSLOT == 0
assert E == EC * P and N == T * P and D == KT * 128


class Ring:

    def __init__(self, pairs, jobs):
        self.pairs = pairs
        self.jobs = jobs
        self.index = {name: i for i, (name, _) in enumerate(jobs)}
        assert len(self.index) == len(jobs)

    def pair(self, name):
        return self.pairs[self.index[name] % len(self.pairs)]

    def emptied(self, i):
        engine = self.jobs[i][1]
        return engine, sum(1 for _, e in self.jobs[:i + 1] if e == engine)


def gat_schedule0():
    def prob(l, h, fill, agg):
        return [("bc", l, h, 0), ("lin", l, h)] + fill[:1] + [("bc", l, h, 1), ("prob", l, h)] + fill[1:] + agg

    steps = [("ln", 0)] + [("h", 1, t) for t in range(T)] + [("edges",)] + [("lg", 1, t) for t in range(T)]
    steps += [("q", 0), ("q", 1), ("logit", 1), ("q", 2), ("q", 3)] + [("mask", t) for t in range(T)]
    steps += [("asmax", 1, 0), ("asmax", 1, 1), ("q", 4), ("asmax", 1, 2), ("q", 5), ("asmax", 1, 3), ("k", 0)]
    steps += [("shift", 1), ("k", 1)]
    steps += prob(1, 0, [("k", 2)], [])
    steps += prob(1, 1, [("k", 3), ("k", 4)], [("agg", 1, 0)])
    steps += prob(1, 2, [("v", 0), ("v", 1)], [("agg", 1, 1)])
    steps += prob(1, 3, [("v", 2), ("v", 3)], [("agg", 1, 2)])
    steps += [("v", 4), ("agg", 1, 3)] + [("kv", p) for p in range(KT)] + [("relu",)]
    for t in range(T):
        steps += [("h", 2, t), ("lg", 2, t), ("mix", t)]
    steps += [("mix", 5), ("logit", 2), ("out", 0)] + [("asmax", 2, h) for h in range(H0)] + [("out", 1), ("shift", 2)]
    for h in range(H0):
        steps += [("bc", 2, h, 0), ("bc", 2, h, 1), ("lin", 2, h)]
        if h:
            steps += [("agg", 2, h - 1)]
        steps += [("prob", 2, h)]
        if h < 3:
            steps += [("out", 2 + h)]
    steps += [("agg", 2, H0 - 1)]
    return steps


AGG_GROUPS = [(0, 1), (2, 3), (4,)]

UPJ = 4
NJ = H1 * T // UPJ


def units(j):
    return [divmod(u, T) for u in range(UPJ * j, UPJ * (j + 1))]


def segments(j):
    found = []
    for i, (h, t) in enumerate(units(j)):
        if found and found[-1][0] == h:
            found[-1][2] += 1
        else:
            found.append([h, t, 1, i])
    return found


def gat_schedule1():
    steps = [("ln",)] + [("ft", t, g) for t in range(T) for g in range(2)] + [("logit",)]
    for m in range(KT):
        steps += [("q", m), ("asmax", 2 * m), ("asmax", 2 * m + 1)]
        if m:
            steps += [("sq", "q", m - 1)]
    steps += [("shift",), ("sq", "q", KT - 1)]
    fill = [("k", m) for m in range(KT)] + [("v", t) for t in range(T)]
    for h in range(H1):
        steps += [("bc", h, 0), ("bc", h, 1), ("lin", h)]
        if h:
            steps += [("agg", h - 1)]
        steps += [("prob", h)]
        steps += fill[h:h + 1]
        if 1 <= h <= KT:
            steps += [("sq", "k", h - 1)]
    steps += [("agg", H1 - 1)]
    steps += [("kmax", j) for j in range(NJ)] + [("kstab",)]
    for j in range(NJ + 2):
        if j < NJ:
            steps += [("kexp", j)]
        if j > 1:
            steps += [("ctx", h) for h in range(H1) if UPJ * (j - 2) < (h + 1) * T <= UPJ * (j - 1)]
    for j in range(NJ + 2):
        if j >= 2:
            steps += [("qpT", j - 2)]
        if j < NJ:
            steps += [("qexp", j)]
        if j >= 2:
            steps += [("mo", j - 2)]
    steps += [("oT", t) for t in range(T)] + [("wo", t) for t in range(T)]
    return steps


def build(nc, dram, out, stop=None):
    sbase = 16512
    off = {}
    at = sbase
    for name, size in [("x", 15360), ("T1", 15072), ("C", 12576), ("MASK", 6304), ("W0", 18432), ("W1", 18432),
                       ("H", 15616), ("A", 25152), ("E2", 5024), ("Q", 15072), ("K", 15360), ("V", 15616),
                       ("KB", 6144), ("TM", 15360), ("B1", 3072), ("AROW", 6144)]:
        off[name] = at
        assert at % 32 == 0
        at += size
    small = [at]

    def place(name, shape, dtype, region, extra=0):
        return nc.alloc_sbuf_tensor_at(name, shape, dtype, offset=off[region] + extra, align_bytes=16)

    def tiny(name, shape, dtype):
        size = int(np.prod(shape[1:])) * (2 if dtype in (FP16, BF16) else 4)
        t = nc.alloc_sbuf_tensor_at(name, shape, dtype, offset=small[0], align_bytes=4)
        small[0] += (size + 3) // 4 * 4
        assert small[0] <= 229368, small[0]
        return t

    x = place("x_res", [P, T, D], FP32, "x")
    cnt = place("edge_count", [P, T, NP], FP32, "C")
    far = place("far", [P, T, NP], BF16, "MASK")
    ident = tiny("ident", [128, 128], FP32)
    eps_ln = tiny("eps_ln", [128, 1], FP32)
    stats = tiny("ln_stats", [P, T, 2, 6], FP32)
    mv = tiny("ln_mean_var", [P, T, 2], FP32)
    std = tiny("ln_std", [P, T], FP32)
    rstd = tiny("ln_rstd", [P, T], FP32)
    nmr = tiny("ln_shift", [P, T], FP32)
    layer_small = small[0]
    rows = tiny("rows", [2 * RPAD, NP], FP32R)
    logit = tiny("logit_cols", [P, T, RPAD], FP32)
    as02 = place("as_slope", [P, T, H0], FP32, "H", 15440)
    asmax = place("as_max", [P, T, H0], FP32, "H", 15520)
    mcol = place("m_col", [P, T, H0], FP32, "V", 15488)
    recip = place("recip", [P, 8], FP32, "V", 15568)
    pick = {0: place("pick_row0", [2 * RPAD, RPAD], FP32R, "V", 15360), 1: place("pick_row1", [2 * RPAD, RPAD], FP32R, "AROW", 1280)}
    xn = place("xn_tok", [P, T, D], FP32, "TM")
    xnT = place("xn_T", [128, KT, NP], FP32, "T1")
    x1 = place("gat1_tok", [P, T, D], FP32, "TM")
    x1T = place("gat1_T", [128, KT, NP], FP32, "T1")
    wslot = [place("w_slot0", [128, KT, D], FP32, "W0"), place("w_slot1", [128, KT, D], FP32, "W1")]
    haug = place("h_aug", [P, T, H0, AUG0], FP32, "H")
    probs = [place(f"gat_prob{i}", [P, T, NP], FP32, "A", i * 12576) for i in range(2)]
    e2 = [place(f"gat_slope{i}", [P, NP], FP32, "E2", i * 2512) for i in range(2)]
    junk = place("junk", [P, 2 * NP], FP32, "E2")
    qT = place("q_T", [128, KT, NP], FP32, "Q")
    kk = place("k_tok", [P, T, D], FP32, "K")
    vv = place("v_tok", [P, T, D], FP32, "V")
    phie = [place(f"phi_exp{i}", [128, D], FP32, "KB", i * 3072) for i in range(2)]
    kvb = place("kv_blocks", [128, KT, 128], FP32, "KB")
    ksb = place("ksum_blocks", [128, KT, 128], FP32, "KB", 3072)
    den = [place(f"mix_den{i}", [128, NP], FP32, "K", i * 2528) for i in range(2)]
    b1 = place("b1_rows", [P, D], FP32, "B1")
    b2 = place("b2_rows", [P, D], FP32, "A")
    bo = place("bo_rows", [P, D], FP32, "A", 3072)
    arow = place("a_rows", [P, 2, D], FP32, "AROW")
    craw = place("count_raw", [P, T, HALF], FP32, "K")
    chi = place("count_hi", [P, T, HALF], I32, "K", 6304)
    chif = place("count_hi_float", [P, T, HALF], FP32, "TM")
    hot_at = [("Q", 0), ("Q", 7520), ("A", 6144)]
    shot = [place(f"src_onehot{i}", [P, SLOT, 626], FP16, *hot_at[i]) for i in range(NSLOT)]
    dhot = [place(f"dst_onehot{i}", [P, SLOT, HALF], FP16, hot_at[i][0], hot_at[i][1] + 5008) for i in range(NSLOT)]
    iota16 = place("iota16", [P, NP], FP16, "V", 7552)
    ids = place("ids", [P, 2, ECP], I32, "V", 8832)
    sid = place("src_id", [P, ECP], FP32, "V", 10176)
    dlo = place("dst_lo", [P, ECP], FP32, "V", 10848)
    dwt = place("dst_weight", [P, ECP], FP32, "V", 11520)
    did = place("dst_id", [P, ECP], FP32, "V", 12192)

    small[0] = layer_small
    xh = place("x_hi", [128, KT, NP], FP32R, "T1")
    xl = place("x_lo", [128, KT, NP], FP32R, "Q")
    xn2 = place("xn2_tok", [P, T, D], FP32, "TM")
    w1raw = [place(f"w1_raw{i}", [128, KT, CH], FP32, f"W{i}") for i in range(2)]
    w1hi = [place(f"w1_hi{i}", [128, KT, CH], FP32R, f"W{i}", 6144) for i in range(2)]
    w1lo = [place(f"w1_lo{i}", [128, KT, CH], FP32R, f"W{i}", 12288) for i in range(2)]
    w2raw = [place(f"w2_raw{i}", [128, 2, D], FP32, ("A", "K")[i]) for i in range(2)]
    w2hi = [place(f"w2_hi{i}", [128, 2, D], FP32R, ("A", "K")[i], 6144) for i in range(2)]
    w2lo = [place(f"w2_lo{i}", [128, 2, D], FP32R, ("A", "K")[i], 12288) for i in range(2)]
    hid = [place(f"hid{i}", [128, 2, NP], FP32, ("H", "TM")[i]) for i in range(2)]
    hidh = [place(f"hid_hi{i}", [128, 2, NP], FP32R, ("H", "TM")[i], 5024) for i in range(2)]
    hidl = [place(f"hid_lo{i}", [128, 2, NP], FP32R, ("H", "TM")[i], 10048) for i in range(2)]
    rw = place("router0", [128, KT, NEXP0], FP32, "KB")
    rwh = place("router0_hi", [128, KT, NEXP0], FP32R, "KB", 384)
    rwl = place("router0_lo", [128, KT, NEXP0], FP32R, "KB", 768)
    pr = place("router0_prob", [P, T, NEXP0], FP32, "KB", 1152)
    rest = place("router0_rest", [P, T, NEXP0], FP32, "KB", 1472)
    top = place("router0_top", [P, T, 8], FP32, "KB", 1792)
    col = [place(f"router0_col{i}", [P, T], FP32, "KB", 1952 + 32 * i) for i in range(2)]
    comb = place("router0_comb", [P, T, NCH], FP32, "KB", 2048)

    ft = place("ft_aug", [P, T, H1, AUG1], FP32, "H")
    res = place("gat_res", [P, T, D], FP32, "TM")
    xn3 = place("xn3_tok", [P, T, D], FP32, "TM")
    q1T = place("q1_T", [128, KT, NP], FP32, "Q")
    k1T = place("k1_T", [128, KT, NP], FP32, "K")
    v1 = place("v1_aug", [P, T, H1, AUG1], FP32, "V")
    sq = [place(f"sq{i}", [128, NP], FP32, "KB", i * 2528) for i in range(2)]
    wblk = place("wt_blocks", [128, 256], FP32, "B1")
    wab = place("logit_weights", [128, KT, 2 * H1], FP32, "B1", 1024)
    wpair = place("w_pair", [64, 128], FP32, "B1", 1600)
    attn = place("attn_T", [64, 2 * H1], FP32, "B1", 2112)
    halves = place("half_ones", [128, 2], FP32, "B1", 2208)
    projT = place("proj_T", [128, 2, M1], FP32, "MASK")
    acol = place("logit1_cols", [P, T, RPAD], FP32, "AROW", 0)
    as02b = place("as1_slope", [P, T, H1], FP32, "AROW", 1504)
    asmaxb = place("as1_max", [P, T, H1], FP32, "AROW", 1744)
    mcolb = place("m1_col", [P, T, H1], FP32, "AROW", 1984)
    shiftb = place("shift1_cols", [P, T, RPAD], FP32, "AROW", 640)
    diag = {"q": place("diag_q", [P, H1, T], FP32, "AROW", 2704), "k": place("diag_k", [P, H1, T], FP32, "AROW", 2944)}
    kmax = place("k_max", [P, H1, T], FP32, "AROW", 3184)
    kmaxh = place("k_max_head", [P, H1], FP32, "AROW", 3424)
    gmax = place("k_max_all", [H1, 1], FP32, "AROW", 3472)
    nstab = place("k_bias", [P, H1, T], FP32, "AROW", 3488)
    qmax = place("q_max", [P, H1, T], FP32, "AROW", 3728)
    qbias = place("q_bias", [P, H1, T], FP32, "AROW", 3968)
    kmaxb = place("k_max_everywhere", [P, H1], FP32, "AROW", 4208)
    aggr = place("agg1_recip", [P, T, 1], FP32, "AROW", 4256)
    aggv = place("agg1_value", [P, T, C1], FP32, "AROW", 4288)
    morec = place("mo_recip", [P, 8], FP32, "AROW", 5568)
    kp = place("k_prime", [P, 5 * UPJ, M1], FP32, "A")
    qp = place("q_prime", [P, 3 * UPJ, M1], FP32, "A")
    qpT = place("q_prime_T", [128, 2, UPJ, 2, P], FP32, "A", 12288)
    ctx = place("performer_ctx", [128, H1, 2, AUG1], FP32, "C")
    mo = place("performer_tok", [P, T, D], FP32, "TM")
    moT = place("performer_T", [128, KT, NP], FP32, "H")
    xn4 = place("xn4_tok", [P, T, D], FP32, "TM")
    f1 = place("experts1_w1", [128, KT, E1, I1], FP32, "W0")
    f2 = place("experts1_w2", [128, 4, D], FP32, "K")
    r1 = place("router1", [128, KT, E1], FP32, "KB")
    p1 = place("router1_prob", [P, T, E1], FP32, "KB", 192)
    t1 = place("router1_top", [P, T, 8], FP32, "KB", 352)
    i1 = place("router1_index", [P, T, 8], mybir.dt.uint32, "KB", 512)
    f1i = place("router1_index_f", [P, T, 2], FP32, "KB", 672)
    mk = place("router1_mask", [P, T, E1], FP32, "KB", 720)
    c1 = [place(f"router1_col{i}", [P, T], FP32, "KB", 880 + 32 * i) for i in range(3)]
    io8 = place("iota8", [P, E1], FP32, "KB", 976)
    mkT = place("router1_mask_T", [E1, NP], FP32, "KB", 1024)
    sel1 = place("expert_rows", [E1, E1 * I1], FP32, "KB", 3552)
    hid1 = place("hid1_T", [128, 4, NP], FP32, "A")

    ps = nc.alloc_psum_tensor("ps", [128, 8, 512], FP32)

    sems = {}

    def S(name):
        if name not in sems:
            sems[name] = nc.alloc_semaphore("s_" + name)
        return sems[name]

    steps0 = gat_schedule0()
    jobs = []
    bjobs = []
    for st in steps0:
        k, a = st[0], st[1:]
        if k == "ln":
            jobs += [(("lnT", t), "act" if t % 2 else "dve") for t in range(T)]
        elif k == "h":
            jobs += [(("h",) + a, "act")]
        elif k == "mask":
            jobs += [(("mask",) + a, "dve")]
        elif k == "logit":
            jobs += [(("logitT",) + a, "dve")]
        elif k == "asmax":
            bjobs += [(("asmax",) + a, "dve")]
        elif k == "shift":
            jobs += [(("shiftT",) + a, "dve")]
        elif k == "prob":
            bjobs += [(("prob",) + a + (0,), "act"), (("prob",) + a + (1,), "slope")]
        elif k in ("q", "k", "v"):
            jobs += [((k,) + a, "act")]
        elif k == "agg":
            jobs += [(("agg",) + a + (j,), "dve") for j in range(len(AGG_GROUPS))]
        elif k == "relu":
            jobs += [(("x1T", t), "act") for t in range(T)]
        elif k == "kv":
            jobs += [(("kv",) + a, "dve")]
        elif k == "mix":
            jobs += [(("den",) + a, "act"), (("num",) + a, "num")]
        elif k == "out":
            jobs += [(("out",) + a, "dve")]
    ring0 = Ring([(0, 1), (2, 3)], jobs)
    steps1 = gat_schedule1()
    jobs1, bjobs1, cjobs, tjobs, ojobs = [], [], [], [], []
    for st in steps1:
        k, a = st[0], st[1:]
        if k == "ln":
            jobs1 += [(("lnT", t), "act" if t % 2 else "dve") for t in range(T)]
        elif k == "logit":
            jobs1 += [(("wal",), "dve"), (("logit",), "dve"), (("logitT",), "dve")]
        elif k == "shift":
            jobs1 += [(("shiftT",), "dve")]
        elif k == "asmax":
            bjobs1 += [(st, "dve")]
        elif k == "prob":
            bjobs1 += [(st + (0,), "act"), (st + (1,), "slope")]
        elif k in ("ft", "q", "k", "v", "kexp", "qexp"):
            jobs1 += [(st, "act")]
        elif k == "oT":
            jobs1 += [(st, "act" if a[0] % 2 else "dve")]
        elif k in ("sq", "agg", "kmax", "wo"):
            jobs1 += [(st, "dve")]
        elif k == "kstab":
            jobs1 += [(("kstabT",), "dve"), (("kstabB",), "dve")]
        elif k == "ctx":
            cjobs += [(st, "dve")]
        elif k == "qpT":
            tjobs += [(st, "act")]
        elif k == "mo":
            ojobs += [(st, "dve")]
    ring1 = Ring([(0, 1), (2, 3)], jobs1)
    bring1 = Ring([(4, 5), (6, 7)], bjobs1)
    cring = Ring([(6,), (7,)], cjobs)
    tring = Ring([(4, 5)], tjobs)
    oring = Ring([(6,), (7,)], ojobs)
    bring0 = Ring([(4, 5), (6, 7)], bjobs)

    phis = [st for st in steps0 if st[0] in ("q", "k")]
    prob_steps = [st for st in steps0 if st[0] == "prob"]

    def rowsT(a, b):
        return a.rearrange(b)

    def tok(ap):
        return ap.rearrange("(t p) d -> p t d", p=P)

    def feat(ap):
        return ap.rearrange("(k p) n -> p k n", p=128)

    W_ORDER = [("W1", dram["L0_gnn_W1"]), ("Wq", dram["L0_mix_W_qkv"][:, 0:D]), ("Wk", dram["L0_mix_W_qkv"][:, D:2 * D]),
               ("Wv", dram["L0_mix_W_qkv"][:, 2 * D:3 * D]), ("W2", dram["L0_gnn_W2"]), ("Wo", dram["L0_mix_W_out"])]
    W_INDEX = {n: i for i, (n, _) in enumerate(W_ORDER)}
    W_LAST = {"W1": ("h", 1, T - 1), "Wq": ("q", KT - 1), "Wk": ("k", T - 1), "Wv": ("v", T - 1), "W2": ("h", 2, T - 1)}

    def ln_std(act, l):
        act.wait_ge(S("ln_var"), l)
        act.activation(std[:, :], mv[:, :, 1], ACT.Sqrt, bias=eps_ln[0:P, :]).then_inc(S("ln_std"), 1)

    NORM = float(C1) ** -0.25
    far_t = place("far_diag", [P, 640], FP32, "E2")
    sq_jobs = [st for st in steps1 if st[0] == "sq"]
    block = nc.Block()
    block.__enter__()

    def bcast_rows(ap):
        return ap.rearrange("(a n) -> a n", a=1).broadcast_to([P, ap.shape[0]])

    @block.sync
    def _(sp):
        for t in range(T):
            sp.dma_start(x[:, t, :], dram["x"][t * P:(t + 1) * P, :]).then_inc(S(f"x_in{t}"), 16)
        for i, (name, src) in enumerate(W_ORDER):
            if i >= 2:
                sp.wait_ge(S("pe_job"), ring0.index[W_LAST[W_ORDER[i - 2][0]]] + 1)
            sp.dma_start(wslot[i % 2][:, :, :], feat(src)).then_inc(S(f"w_in{i % 2}"), 16)
            if name == "W1":
                sp.dma_start(arow[:, 0, :], bcast_rows(dram["L0_gnn_a_src1"])).then_inc(S("arow_in"), 16)
                sp.dma_start(arow[:, 1, :], bcast_rows(dram["L0_gnn_a_dst1"])).then_inc(S("arow_in"), 16)
                sp.dma_start(b1[:, :], bcast_rows(dram["L0_gnn_b1"])).then_inc(S("b1_in"), 16)
                sp.dma_start(b2[:, :], bcast_rows(dram["L0_gnn_b2"])).then_inc(S("bias_in"), 16)
                sp.dma_start(bo[:, :], bcast_rows(dram["L0_mix_b_out"])).then_inc(S("bias_in"), 16)
            if name == "W2":
                sp.wait_ge(S("logit_cols"), 1)
                sp.dma_start(arow[:, 0, :], bcast_rows(dram["L0_gnn_a_src2"])).then_inc(S("arow_in"), 16)
                sp.dma_start(arow[:, 1, :], bcast_rows(dram["L0_gnn_a_dst2"])).then_inc(S("arow_in"), 16)
        def load_w1(c, b):
            sp.dma_start(w1raw[b][:, :, :], feat(dram["L0_ffn_w1"][:, bass.ds(c * CH, CH)])).then_inc(S(f"w1_in{b}"), 16)

        def load_w2(c, b):
            sp.dma_start(w2raw[b][:, :, :], dram["L0_ffn_w2"][bass.ds(c * CH, CH), :].rearrange("(j p) d -> p j d", p=128)
                         ).then_inc(S(f"w2_in{b}"), 16)

        if stop != 0:
            sp.wait_ge(S("x_done"), 1)
            sp.dma_start(rw[:, :, :], feat(dram["L0_ffn_router_wT"])).then_inc(S("router_in"), 16)
            for b in range(2):
                load_w1(b, b)
                load_w2(b, b)
            with sp.Fori(1, NCH // 2) as i:
                for b in range(2):
                    c = i * 2 + b
                    sp.wait_ge(S("w1_lo"), c - 1)
                    load_w1(c, b)
                    sp.wait_ge(S("w2_lo"), c - 1)
                    load_w2(c, b)
        if stop is None or stop > 1:
            sp.wait_ge(S("x_done"), 2)
            sp.dma_start(wpair[:, 0:64], dram["L1_gnn_W"]).then_inc(S("gat1_in"), 16)
            sp.dma_start(wpair[:, 64:128], dram["L1_gnn_W"]).then_inc(S("gat1_in"), 16)
            sp.dma_start(attn[:, :], dram["L1_gnn_attnT"]).then_inc(S("gat1_in"), 16)
            sp.wait_ge(S("wblk_clear"), 1)
            for i in range(2):
                hs = slice(64 * i, 64 * i + 64)
                sp.dma_start(wblk[hs, 64 * i:64 * i + 64], dram["L1_gnn_WT"]).then_inc(S("gat1_in"), 16)
                sp.dma_start(wblk[hs, 128 + 64 * i:192 + 64 * i], dram["L1_gnn_W_resT"]).then_inc(S("gat1_in"), 16)
            for i, name in enumerate(("Wq", "Wk", "Wv", "Wo")):
                if i >= 2:
                    last = ("q", KT - 1) if i == 2 else ("k", KT - 1)
                    sp.wait_ge(S("pe_job1"), ring1.index[last] + 1)
                sp.dma_start(wslot[i % 2][:, :, :], feat(dram["L1_mix_" + name])).then_inc(S(f"w_in{i % 2}"), 16)
                if i == 2:
                    sp.wait_ge(S("proj_clear"), 1)
                    for half in range(2):
                        sp.dma_start(projT[64 * half:64 * half + 64, half, :], dram["L1_mix_projT"]).then_inc(S("proj_in"), 16)
            sp.wait_ge(S("pe_job1"), ring1.index[("v", T - 1)] + 1)
            for c in range(KT):
                sp.dma_start(f1[:, c, :, :], dram["L1_ffn_w1"][:, c * 128:(c + 1) * 128, :].rearrange("e p i -> p e i")
                             ).then_inc(S("ffn1_in"), 16)
            sp.wait_ge(S("pe_job1"), ring1.index[("kexp", NJ - 1)] + 1)
            sp.dma_start(f2[:, :, :], dram["L1_ffn_w2"].rearrange("(m p) d -> p m d", p=128)).then_inc(S("ffn1_in"), 16)
            sp.dma_start(r1[:, :, :], feat(dram["L1_ffn_router_wT"])).then_inc(S("ffn1_in"), 16)
            for t in range(T):
                sp.wait_ge(S("x_out"), t + 1)
                sp.dma_start(out["out"][t * P:(t + 1) * P, :], x[:, t, :]).then_inc(S("out"), 16)
            sp.wait_ge(S("out"), 16 * T)
        if stop == 1:
            sp.wait_ge(S("x_done"), 2)
            sp.dma_start(out["dbg"]["x_res"], x[:, :, :]).then_inc(S("out"), 16)
            sp.dma_start(out["dbg"]["comb"], comb[:, :, :]).then_inc(S("out"), 16)
            sp.wait_ge(S("out"), 32)
        if stop == 0:
            sp.wait_ge(S("x_done"), 1)
            for nm, tns in out["dbg"].items():
                if nm in ("x_res",):
                    sp.dma_start(tns, x[:, :, :]).then_inc(S("out"), 16)
                elif nm == "cnt":
                    sp.dma_start(tns, cnt[:, :, :]).then_inc(S("out"), 16)
                elif nm == "x1":
                    sp.dma_start(tns, x1[:, :, :]).then_inc(S("out"), 16)
                elif nm == "qT":
                    sp.dma_start(tns, qT[:, :, :]).then_inc(S("out"), 16)
                elif nm == "asmax":
                    sp.dma_start(tns, asmax[:, :, :]).then_inc(S("out"), 16)
            sp.wait_ge(S("out"), 16 * len(out["dbg"]))

    @block.gpsimd
    def _(pool):
        pool.sem_inc(S("count_added"), 1)
        pool.memset(ident[:, :], 0.0).then_inc(S("pool_chain"), 1)
        pool.memset(ids[:, :, :], -1).then_inc(S("ids_clear"), 1)
        pool.wait_ge(S("ids_clear"), 1)
        pool.dma_start(ids[:, 0, 0:EC], dram["src"].rearrange("(p c) -> p c", p=P)).then_inc(S("ids_in"), 16)
        pool.dma_start(ids[:, 1, 0:EC], dram["dst"].rearrange("(p c) -> p c", p=P)).then_inc(S("ids_in"), 16)
        pool.wait_ge(S("pool_chain"), 1)
        pool.affine_select(out=ident[:, :], in_=ident[:, :], compare_op=ALU.not_equal, fill=1.0, base=0,
                           pattern=[[-1, 128]], channel_multiplier=1).then_inc(S("ident"), 1)
        pool.memset(eps_ln[:, :], LN_EPS).then_inc(S("const"), 1)
        pool.iota(iota16[:, :], [[1, NP]], base=0, channel_multiplier=0,
                  allow_small_or_imprecise_dtypes=True).then_inc(S("const"), 1)
        pool.memset(xnT[:, :, N:NP], 0.0).then_inc(S("const"), 1)
        pool.memset(cnt[:, :, :], 0.0).then_inc(S("const"), 1)
        pool.memset(far[:, :, :], FAR).then_inc(S("const"), 1)
        pool.memset(haug[:, :, :, C0:AUG0], 1.0).then_inc(S("const"), 1)
        pool.memset(rows[:, :].bitcast(FP32), 0.0).then_inc(S("const"), 1)
        pool.memset(logit[:, :, :], 0.0).then_inc(S("const"), 1)
        pool.wait_ge(S("bias_in"), 32)
        pool.wait_ge(S("xn_tok"), T)
        for t in range(T):
            pool.tensor_tensor(x[:, t, :], x[:, t, :], b2[:, :], ALU.add).then_inc(S("x_bias"), 1)
        pool.wait_ge(S("x_bias"), T)
        for t in range(T):
            pool.tensor_tensor(x[:, t, :], x[:, t, :], bo[:, :], ALU.add).then_inc(S("x_bias"), 1)
        pool.wait_ge(S("const"), 8)
        with pool.Fori(0, G_EDGE) as g:
            pool.wait_ge(S("count_float"), g + 1)
            pool.tensor_tensor(cnt[:, :, HALF:NP], cnt[:, :, HALF:NP], chif[:, :, :], ALU.add)
            pool.wait_ge(S("count_split"), g + 1)
            pool.tensor_tensor(cnt[:, :, 0:HALF], cnt[:, :, 0:HALF], craw[:, :, :], ALU.add).then_inc(S("count_added"), 1)
        pool.wait_ge(S("count_added"), G_EDGE + 1)
        for t in range(T):
            pool.tensor_tensor(cnt[:, t, t * P:(t + 1) * P], cnt[:, t, t * P:(t + 1) * P], ident[0:P, 0:P],
                               ALU.add).then_inc(S("count_ready"), 1)
        pool.wait_ge(S("phi_done"), len(phis))
        pool.memset(kvb[:, :, :], 0.0).then_inc(S("blocks_clear"), 1)
        pool.memset(ksb[:, :, :], 0.0).then_inc(S("blocks_clear"), 1)

        if stop == 0:
            return
        pool.wait_ge(S("x_done"), 1)
        pool.memset(xh[:, :, N:NP].bitcast(FP32), 0.0).then_inc(S("pads"), 1)
        pool.memset(xl[:, :, N:NP].bitcast(FP32), 0.0).then_inc(S("pads"), 1)

        def low1(c, b):
            pool.wait_ge(S("w1_hi"), c + 1)
            pool.tensor_tensor(w1lo[b][:, :, :], w1raw[b][:, :, :], w1hi[b][:, :, :].bitcast(FP32),
                               ALU.subtract).then_inc(S("w1_lo"), 1)

        with pool.Fori(0, NCH // 2) as i:
            for b in range(2):
                low1(i * 2 + b, b)

        if stop == 1:
            return
        pool.wait_ge(S("x_done"), 2)
        pool.memset(wblk[:, :], 0.0).then_inc(S("wblk_clear"), 1)
        pool.memset(wab[:, :, :], 0.0).then_inc(S("const1"), 1)
        pool.memset(halves[:, :], 0.0).then_inc(S("halves0"), 1)
        pool.memset(xnT[:, :, N:NP], 0.0).then_inc(S("const1"), 1)
        pool.memset(ft[:, :, :, C1:AUG1], 1.0).then_inc(S("const1"), 1)
        pool.memset(v1[:, :, :, C1:AUG1], 1.0).then_inc(S("const1"), 1)
        pool.memset(acol[:, :, :], 0.0).then_inc(S("const1"), 1)
        pool.memset(shiftb[:, :, :], 0.0).then_inc(S("const1"), 1)
        pool.wait_ge(S("halves0"), 1)
        for i in range(2):
            pool.wait_ge(S("const1"), 6 + i)
            pool.memset(halves[64 * i:64 * i + 64, i:i + 1], 1.0).then_inc(S("const1"), 1)
        pool.wait_ge(S("const1"), 8)
        for t in range(T):
            pool.tensor_tensor(cnt[:, t, t * P:(t + 1) * P], cnt[:, t, t * P:(t + 1) * P], ident[0:P, 0:P],
                               ALU.subtract).then_inc(S("count1"), 1)
        pool.wait_ge(S("shift1"), 1)
        pool.memset(projT[:, :, :], 0.0).then_inc(S("proj_clear"), 1)
        pool.wait_ge(S("pe_job1"), ring1.index[sq_jobs[-1]] + 1)
        pool.iota(io8[:, :], [[1, E1]], base=0, channel_multiplier=0, allow_small_or_imprecise_dtypes=True).then_inc(S("const2"), 1)
        pool.memset(mkT[:, :], 0.0).then_inc(S("const2"), 1)
        pool.memset(sel1[:, :], 1.0).then_inc(S("const2"), 1)
        pool.wait_ge(S("const2"), 3)
        pool.affine_select(out=sel1[:, :], in_=sel1[:, :], compare_op=ALU.is_ge, fill=0.0, base=0,
                           pattern=[[1, E1 * I1]], channel_multiplier=-I1).then_inc(S("const2"), 1)
        pool.wait_ge(S("const2"), 4)
        pool.affine_select(out=sel1[:, :], in_=sel1[:, :], compare_op=ALU.is_ge, fill=0.0, base=I1 - 1,
                           pattern=[[-1, E1 * I1]], channel_multiplier=I1).then_inc(S("const2"), 1)

    def job_full(eng, ring, sem, name):
        eng.wait_ge(S(sem), ring.index[name] + 1)

    @block.scalar
    def _(act):
        def general(name):
            act.wait_ge(S("pe_job"), ring0.index[name] + 1)
            a, b = ring0.pair(name)
            return ps[:, a:b + 1, :]

        def lin(l, h):
            j = prob_steps.index(("prob", l, h))
            if j >= 2:
                act.wait_ge(S("pe_job"), ring0.index[("agg",) + prob_steps[j - 2][1:] + (2,)] + 1)
            if (l, h) == (1, 0):
                act.wait_ge(S("x_bias"), 2 * T)
            act.wait_ge(S("shift_cols"), l)
            name = ("prob", l, h, 0)
            act.wait_ge(S("pe_bjob"), bring0.index[name] + 1)
            a, b = bring0.pair(name)
            for t in range(T):
                dst = probs[j % 2][:, t, :]
                act.activation(dst.rearrange("p (a b) -> p a b", a=2), ps[0:P, a:b + 1, 0:HALF], ACT.Exp,
                               bias=logit[:, t, h:h + 1]).then_inc(S("b_act" if t == T - 1 else "prob_lin"), 1)

        def slope(l, h):
            j = prob_steps.index(("prob", l, h))
            name = ("prob", l, h, 1)
            act.wait_ge(S("pe_bjob"), bring0.index[name] + 1)
            a, b = bring0.pair(name)
            for t in range(T):
                n = j * T + t
                if n >= 2:
                    act.wait_ge(S("prob_max"), n - 1)
                dst = e2[n % 2][:, :]
                act.activation(dst.rearrange("p (a b) -> p a b", a=2), ps[0:P, a:b + 1, 0:HALF], ACT.Exp,
                               bias=as02[:, t, h:h + 1]).then_inc(S("prob_slope"), 1)

        act.sem_inc(S("count_copied"), T)
        for st in steps0:
            k, a = st[0], st[1:]
            if k == "ln":
                act.wait_ge(S("ln_var0"), 1)
                act.wait_ge(S("const"), 8)
                act.activation(std[:, :], mv[:, :, 1], ACT.Sqrt, bias=eps_ln[0:P, :]).then_inc(S("ln_std0"), 1)
                for t in range(1, T, 2):
                    src = general(("lnT", t))[:, :, 0:3 * P].rearrange("p a (b c) -> p a b c", b=3)
                    act.activation(xnT[:, :, t * P:(t + 1) * P].rearrange("p (a b) c -> p a b c", a=2), src,
                                   ACT.Copy).then_inc(S("g_act"), 1)
            elif k == "h":
                l, t = a
                if l == 2:
                    act.wait_ge(S("pe_job"), ring0.index[("agg", 1, H0 - 1, 2)] + 1)
                else:
                    act.wait_ge(S("const"), 8)
                src = general(st)[0:P, :, 0:DH].rearrange("p a (b c) -> p a b c", b=2)
                act.activation(haug[:, t, :, 0:C0].rearrange("p (a b) c -> p a b c", a=2), src, ACT.Copy).then_inc(S("g_act"), 1)
            elif k == "edges":
                with act.Fori(0, G_EDGE) as g:
                    act.wait_ge(S("count_added"), g + 1)
                    for t in range(T):
                        if t < T - 1:
                            act.wait_ge(S("edge_tile"), g * (T - 1) + t + 1)
                        else:
                            act.wait_ge(S("edge_used"), NSLOT + (g + 1) * SPG)
                        act.activation(craw[:, t, :], ps[0:P, t, 0:HALF], ACT.Copy).then_inc(S("count_copied"), 1)
                    act.wait_ge(S("count_high"), g + 1)
                    act.activation(chif[:, :, :], chi[:, :, :], ACT.Copy).then_inc(S("count_float"), 1)
            elif k == "lin":
                lin(*a)
            elif k == "prob":
                slope(*a)
            elif k in ("q", "k"):
                i = phis.index(st)
                if i >= 2:
                    act.wait_ge(S("phi_done"), i - 1)
                if st == ("k", 0):
                    act.wait_ge(S("count_ready"), T)
                if k == "q":
                    src = general(st)[:, :, 0:HALF]
                    dst = qT[:, a[0], :].rearrange("p (a b) -> p a b", a=2)
                    ex = phie[i % 2][:, 0:NP].rearrange("p (a b) -> p a b", a=2)
                else:
                    src = general(st)[0:P, :, 0:DH]
                    dst = kk[:, a[0], :].rearrange("p (a b) -> p a b", a=2)
                    ex = phie[i % 2][0:P, :].rearrange("p (a b) -> p a b", a=2)
                act.activation(ex, src, ACT.Exp).then_inc(S("phi_exp"), 1)
                act.activation(dst, src, ACT.Relu).then_inc(S("g_act"), 1)
            elif k == "v":
                src = general(st)[0:P, :, 0:DH]
                act.activation(vv[:, a[0], :].rearrange("p (a b) -> p a b", a=2), src, ACT.Copy).then_inc(S("g_act"), 1)
            elif k == "relu":
                for t in range(T):
                    src = general(("x1T", t))[:, :, 0:3 * P].rearrange("p a (b c) -> p a b c", b=3)
                    act.activation(x1T[:, :, t * P:(t + 1) * P].rearrange("p (a b) c -> p a b c", a=2), src,
                                   ACT.Relu).then_inc(S("g_act"), 1)
            elif k == "mix":
                p = a[0]
                if p >= 2:
                    act.wait_ge(S("num_done"), p - 1)
                src = general(("den", p))[:, :, 0:HALF]
                act.activation(den[p % 2][:, :].rearrange("p (a b) -> p a b", a=2), src, ACT.Copy,
                               bias=MIX_EPS).then_inc(S("g_act"), 1)

        if stop == 0:
            return
        ln_std(act, 1)
        for t in range(T):
            a = 2 * (t % 2)
            act.wait_ge(S("lnT1"), t + 1)
            src = ps[:, a:a + 2, 0:3 * P].rearrange("p a (b c) -> p a b c", b=3)
            act.activation(xh[:, :, t * P:(t + 1) * P].rearrange("p (a b) c -> p a b c", a=2), src,
                           ACT.Copy).then_inc(S("xh1"), 1)

        def high1(c, b):
            act.wait_ge(S(f"w1_in{b}"), 16 * (c // 2 + 1) if isinstance(c, int) else (c - b) * 8 + 16)
            act.activation(w1hi[b][:, :, :], w1raw[b][:, :, :], ACT.Copy).then_inc(S("w1_hi"), 1)

        def high2(c, b):
            act.wait_ge(S(f"w2_in{b}"), 16 * (c // 2 + 1) if isinstance(c, int) else (c - b) * 8 + 16)
            act.activation(w2hi[b][:, :, :], w2raw[b][:, :, :], ACT.Copy).then_inc(S("w2_hi"), 1)

        def gelu(c, b):
            for j in range(2):
                act.wait_ge(S("hid_job"), 2 * c + j + 1)
                act.activation(hid[b][:, j, :].rearrange("p (a b) -> p a b", a=2), ps[:, 2 * j:2 * j + 2, 0:HALF],
                               ACT.Gelu_apprx_tanh).then_inc(S("gelu"), 1)

        def after_o(c):
            act.wait_ge(S("out_job"), T * c + T)

        act.wait_ge(S("router_in"), 16)
        act.activation(rwh[:, :, :], rw[:, :, :], ACT.Copy).then_inc(S("router_hi"), 1)
        high1(0, 0)
        high1(1, 1)
        high2(0, 0)
        act.wait_ge(S("router_max"), 1)
        act.activation(pr[:, :, :], pr[:, :, :], ACT.Exp).then_inc(S("router_exp"), 1)
        with act.Fori(0, NCH // 2 - 1) as i:
            for b in range(2):
                c = i * 2 + b
                gelu(c, b)
                high1(c + 2, b)
                after_o(c)
                high2(c + 1, 1 - b)
        gelu(NCH - 2, 0)
        after_o(NCH - 2)
        high2(NCH - 1, 1)
        gelu(NCH - 1, 1)
        if stop == 1:
            return
        def general1(name):
            act.wait_ge(S("pe_job1"), ring1.index[name] + 1)
            a, b = ring1.pair(name)
            return ps[:, a:b + 1, :]

        def flat(name):
            act.wait_ge(S("pe_job1"), ring1.index[name] + 1)
            a, b = ring1.pair(name)
            return ps[:, :, :].rearrange("p b n -> p (b n)")[:, a * 512:(b + 1) * 512]

        def two(ap):
            return ap.rearrange("p (a b) -> p a b", a=2)

        nsq = 0
        for st in steps1:
            k, a = st[0], st[1:]
            if k == "ln":
                ln_std(act, 2)
                act.wait_ge(S("const1"), 8)
                for t in range(1, T, 2):
                    src = general1(("lnT", t))[:, :, 0:3 * P].rearrange("p a (b c) -> p a b c", b=3)
                    act.activation(xnT[:, :, t * P:(t + 1) * P].rearrange("p (a b) c -> p a b c", a=2), src,
                                   ACT.Copy).then_inc(S("g1_act"), 1)
            elif k == "ft":
                t, g = a
                nk = (4, 2)[g]
                act.wait_ge(S("pe_job1"), ring1.index[("lnT", T - 1)] + 1)
                src = flat(st)[0:P, 0:nk * 256].rearrange("p (q z) -> p q z", q=nk)
                act.activation(res[:, t, g * 512:g * 512 + nk * 128].rearrange("p (q z) -> p q z", q=nk),
                               src[:, :, 128:256], ACT.Copy).then_inc(S("res_done"), 1)
                act.activation(ft[:, t, g * 8:g * 8 + 2 * nk, 0:C1].rearrange("p (q i) c -> p q i c", q=nk),
                               src[:, :, 0:128].rearrange("p q (i c) -> p q i c", i=2), ACT.Copy).then_inc(S("g1_act"), 1)
            elif k in ("q", "k"):
                m = a[0]
                src = general1(st)[:, :, 0:HALF]
                dst = (q1T if k == "q" else k1T)[:, m, :]
                if nsq >= 2:
                    act.wait_ge(S("pe_job1"), ring1.index[sq_jobs[nsq - 2]] + 1)
                act.activation(two(dst), src, ACT.Copy).then_inc(S("qk1"), 1)
                act.activation(two(sq[nsq % 2][:, :]), src, ACT.Square).then_inc(S("g1_act"), 1)
                nsq += 1
            elif k == "v":
                t = a[0]
                act.wait_ge(S("const1"), 8)
                src = general1(st)[0:P, :, 0:DH].rearrange("p a (b c) -> p a b c", b=6)
                act.activation(v1[:, t, :, 0:C1].rearrange("p (a b) c -> p a b c", a=2), src, ACT.Copy).then_inc(S("g1_act"), 1)
            elif k == "lin":
                h = a[0]
                if h >= 2:
                    act.wait_ge(S("pe_job1"), ring1.index[("agg", h - 2)] + 1)
                act.wait_ge(S("shift1"), 1)
                name = ("prob", h, 0)
                act.wait_ge(S("pe_bjob1"), bring1.index[name] + 1)
                lo, hi = bring1.pair(name)
                for t in range(T):
                    act.activation(two(probs[h % 2][:, t, :]), ps[0:P, lo:hi + 1, 0:HALF], ACT.Exp,
                                   bias=acol[:, t, h:h + 1]).then_inc(S("b1_act" if t == T - 1 else "prob_lin1"), 1)
            elif k == "prob":
                h = a[0]
                name = ("prob", h, 1)
                act.wait_ge(S("pe_bjob1"), bring1.index[name] + 1)
                lo, hi = bring1.pair(name)
                for t in range(T):
                    n = h * T + t
                    if n >= 2:
                        act.wait_ge(S("prob_max1"), n - 1)
                    act.activation(two(e2[n % 2][:, :]), ps[0:P, lo:hi + 1, 0:HALF], ACT.Exp,
                                   bias=as02b[:, t, h:h + 1]).then_inc(S("prob_slope1"), 1)
            elif k == "kexp":
                j = a[0]
                if j == 0:
                    act.wait_ge(S("nstab"), 1)
                    act.wait_ge(S("pe_job1"), ring1.index[("agg", H1 - 1)] + 1)
                if j >= 5:
                    last = [st_ for st_ in steps1 if st_[0] == "ctx" and T * st_[1] < UPJ * (j - 4)][-1]
                    act.wait_ge(S("pe_cjob"), cring.index[last] + 1)
                src = flat(st)
                for i, (h, t) in enumerate(units(j)):
                    ins = act.activation(kp[:, (UPJ * j + i) % (5 * UPJ), :], src[0:P, i * M1:(i + 1) * M1], ACT.Exp,
                                         bias=nstab[:, h, t:t + 1], scale=NORM)
                ins.then_inc(S("g1_act"), 1)
            elif k == "qexp":
                j = a[0]
                if j == 0:
                    act.wait_ge(S("pe_cjob"), H1)
                if j >= 3:
                    act.wait_ge(S("pe_tjob"), j - 2)
                src = flat(st)
                act.wait_ge(S("qbias"), j + 1)
                for i, (h, t) in enumerate(units(j)):
                    ins = act.activation(qp[:, (j % 3) * UPJ + i, :], src[0:P, i * M1:(i + 1) * M1], ACT.Exp,
                                         bias=qbias[:, h, t:t + 1], scale=NORM)
                ins.then_inc(S("g1_act"), 1)
            elif k == "qpT":
                j = a[0]
                act.wait_ge(S("pe_tjob"), j + 1)
                if j >= 2:
                    act.wait_ge(S("pe_ojob"), j - 1)
                lo, hi = tring.pair(st)
                dst = qpT[:, j % 2, :, :, :].rearrange("p (a u) m n -> p a (u m n)", a=2)
                act.activation(dst, ps[:, lo:hi + 1, 0:4 * P], ACT.Copy, bias=K_EPS).then_inc(S("qpT_ready"), 1)
            elif k == "oT":
                t = a[0]
                if t % 2:
                    src = general1(st)[:, :, 0:3 * P].rearrange("p a (b c) -> p a b c", b=3)
                    act.activation(moT[:, :, t * P:(t + 1) * P].rearrange("p (a b) c -> p a b c", a=2), src,
                                   ACT.Copy).then_inc(S("g1_act"), 1)
        ln_std(act, 3)
        for t in range(T):
            lo = 2 * (t % 2)
            act.wait_ge(S("lnT4"), t + 1)
            src = ps[:, lo:lo + 2, 0:3 * P].rearrange("p a (b c) -> p a b c", b=3)
            act.activation(xnT[:, :, t * P:(t + 1) * P].rearrange("p (a b) c -> p a b c", a=2), src,
                           ACT.Copy).then_inc(S("xT4"), 1)
        act.wait_ge(S("router1_max"), 1)
        act.activation(p1[:, :, :], p1[:, :, :], ACT.Exp).then_inc(S("router1_exp"), 1)
        for m in range(4):
            act.wait_ge(S("hid1_job"), m + 1)
            lo = 2 * (m % 2)
            act.activation(two(hid1[:, m, :]), ps[:, lo:lo + 2, 0:HALF], ACT.Silu).then_inc(S("silu"), 1)

    @block.vector
    def _(dve):
        chain = [0]

        def link(ins):
            chain[0] += 1
            ins.then_inc(S("dve_chain"), 1)
            dve.wait_ge(S("dve_chain"), chain[0])

        def general(name):
            dve.wait_ge(S("pe_job"), ring0.index[name] + 1)
            a, b = ring0.pair(name)
            return ps[:, a:b + 1, :]

        def split_rows(src):
            high, low = slice(0, RPAD), slice(RPAD, 2 * RPAD)
            dve.tensor_copy(rows[high, 0:4 * P], src[high, 0, 0:4 * P])
            link(dve.tensor_copy(rows[high, 4 * P:N], src[high, 1, 0:P]))
            dve.tensor_tensor(rows[low, 0:4 * P], src[high, 0, 0:4 * P], rows[high, 0:4 * P].bitcast(FP32), ALU.subtract)
            return dve.tensor_tensor(rows[low, 4 * P:N], src[high, 1, 0:P], rows[high, 4 * P:N].bitcast(FP32), ALU.subtract)

        def row_picker(layer):
            return dve.tensor_tensor(pick[layer][:, :], ident[0:2 * RPAD, 0:RPAD], ident[0:2 * RPAD, RPAD:2 * RPAD], ALU.add)

        scrap = [0, 0]

        def scrapped(slots):
            n = scrap[0]
            if scrap[1] != slots:
                if n:
                    dve.wait_ge(S("scrap"), n)
                scrap[1], scrap[0] = slots, n
                scrap.append(n)
            elif n - scrap[-1] >= slots:
                dve.wait_ge(S("scrap"), n - slots + 1)
            scrap[0] += 1
            return (n - scrap[-1]) % slots

        def ln_stats(src, ready):
            for t in range(T):
                ready(t)
                for half in range(2):
                    last = dve.bn_stats(stats[:, t, half, :], src[:, t, half * DH:(half + 1) * DH])
                link(last)
                last = dve.bn_aggr(mv[:, t, :], stats[:, t, :, :])
            return last

        for st in steps0:
            k, a = st[0], st[1:]
            if k == "ln":
                ln_stats(x, lambda t: dve.wait_ge(S(f"x_in{t}"), 16)).then_inc(S("ln_var0"), 1)
                dve.wait_ge(S("ln_std0"), 1)
                link(dve.reciprocal(rstd[:, :], std[:, :]))
                link(dve.scalar_tensor_tensor(nmr[:, :], mv[:, :, 0], -1.0, rstd[:, :], ALU.mult, ALU.mult))
                for t in range(T):
                    dve.tensor_scalar(xn[:, t, :], x[:, t, :], rstd[:, t:t + 1], nmr[:, t:t + 1], ALU.mult,
                                      ALU.add).then_inc(S("xn_tok"), 1)
                dve.wait_ge(S("const"), 8)
                for t in range(0, T, 2):
                    src = general(("lnT", t))[:, :, 0:3 * P].rearrange("p a (b c) -> p a b c", b=3)
                    dve.tensor_copy(xnT[:, :, t * P:(t + 1) * P].rearrange("p (a b) c -> p a b c", a=2),
                                    src).then_inc(S("g_dve"), 1)
                link(row_picker(0))
                dve.wait_ge(S("ids_in"), 32)
                dve.tensor_copy(sid[:, :], ids[:, 0, :])
                link(dve.tensor_copy(did[:, :], ids[:, 1, :]))
                link(dve.tensor_scalar(dwt[:, :], did[:, :], float(HALF), None, ALU.is_ge))
                link(dve.scalar_tensor_tensor(dlo[:, :], dwt[:, :], -float(HALF), did[:, :], ALU.mult, ALU.add))
                link(dve.tensor_scalar(dwt[:, :], dwt[:, :], PACK - 1.0, 1.0, ALU.mult, ALU.add))
            elif k == "edges":
                def onehot(n, b):
                    dve.wait_ge(S("edge_used"), n + 1)
                    for r in range(SLOT):
                        c = n * SLOT + r
                        dve.tensor_scalar(shot[b][:, r, 0:N], iota16[:, 0:N], sid[:, bass.ds(c, 1)], None, ALU.is_equal)
                        last = dve.tensor_scalar(dhot[b][:, r, :], iota16[:, 0:HALF], dlo[:, bass.ds(c, 1)],
                                                 dwt[:, bass.ds(c, 1)], ALU.is_equal, ALU.mult)
                    last.then_inc(S("edge_hot"), 1)

                def onehots(g, lo, hi):
                    for i in range(lo, hi):
                        onehot(g * SPG + i, i % NSLOT)

                def split_high(g):
                    dve.wait_ge(S("count_copied"), g * T + 2 * T)
                    dve.tensor_scalar(chi[:, :, :], craw[:, :, :], 1.0 / PACK, -0.5 + 0.5 / PACK, ALU.mult,
                                      ALU.add).then_inc(S("count_high"), 1)

                def split_low(g):
                    dve.wait_ge(S("count_high"), g + 1)
                    dve.scalar_tensor_tensor(craw[:, :, :], chi[:, :, :], -PACK, craw[:, :, :], ALU.mult,
                                             ALU.add).then_inc(S("count_split"), 1)

                onehots(0, 0, SPG)
                with dve.Fori(1, G_EDGE) as g:
                    onehots(g, 0, 1)
                    split_high(g - 1)
                    onehots(g, 1, 3)
                    split_low(g - 1)
                    onehots(g, 3, SPG)
                split_high(G_EDGE - 1)
                split_low(G_EDGE - 1)
            elif k == "mask":
                t = a[0]
                src = general(st)[0:P]
                dve.tensor_scalar(far[:, t, 0:3 * P], src[:, 0, 0:3 * P], 0.5, FAR, ALU.is_lt, ALU.mult)
                dve.tensor_scalar(far[:, t, 3 * P:N], src[:, 1, 0:2 * P], 0.5, FAR, ALU.is_lt, ALU.mult).then_inc(S("g_dve"), 1)
            elif k == "lg":
                l, t = a
                dve.wait_ge(S("arow_in"), 32 * l)
                eng, n = ring0.emptied(ring0.index[("h", l, t)])
                dve.wait_ge(S("g_act"), n)
                for s in range(2):
                    for h in range(H0):
                        z = scrapped(6) * C0
                        dve.tensor_tensor_reduce(
                            out=junk[:, z:z + C0], in0=haug[:, t, h, 0:C0], in1=arow[:, s, h * C0:(h + 1) * C0],
                            scale=1.0, scalar=0.0, op0=ALU.mult, op1=ALU.add,
                            accum_out=logit[:, t, s * H0 + h:s * H0 + h + 1]).then_inc(S("scrap"), 1)
            elif k == "logit":
                l = a[0]
                dve.wait_ge(S("scrap"), scrap[0])
                dve.sem_inc(S("logit_cols"), 1)
                link(dve.tensor_scalar(as02[:, :, :], logit[:, :, 0:H0], SLOPE, None, ALU.mult))
                split_rows(general(("logitT", l))).then_inc(S("g_dve"), 1)
            elif k == "asmax":
                l, h = a
                dve.wait_ge(S("pe_bjob"), bring0.index[st] + 1)
                pa, pb = bring0.pair(st)
                src = ps[0:P, pa:pb + 1, 0:HALF]
                for t in range(T):
                    z = scrapped(2) * NP
                    last = dve.tensor_tensor_reduce(
                        out=junk[:, z:z + NP].rearrange("p (a b) -> p a b", a=2), in0=far[:, t, :].rearrange("p (a b) -> p a b", a=2),
                        in1=src, scale=1.0, scalar=-3.0e38, op0=ALU.add, op1=ALU.max, accum_out=asmax[:, t, h:h + 1]).then_inc(S("scrap"), 1)
                dve.wait_ge(S("scrap"), scrap[0])
                dve.sem_inc(S("b_dve"), 1)
            elif k == "shift":
                l = a[0]
                dve.wait_ge(S("b_dve"), H0 * l)
                ad = logit[:, :, H0:2 * H0]
                link(dve.tensor_tensor(mcol[:, :, :], asmax[:, :, :], ad, ALU.add))
                link(dve.scalar_tensor_tensor(mcol[:, :, :], mcol[:, :, :], SLOPE, mcol[:, :, :], ALU.mult, ALU.max))
                dve.tensor_tensor(logit[:, :, 2 * H0:3 * H0], ad, mcol[:, :, :], ALU.subtract)
                dve.scalar_tensor_tensor(logit[:, :, 3 * H0:4 * H0], ad, SLOPE, mcol[:, :, :], ALU.mult,
                                         ALU.subtract).then_inc(S("shift_cols"), 1)
                split_rows(general(("shiftT", l))).then_inc(S("g_dve"), 1)
            elif k == "prob":
                j = prob_steps.index(st)
                for t in range(T):
                    n = j * T + t
                    dve.wait_ge(S("prob_slope"), n + 1)
                    dst = probs[j % 2][:, t, :]
                    dve.tensor_tensor(dst, dst, e2[n % 2][:, :], ALU.max).then_inc(S("prob_max"), 1)
                    dve.wait_ge(S("prob_max"), n + 1)
                    dve.scalar_tensor_tensor(dst, dst, 1.0, cnt[:, t, :], ALU.min, ALU.mult).then_inc(S("prob_ready"), 1)
            elif k in ("q", "k"):
                i = phis.index(st)
                eng, n = ring0.emptied(ring0.index[st])
                dve.wait_ge(S("g_act"), n)
                if k == "q":
                    dst, ex = qT[:, a[0], :], phie[i % 2][:, 0:NP]
                else:
                    dst, ex = kk[:, a[0], :], phie[i % 2][0:P, :]
                dve.scalar_tensor_tensor(dst, ex, 1.0, dst, ALU.min, ALU.add).then_inc(S("phi_done"), 1)
            elif k == "agg":
                l, h = a
                if (l, h) == (1, 0):
                    dve.wait_ge(S("b1_in"), 16)
                if (l, h) == (2, 0):
                    dve.wait_ge(S("x_bias"), 2 * T)
                for j, group in enumerate(AGG_GROUPS):
                    src = general(("agg", l, h, j))[0:P]
                    for i, t in enumerate(group):
                        r = recip[:, (j * 2 + i):(j * 2 + i) + 1]
                        link(dve.reciprocal(r, src[:, i, C0:AUG0]))
                        cols = slice(h * C0, (h + 1) * C0)
                        dst = x1[:, t, cols] if l == 1 else x[:, t, cols]
                        add = b1[:, cols] if l == 1 else x[:, t, cols]
                        ins = dve.scalar_tensor_tensor(dst, src[:, i, 0:C0], r, add, ALU.mult, ALU.add)
                    ins.then_inc(S("g_dve"), 1)
            elif k == "kv":
                p = a[0]
                dve.wait_ge(S("blocks_clear"), 2)
                src = general(st)
                for i in range(2):
                    hs = slice(i * 64, (i + 1) * 64)
                    dve.tensor_copy(kvb[hs, p, hs], src[hs, 0, i * 64:(i + 1) * 64])
                    ins = dve.tensor_scalar(ksb[hs, p, hs], src[hs, 1, i * 64:(i + 1) * 64], 1.0, None, ALU.add)
                ins.then_inc(S("g_dve"), 1)
            elif k == "mix":
                p = a[0]
                eng, n = ring0.emptied(ring0.index[("den", p)])
                dve.wait_ge(S("g_act"), n)
                link(dve.reciprocal(den[p % 2][:, :], den[p % 2][:, :]))
                src = general(("num", p))[:, :, 0:HALF]
                dve.tensor_tensor(qT[:, p, :].rearrange("p (a b) -> p a b", a=2), src,
                                  den[p % 2][:, :].rearrange("p (a b) -> p a b", a=2), ALU.mult).then_inc(S("num_done"), 1)
            elif k == "out":
                t = a[0]
                src = general(st)[0:P, :, 0:DH]
                dst = x[:, t, :].rearrange("p (a b) -> p a b", a=2)
                dve.wait_ge(S("x_bias"), 2 * T)
                dve.tensor_tensor(dst, dst, src, ALU.add).then_inc(S("g_dve"), 1)
        eng, n = ring0.emptied(len(ring0.jobs) - 1)
        dve.wait_ge(S("g_dve"), n)
        dve.sem_inc(S("x_done"), 1)
        if stop == 0:
            return

        def ln_apply(l, dst):
            dve.wait_ge(S("ln_std"), l)
            link(dve.reciprocal(rstd[:, :], std[:, :]))
            link(dve.scalar_tensor_tensor(nmr[:, :], mv[:, :, 0], -1.0, rstd[:, :], ALU.mult, ALU.mult))
            for t in range(T):
                dve.tensor_scalar(dst[:, t, :], x[:, t, :], rstd[:, t:t + 1], nmr[:, t:t + 1], ALU.mult,
                                  ALU.add).then_inc(S("xn_tok"), 1)

        ln_stats(x, lambda t: None).then_inc(S("ln_var"), 1)
        ln_apply(1, xn2)
        for t in range(T):
            a = 2 * (t % 2)
            dve.wait_ge(S("xh1"), t + 1)
            src = ps[:, a:a + 2, 0:3 * P].rearrange("p a (b c) -> p a b c", b=3)
            cols = slice(t * P, (t + 1) * P)
            dve.tensor_tensor(xl[:, :, cols].rearrange("p (a b) c -> p a b c", a=2), src,
                              xh[:, :, cols].bitcast(FP32).rearrange("p (a b) c -> p a b c", a=2), ALU.subtract
                              ).then_inc(S("xl1"), 1)
        dve.wait_ge(S("router_hi"), 1)
        dve.tensor_tensor(rwl[:, :, :], rw[:, :, :], rwh[:, :, :].bitcast(FP32), ALU.subtract).then_inc(S("router_lo"), 1)

        def low2(c, b):
            dve.wait_ge(S("w2_hi"), c + 1)
            dve.tensor_tensor(w2lo[b][:, :, :], w2raw[b][:, :, :], w2hi[b][:, :, :].bitcast(FP32),
                              ALU.subtract).then_inc(S("w2_lo"), 1)

        def split(c, b):
            for j in range(2):
                dve.wait_ge(S("gelu"), 2 * c + j + 1)
                dve.tensor_copy(hidh[b][:, j, :], hid[b][:, j, :]).then_inc(S("hid_hi"), 1)
                dve.wait_ge(S("hid_hi"), 2 * c + j + 1)
                dve.tensor_tensor(hidl[b][:, j, :], hid[b][:, j, :], hidh[b][:, j, :].bitcast(FP32),
                                  ALU.subtract).then_inc(S("hid_lo"), 1)

        def gather(c, b):
            for t in range(T):
                a = 4 + 2 * ((T * b + t) % 2)
                dve.wait_ge(S("out_job"), T * c + t + 1 + T)
                dst = x[:, t, :].rearrange("p (a b) -> p a b", a=2)
                dve.scalar_tensor_tensor(dst, ps[0:P, a:a + 2, 0:DH], comb[:, t, bass.ds(c, 1)], dst, ALU.mult,
                                         ALU.add).then_inc(S("out_added"), 1)

        low2(0, 0)
        dve.wait_ge(S("router_job"), 1)
        lg = ps[0:P, 4, 0:T * NEXP0].rearrange("p (t e) -> p t e", t=T)
        link(dve.tensor_reduce(col[0][:, :], lg, AX.X, ALU.max))
        dve.tensor_tensor(pr[:, :, :], lg, col[0][:, :].unsqueeze(2).broadcast_to([P, T, NEXP0]),
                          ALU.subtract).then_inc(S("router_max"), 1)
        dve.wait_ge(S("router_exp"), 1)
        link(dve.tensor_reduce(col[0][:, :], pr[:, :, :], AX.X, ALU.add))
        link(dve.reciprocal(col[1][:, :], col[0][:, :]))
        link(dve.tensor_tensor(pr[:, :, :], pr[:, :, :], col[1][:, :].unsqueeze(2).broadcast_to([P, T, NEXP0]), ALU.mult))
        for t in range(T):
            last = dve.max(top[:, t, :], pr[:, t, :])
        link(last)
        for t in range(T):
            last = dve.match_replace(rest[:, t, :], top[:, t, :], pr[:, t, :], 0.0)
        dve.tensor_reduce(col[0][:, :], top[:, :, :], AX.X, ALU.add)
        link(last)
        link(dve.tensor_tensor(pr[:, :, :], pr[:, :, :], rest[:, :, :], ALU.subtract))
        link(dve.reciprocal(col[1][:, :], col[0][:, :]))
        link(dve.tensor_tensor(pr[:, :, :], pr[:, :, :], col[1][:, :].unsqueeze(2).broadcast_to([P, T, NEXP0]), ALU.mult))
        at, e0 = 0, 0
        for width in sorted(set(WIDTHS)):
            ne, nch = WIDTHS.count(width), width // CH
            for t in range(T):
                last = dve.tensor_copy(comb[:, t, at:at + ne * nch].rearrange("p (e c) -> p e c", c=nch),
                                       pr[:, t, e0:e0 + ne].unsqueeze(2).broadcast_to([P, ne, nch]))
            at, e0 = at + ne * nch, e0 + ne
        link(last)
        dve.sem_inc(S("out_added"), 2)
        split(0, 0)
        low2(1, 1)
        with dve.Fori(0, NCH // 2 - 1) as i:
            for b in (1, 0):
                c = i * 2 + (2 - b)
                split(c, b)
                gather(c - 1, 1 - b)
                low2(c + 1, 1 - b)
        split(NCH - 1, 1)
        gather(NCH - 2, 0)
        gather(NCH - 1, 1)
        dve.wait_ge(S("out_added"), 2 + T * NCH)
        dve.sem_inc(S("x_done"), 1)
        if stop == 1:
            return

        def general1(name):
            dve.wait_ge(S("pe_job1"), ring1.index[name] + 1)
            a, b = ring1.pair(name)
            return ps[:, a:b + 1, :]

        def two(ap):
            return ap.rearrange("p (a b) -> p a b", a=2)

        for st in steps1:
            k, a = st[0], st[1:]
            if k == "ln":
                ln_stats(x, lambda t: None).then_inc(S("ln_var"), 1)
                ln_apply(2, xn3)
                dve.wait_ge(S("const1"), 8)
                for t in range(0, T, 2):
                    src = general1(("lnT", t))[:, :, 0:3 * P].rearrange("p a (b c) -> p a b c", b=3)
                    dve.tensor_copy(xnT[:, :, t * P:(t + 1) * P].rearrange("p (a b) c -> p a b c", a=2),
                                    src).then_inc(S("g1_dve"), 1)
                link(row_picker(1))
                dve.wait_ge(S("diag_job"), 1)
                dve.tensor_scalar(far_t[:, 0:4 * P], ps[0:P, 4, 0:4 * P], 0.5, FAR, ALU.is_lt, ALU.mult)
                link(dve.tensor_scalar(far_t[:, 4 * P:N], ps[0:P, 5, 0:P], 0.5, FAR, ALU.is_lt, ALU.mult))
                for t in range(T):
                    last = dve.tensor_copy(far[:, t, t * P:(t + 1) * P], far_t[:, t * P:(t + 1) * P])
                last.then_inc(S("far1"), 1)
            elif k == "logit":
                src = general1(("wal",))
                for i in range(2):
                    hs = slice(64 * i, 64 * i + 64)
                    for c in range(KT):
                        h = 2 * c + i
                        last = dve.tensor_copy(wab[hs, c, h:h + H1 + 1:H1], src[hs, 0, h:h + H1 + 1:H1])
                last.then_inc(S("g1_dve"), 1)
                src = general1(("logit",))[0:P, 0, 0:T * 2 * H1].rearrange("p (t h) -> p t h", t=T)
                dve.tensor_copy(acol[:, :, 0:2 * H1], src)
                link(dve.tensor_scalar(as02b[:, :, :], src[:, :, 0:H1], SLOPE, None, ALU.mult))
                dve.sem_inc(S("g1_dve"), 1)
                split_rows(general1(("logitT",))).then_inc(S("g1_dve"), 1)
            elif k == "asmax":
                h = a[0]
                dve.wait_ge(S("far1"), 1)
                dve.wait_ge(S("pe_bjob1"), bring1.index[st] + 1)
                lo, hi = bring1.pair(st)
                for t in range(T):
                    z = scrapped(2) * NP
                    dve.tensor_tensor_reduce(out=two(junk[:, z:z + NP]), in0=two(far[:, t, :]), in1=ps[0:P, lo:hi + 1, 0:HALF],
                                             scale=1.0, scalar=-3.0e38, op0=ALU.add, op1=ALU.max,
                                             accum_out=asmaxb[:, t, h:h + 1]).then_inc(S("scrap"), 1)
                dve.wait_ge(S("scrap"), scrap[0])
                dve.sem_inc(S("b1_dve"), 1)
            elif k == "shift":
                ad = acol[:, :, H1:2 * H1]
                link(dve.tensor_tensor(mcolb[:, :, :], asmaxb[:, :, :], ad, ALU.add))
                link(dve.scalar_tensor_tensor(mcolb[:, :, :], mcolb[:, :, :], SLOPE, mcolb[:, :, :], ALU.mult, ALU.max))
                link(dve.tensor_scalar(asmaxb[:, :, :], asmaxb[:, :, :], 0.5 * FAR, None, ALU.is_gt))
                link(dve.tensor_tensor(mcolb[:, :, :], mcolb[:, :, :], asmaxb[:, :, :], ALU.mult))
                dve.tensor_tensor(shiftb[:, :, 0:H1], ad, mcolb[:, :, :], ALU.subtract)
                link(dve.scalar_tensor_tensor(shiftb[:, :, H1:2 * H1], ad, SLOPE, mcolb[:, :, :], ALU.mult, ALU.subtract))
                dve.sem_inc(S("shift1"), 1)
                split_rows(general1(("shiftT",))).then_inc(S("g1_dve"), 1)
            elif k == "sq":
                src = general1(st)[0:P, 0, 0:2 * T].rearrange("p (t i) -> p t i", t=T)
                m = a[1]
                dve.tensor_scalar(diag[a[0]][:, 2 * m:2 * m + 2, :].rearrange("p i t -> p t i"), src, 0.5 * NORM * NORM, None,
                                  ALU.mult).then_inc(S("g1_dve"), 1)
            elif k == "prob":
                h = a[0]
                if h == 0:
                    dve.wait_ge(S("count1"), T)
                for t in range(T):
                    n = h * T + t
                    dve.wait_ge(S("prob_slope1"), n + 1)
                    dst = probs[h % 2][:, t, :]
                    dve.tensor_tensor(dst, dst, e2[n % 2][:, :], ALU.max).then_inc(S("prob_max1"), 1)
                    dve.wait_ge(S("prob_max1"), n + 1)
                    dve.scalar_tensor_tensor(dst, dst, 1.0, cnt[:, t, :], ALU.min, ALU.mult).then_inc(S("prob_ready1"), 1)
            elif k == "agg":
                h = a[0]
                dve.wait_ge(S("res_done"), 2 * T)
                src = general1(st)[0:P, 0, 0:T * AUG1].rearrange("p (t c) -> p t c", t=T)
                cols = slice(h * C1, (h + 1) * C1)
                link(dve.tensor_scalar(aggr[:, :, :], src[:, :, C1:AUG1], 1e-16, None, ALU.max))
                link(dve.reciprocal(aggr[:, :, :], aggr[:, :, :]))
                link(dve.tensor_tensor(aggv[:, :, :], src[:, :, 0:C1], aggr[:, :, :].broadcast_to([P, T, C1]), ALU.mult))
                link(dve.tensor_tensor(aggv[:, :, :], aggv[:, :, :], res[:, :, cols], ALU.add))
                dve.scalar_tensor_tensor(x[:, :, cols], aggv[:, :, :], 0.0, x[:, :, cols], ALU.max, ALU.add
                                         ).then_inc(S("g1_dve"), 1)
            elif k == "kmax":
                j = a[0]
                dve.wait_ge(S("pe_job1"), ring1.index[st] + 1)
                lo, hi = ring1.pair(st)
                src = ps[0:P, lo:hi + 1, :].rearrange("p a (u m) -> p (a u) m", u=2)
                dst = kmax[:, :, :].rearrange("p h t -> p (h t)")[:, UPJ * j:UPJ * (j + 1)]
                dve.tensor_reduce(dst, src, AX.X, ALU.max).then_inc(S("g1_dve"), 1)
            elif k == "kstab":
                dve.wait_ge(S("g1_dve"), ring1.emptied(ring1.index[("kmax", NJ - 1)])[1])
                dve.tensor_reduce(kmaxh[:, :], kmax[:, :, :], AX.X, ALU.max).then_inc(S("kmax_head"), 1)
                src = general1(("kstabT",))[0:H1, 0, 0:P]
                dve.tensor_reduce(gmax[:, :], src, AX.X, ALU.max).then_inc(S("g1_dve"), 1)
                src = general1(("kstabB",))[0:P, 0, 0:H1]
                link(dve.tensor_copy(kmaxb[:, :], src))
                link(dve.scalar_tensor_tensor(nstab[:, :, :], kmaxb[:, :].unsqueeze(2).broadcast_to([P, H1, T]), -NORM,
                                              diag["k"][:, :, :], ALU.mult, ALU.subtract))
                dve.sem_inc(S("nstab"), 1)
                dve.sem_inc(S("g1_dve"), 1)
            elif k == "kexp":
                j = a[0]
                dve.wait_ge(S("g1_act"), ring1.emptied(ring1.index[st])[1])
                u = (UPJ * j) % (5 * UPJ)
                dve.tensor_scalar(kp[:, u:u + UPJ, :], kp[:, u:u + UPJ, :], K_EPS, None, ALU.add).then_inc(S("kp_ready"), 1)
            elif k == "ctx":
                dve.wait_ge(S("pe_cjob"), cring.index[st] + 1)
                b = cring.pair(st)[0]
                dve.tensor_copy(ctx[:, a[0], :, :].rearrange("p m c -> p (m c)"), ps[:, b, 0:2 * AUG1]).then_inc(S("ctx_ready"), 1)
            elif k == "qexp":
                j = a[0]
                dve.wait_ge(S("pe_job1"), ring1.index[st] + 1)
                lo, hi = ring1.pair(st)
                src = ps[0:P, lo:hi + 1, :].rearrange("p a (u m) -> p (a u) m", u=2)
                us = slice(UPJ * j, UPJ * (j + 1))
                f_ = lambda t_: t_[:, :, :].rearrange("p h t -> p (h t)")[:, us]
                link(dve.tensor_reduce(f_(qmax), src, AX.X, ALU.max))
                dve.scalar_tensor_tensor(f_(qbias), f_(qmax), -NORM, f_(diag["q"]), ALU.mult, ALU.subtract).then_inc(S("qbias"), 1)
            elif k == "mo":
                j = a[0]
                dve.wait_ge(S("pe_ojob"), j + 1)
                b = oring.pair(st)[0]
                src = ps[0:P, b, 0:UPJ * AUG1].rearrange("p (u c) -> p u c", u=UPJ)
                r = morec[:, (j % 2) * UPJ:(j % 2 + 1) * UPJ]
                link(dve.reciprocal(r, src[:, :, C1]))
                for h, t, nt, i in segments(j):
                    last = dve.tensor_tensor(mo[:, t:t + nt, h * C1:(h + 1) * C1], src[:, i:i + nt, 0:C1],
                                             r[:, i:i + nt].unsqueeze(2).broadcast_to([P, nt, C1]), ALU.mult)
                last.then_inc(S("mo_ready"), 1)
            elif k == "oT":
                t = a[0]
                if t % 2 == 0:
                    src = general1(st)[:, :, 0:3 * P].rearrange("p a (b c) -> p a b c", b=3)
                    dve.tensor_copy(moT[:, :, t * P:(t + 1) * P].rearrange("p (a b) c -> p a b c", a=2),
                                    src).then_inc(S("g1_dve"), 1)
            elif k == "wo":
                t = a[0]
                src = general1(st)[0:P, :, 0:DH]
                dst = two(x[:, t, :])
                dve.tensor_tensor(dst, dst, src, ALU.add).then_inc(S("g1_dve"), 1)
        dve.wait_ge(S("g1_dve"), ring1.emptied(len(ring1.jobs) - 1)[1])
        ln_stats(x, lambda t: None).then_inc(S("ln_var"), 1)
        ln_apply(3, xn4)
        dve.wait_ge(S("router1_job"), 1)
        lg = ps[0:P, 4, 0:T * E1].rearrange("p (t e) -> p t e", t=T)
        link(dve.tensor_reduce(c1[0][:, :], lg, AX.X, ALU.max))
        dve.tensor_tensor(p1[:, :, :], lg, c1[0][:, :].unsqueeze(2).broadcast_to([P, T, E1]), ALU.subtract).then_inc(S("router1_max"), 1)
        dve.wait_ge(S("router1_exp"), 1)
        link(dve.tensor_reduce(c1[1][:, :], p1[:, :, :], AX.X, ALU.add))
        link(dve.reciprocal(c1[2][:, :], c1[1][:, :]))
        link(dve.tensor_tensor(p1[:, :, :], p1[:, :, :], c1[2][:, :].unsqueeze(2).broadcast_to([P, T, E1]), ALU.mult))
        for t in range(T):
            last = dve.max(t1[:, t, :], p1[:, t, :])
        link(last)
        for t in range(T):
            last = dve.max_index(i1[:, t, :], t1[:, t, :], p1[:, t, :])
        link(last)
        link(dve.tensor_copy(f1i[:, :, :], i1[:, :, 0:2]))
        link(dve.tensor_tensor(f1i[:, :, 0:1], f1i[:, :, 0:1], f1i[:, :, 1:2], ALU.max))
        dve.wait_ge(S("const2"), 5)
        for t in range(T):
            last = dve.tensor_scalar(mk[:, t, :], io8[:, :], f1i[:, t, 0:1], None, ALU.is_equal)
        last.then_inc(S("mask1"), 1)
        dve.wait_ge(S("mask1T"), 1)
        dve.tensor_copy(mkT[:, 0:4 * P], ps[0:E1, 6, 0:4 * P])
        dve.tensor_copy(mkT[:, 4 * P:N], ps[0:E1, 7, 0:P]).then_inc(S("mask1_rows"), 1)
        for m in range(4):
            dve.wait_ge(S("silu"), m + 1)
            dve.wait_ge(S("mask1_bc"), m + 1)
            lo = 4 + 2 * (m % 2)
            dve.tensor_tensor(two(hid1[:, m, :]), two(hid1[:, m, :]), ps[:, lo:lo + 2, 0:HALF], ALU.mult).then_inc(S("hid1"), 1)
        for t in range(T):
            lo = 2 * (t % 4)
            dve.wait_ge(S("out1_job"), t + 1)
            dve.tensor_tensor(two(x[:, t, :]), two(x[:, t, :]), ps[0:P, lo:lo + 2, 0:DH], ALU.add).then_inc(S("x_out"), 1)

    @block.tensor
    def _(pe):
        def emptied(name):
            eng, n = ring0.emptied(ring0.index[name])
            pe.wait_ge(S("num_done" if eng == "num" else "g_" + eng), n)

        def general(name):
            i = ring0.index[name]
            if i >= 2:
                eng, n = ring0.emptied(i - 2)
                pe.wait_ge(S("num_done" if eng == "num" else "g_" + eng), n)
            a, b = ring0.pair(name)
            return ps[:, a:b + 1, :]

        def bring(name):
            i = bring0.index[name]
            if i >= 2:
                eng, n = bring0.emptied(i - 2)
                if eng == "slope":
                    pe.wait_ge(S("prob_slope"), n * T)
                else:
                    pe.wait_ge(S("b_" + eng), n)
            a, b = bring0.pair(name)
            return ps[0:P, a:b + 1, 0:HALF]

        def as_rows(dst, cols, t):
            return pe.transpose(dst[0:RPAD, t // 4, (t % 4) * P:(t % 4 + 1) * P], cols[:, t, :], ident[0:P, 0:P])

        def spread(dst, pick, r):
            for half in range(2):
                last = pe.matmul(dst[:, half, :], pick[:, r:r + 1].broadcast_to([2 * RPAD, P]),
                                 rows[:, half * HALF:(half + 1) * HALF], start=True, stop=True)
            return last

        def project_tok(dst, actT, w, t):
            for half in range(2):
                for k in range(KT):
                    last = pe.matmul(dst[0:P, half, 0:DH], actT[:, k, t * P:(t + 1) * P], w[:, k, half * DH:(half + 1) * DH],
                                     start=k == 0, stop=k == KT - 1)
            return last

        def weights(name):
            i = W_INDEX[name]
            pe.wait_ge(S(f"w_in{i % 2}"), 16 * (i // 2 + 1))
            return wslot[i % 2]

        pe.sem_inc(S("edge_used"), NSLOT)
        pe.wait_ge(S("ident"), 1)
        for st in steps0:
            k, a = st[0], st[1:]
            if k == "ln":
                for t in range(T):
                    dst = general(("lnT", t))
                    pe.wait_ge(S("xn_tok"), t + 1)
                    for j in range(KT):
                        last = pe.transpose(dst[:, j // 3, (j % 3) * P:(j % 3 + 1) * P], xn[:, t, j * 128:(j + 1) * 128],
                                            ident[0:P, 0:P])
                    last.then_inc(S("pe_job"), 1)
            elif k == "h":
                l, t = a
                dst = general(st)
                emptied(("lnT", t) if l == 1 else ("x1T", t))
                if l == 1:
                    emptied(("lnT", max(t - 1, 0)))
                project_tok(dst, xnT if l == 1 else x1T, weights(f"W{l}"), t).then_inc(S("pe_job"), 1)
            elif k == "edges":
                emptied(("h", 1, T - 1))
                emptied(("h", 1, T - 2))

                def count(n, b, g, first=False, last=False):
                    pe.wait_ge(S("edge_hot"), n + 1)
                    for t in range(T):
                        if first:
                            pe.wait_ge(S("count_copied"), g * T + t + 1)
                        for r in range(SLOT):
                            ins = pe.matmul(ps[0:P, t, 0:HALF], shot[b][:, r, t * P:(t + 1) * P], dhot[b][:, r, :],
                                            start=first and r == 0, stop=last and r == SLOT - 1)
                        if t == T - 1:
                            ins.then_inc(S("edge_used"), 1)
                        elif last:
                            ins.then_inc(S("edge_tile"), 1)

                with pe.Fori(0, G_EDGE) as g:
                    for i in range(SPG):
                        count(g * SPG + i, i % NSLOT, g, first=i == 0, last=i == SPG - 1)
                pe.wait_ge(S("count_copied"), (G_EDGE + 1) * T)
            elif k == "mask":
                t = a[0]
                if t == 0:
                    pe.wait_ge(S("count_ready"), T)
                dst = general(st)
                for s in range(T):
                    last = pe.transpose(dst[0:P, s // 3, (s % 3) * P:(s % 3 + 1) * P], cnt[:, s, t * P:(t + 1) * P],
                                        ident[0:P, 0:P])
                last.then_inc(S("pe_job"), 1)
            elif k in ("logit", "shift"):
                l = a[0]
                name = (k + "T", l)
                dst = general(name)
                pe.wait_ge(S(k + "_cols"), l)
                for t in range(T):
                    last = as_rows(dst, logit, t)
                last.then_inc(S("pe_job"), 1)
            elif k == "asmax":
                l, h = a
                dst = bring(st)
                emptied(("logitT", l))
                spread(dst, pick[0], h).then_inc(S("pe_bjob"), 1)
            elif k == "bc":
                l, h, part = a
                emptied(("shiftT", l))
                dst = bring(("prob", l, h, part))
                spread(dst, pick[0], (2 + part) * H0 + h).then_inc(S("pe_bjob"), 1)
            elif k == "q":
                w = weights("Wq")
                dst = general(st)
                for half in range(2):
                    for c in range(KT):
                        last = pe.matmul(dst[:, half, 0:HALF], w[:, c, a[0] * 128:(a[0] + 1) * 128],
                                         xnT[:, c, half * HALF:(half + 1) * HALF], start=c == 0, stop=c == KT - 1)
                last.then_inc(S("pe_job"), 1)
            elif k in ("k", "v"):
                project_tok(general(st), xnT, weights("W" + k), a[0]).then_inc(S("pe_job"), 1)
            elif k == "agg":
                l, h = a
                j = prob_steps.index(("prob", l, h))
                pe.wait_ge(S("prob_ready"), (j + 1) * T)
                if h == 0:
                    emptied(("h", l, T - 1))
                for g, group in enumerate(AGG_GROUPS):
                    dst = general(("agg", l, h, g))
                    for i, t in enumerate(group):
                        for s in range(T):
                            last = pe.matmul(dst[0:P, i, 0:AUG0], probs[j % 2][:, s, t * P:(t + 1) * P], haug[:, s, h, :],
                                             start=s == 0, stop=s == T - 1)
                    last.then_inc(S("pe_job"), 1)
            elif k == "relu":
                emptied(("agg", 1, H0 - 1, 2))
                for t in range(T):
                    dst = general(("x1T", t))
                    for j in range(KT):
                        last = pe.transpose(dst[:, j // 3, (j % 3) * P:(j % 3 + 1) * P], x1[:, t, j * 128:(j + 1) * 128],
                                            ident[0:P, 0:P])
                    last.then_inc(S("pe_job"), 1)
            elif k == "kv":
                p = a[0]
                if p == 0:
                    pe.wait_ge(S("phi_done"), len(phis))
                    emptied(("v", T - 1))
                dst = general(st)
                pair = slice(p * 128, (p + 1) * 128)
                for t in range(T):
                    pe.matmul(dst[:, 0, 0:128], kk[:, t, pair], vv[:, t, pair], start=t == 0, stop=t == T - 1)
                for t in range(T):
                    last = pe.matmul(dst[:, 1, 0:128], kk[:, t, pair], haug[:, 0, 0, C0:AUG0].broadcast_to([P, 128]),
                                     start=t == 0, stop=t == T - 1)
                last.then_inc(S("pe_job"), 1)
            elif k == "mix":
                p = a[0]
                if p == 0:
                    emptied(("kv", KT - 1))
                for name, w in (("den", ksb), ("num", kvb)):
                    dst = general((name, p))
                    for half in range(2):
                        last = pe.matmul(dst[:, half, 0:HALF], w[:, p, :], qT[:, p, half * HALF:(half + 1) * HALF],
                                         start=True, stop=True)
                    last.then_inc(S("pe_job"), 1)
            elif k == "out":
                emptied(("num", KT - 1))
                project_tok(general(st), qT, weights("Wo"), a[0]).then_inc(S("pe_job"), 1)

        if stop == 0:
            return
        for t in range(T):
            a = 2 * (t % 2)
            pe.wait_ge(S("xn_tok"), T + t + 1)
            if t >= 2:
                pe.wait_ge(S("xl1"), t - 1)
            for j in range(KT):
                last = pe.transpose(ps[:, a + j // 3, (j % 3) * P:(j % 3 + 1) * P], xn2[:, t, j * 128:(j + 1) * 128],
                                    ident[0:P, 0:P])
            last.then_inc(S("lnT1"), 1)
        pe.wait_ge(S("xl1"), T)
        pe.wait_ge(S("router_lo"), 1)
        for t in range(T):
            cols = slice(t * P, (t + 1) * P)
            terms = [(xh, rwh), (xh, rwl), (xl, rwh)]
            for k in range(KT):
                for n, (l_, r_) in enumerate(terms):
                    last = pe.matmul(ps[0:P, 4, t * NEXP0:(t + 1) * NEXP0], l_[:, k, cols], r_[:, k, :],
                                     start=(k == 0 and n == 0), stop=(k == KT - 1 and n == 2))
        last.then_inc(S("router_job"), 1)

        def up(c, b, first=False):
            pe.wait_ge(S("w1_lo"), c + 1)
            for j in range(2):
                if not first:
                    pe.wait_ge(S("gelu"), 2 * c + j - 1)
                m = slice(j * 128, (j + 1) * 128)
                for k in range(KT):
                    for w, xs in ((w1hi[b], (xh, xl)), (w1lo[b], (xh,))):
                        for xx in xs:
                            for half in range(2):
                                last = pe.matmul(ps[:, 2 * j + half, 0:HALF], w[:, k, m], xx[:, k, half * HALF:(half + 1) * HALF],
                                                 start=(k == 0 and w is w1hi[b] and xx is xh),
                                                 stop=(k == KT - 1 and w is w1lo[b]))
                last.then_inc(S("hid_job"), 1)

        def down(c, b):
            pe.wait_ge(S("hid_lo"), 2 * c + 2)
            pe.wait_ge(S("w2_lo"), c + 1)
            for t in range(T):
                a = 4 + 2 * ((T * b + t) % 2)
                pe.wait_ge(S("out_added"), T * c + t + 1)
                cols = slice(t * P, (t + 1) * P)
                for j in range(2):
                    for hh, ws in ((hidh[b], (w2hi[b], w2lo[b])), (hidl[b], (w2hi[b],))):
                        for w in ws:
                            for half in range(2):
                                last = pe.matmul(ps[0:P, a + half, 0:DH], hh[:, j, cols], w[:, j, half * DH:(half + 1) * DH],
                                                 start=(j == 0 and hh is hidh[b] and w is w2hi[b]),
                                                 stop=(j == 1 and hh is hidl[b]))
                last.then_inc(S("out_job"), 1)

        pe.wait_ge(S("pads"), 2)
        pe.sem_inc(S("out_job"), T)
        up(0, 0, first=True)
        with pe.Fori(0, NCH // 2 - 1) as i:
            for b in range(2):
                c = i * 2 + b
                up(c + 1, 1 - b)
                down(c, b)
        up(NCH - 1, 1)
        down(NCH - 2, 0)
        down(NCH - 1, 1)
        if stop == 1:
            return

        def emptied1(name):
            eng, n = ring1.emptied(ring1.index[name])
            pe.wait_ge(S("g1_" + eng), n)

        def general1(name):
            i = ring1.index[name]
            if i >= 2:
                eng, n = ring1.emptied(i - 2)
                pe.wait_ge(S("g1_" + eng), n)
            a, b = ring1.pair(name)
            return ps[:, a:b + 1, :]

        def bring_1(name):
            i = bring1.index[name]
            if i >= 2:
                eng, n = bring1.emptied(i - 2)
                if eng == "slope":
                    pe.wait_ge(S("prob_slope1"), n * T)
                else:
                    pe.wait_ge(S("b1_" + eng), n)
            a, b = bring1.pair(name)
            return ps[0:P, a:b + 1, 0:HALF]

        def weights1(i):
            pe.wait_ge(S(f"w_in{i % 2}"), 16 * (3 + i // 2 + 1))
            return wslot[i % 2]

        def transposed(dst, src, t):
            for j in range(KT):
                last = pe.transpose(dst[:, j // 3, (j % 3) * P:(j % 3 + 1) * P], src[:, t, j * 128:(j + 1) * 128],
                                    ident[0:P, 0:P])
            return last

        def dash(dst, srcT, j):
            for i, (h, t) in enumerate(units(j)):
                last = pe.matmul(dst[0:P, i // 2, (i % 2) * M1:(i % 2 + 1) * M1], srcT[:, h // 2, t * P:(t + 1) * P],
                                 projT[:, h % 2, :], start=True, stop=True)
            return last

        for st in steps1:
            k, a = st[0], st[1:]
            if k == "ln":
                for t in range(T):
                    dst = general1(("lnT", t))
                    pe.wait_ge(S("xn_tok"), 2 * T + t + 1)
                    transposed(dst, xn3, t).then_inc(S("pe_job1"), 1)
                pe.wait_ge(S("count1"), T)
                for t in range(T):
                    last = pe.transpose(ps[0:P, 4 + t // 4, (t % 4) * P:(t % 4 + 1) * P], cnt[:, t, t * P:(t + 1) * P],
                                        ident[0:P, 0:P])
                last.then_inc(S("diag_job"), 1)
            elif k == "ft":
                t, g = a
                if t == 0:
                    pe.wait_ge(S("gat1_in"), 16 * 7)
                    emptied1(("lnT", T - 1))
                    emptied1(("lnT", T - 2))
                dst = general1(st)
                for q_ in range((4, 2)[g]):
                    c = 4 * g + q_
                    last = pe.matmul(dst[0:P, q_ // 2, (q_ % 2) * 256:(q_ % 2 + 1) * 256], xnT[:, c, t * P:(t + 1) * P],
                                     wblk[:, :], start=True, stop=True)
                last.then_inc(S("pe_job1"), 1)
            elif k == "logit":
                dst = general1(("wal",))
                pe.matmul(dst[:, 0, 0:2 * H1], wpair[:, :], attn[:, :], start=True, stop=True).then_inc(S("pe_job1"), 1)
                dst = general1(("logit",))
                emptied1(("wal",))
                for t in range(T):
                    for c in range(KT):
                        last = pe.matmul(dst[0:P, 0, t * 2 * H1:(t + 1) * 2 * H1], xnT[:, c, t * P:(t + 1) * P], wab[:, c, :],
                                         start=c == 0, stop=c == KT - 1)
                last.then_inc(S("pe_job1"), 1)
                dst = general1(("logitT",))
                emptied1(("logit",))
                for t in range(T):
                    last = as_rows(dst, acol, t)
                last.then_inc(S("pe_job1"), 1)
            elif k == "shift":
                dst = general1(("shiftT",))
                pe.wait_ge(S("shift1"), 1)
                for t in range(T):
                    last = as_rows(dst, shiftb, t)
                last.then_inc(S("pe_job1"), 1)
            elif k in ("asmax", "bc"):
                h = a[0]
                emptied1(("logitT",) if k == "asmax" else ("shiftT",))
                if k == "asmax" and h == 0:
                    pe.wait_ge(S("far1"), 1)
                name, r = (st, h) if k == "asmax" else (("prob", h, a[1]), H1 * a[1] + h)
                dst = bring_1(name)
                spread(dst, pick[1], r).then_inc(S("pe_bjob1"), 1)
            elif k in ("q", "k"):
                m = a[0]
                w = weights1(0 if k == "q" else 1)
                dst = general1(st)
                for half in range(2):
                    for c in range(KT):
                        last = pe.matmul(dst[:, half, 0:HALF], w[:, c, m * 128:(m + 1) * 128],
                                         xnT[:, c, half * HALF:(half + 1) * HALF], start=c == 0, stop=c == KT - 1)
                last.then_inc(S("pe_job1"), 1)
            elif k == "sq":
                dst = general1(st)
                emptied1(a)
                n = sq_jobs.index(st)
                for t in range(T):
                    last = pe.matmul(dst[0:P, 0, 2 * t:2 * t + 2], sq[n % 2][:, t * P:(t + 1) * P], halves[:, :], start=True, stop=True)
                last.then_inc(S("pe_job1"), 1)
            elif k == "v":
                project_tok(general1(st), xnT, weights1(2), a[0]).then_inc(S("pe_job1"), 1)
            elif k == "agg":
                h = a[0]
                pe.wait_ge(S("prob_ready1"), (h + 1) * T)
                dst = general1(st)
                for t in range(T):
                    for s in range(T):
                        last = pe.matmul(dst[0:P, 0, t * AUG1:(t + 1) * AUG1], probs[h % 2][:, s, t * P:(t + 1) * P],
                                         ft[:, s, h, :], start=s == 0, stop=s == T - 1)
                last.then_inc(S("pe_job1"), 1)
            elif k == "kmax":
                pe.wait_ge(S("proj_in"), 32)
                dash(general1(st), k1T, a[0]).then_inc(S("pe_job1"), 1)
            elif k == "kstab":
                dst = general1(("kstabT",))
                pe.wait_ge(S("kmax_head"), 1)
                pe.transpose(dst[0:H1, 0, 0:P], kmaxh[:, :], ident[0:P, 0:P]).then_inc(S("pe_job1"), 1)
                dst = general1(("kstabB",))
                emptied1(("kstabT",))
                pe.matmul(dst[0:P, 0, 0:H1], gmax[:, :].broadcast_to([H1, P]), ident[0:H1, 0:H1], start=True,
                          stop=True).then_inc(S("pe_job1"), 1)
            elif k == "kexp":
                dash(general1(st), k1T, a[0]).then_inc(S("pe_job1"), 1)
            elif k == "ctx":
                h = a[0]
                i = cring.index[st]
                if i >= 2:
                    pe.wait_ge(S("ctx_ready"), i - 1)
                else:
                    pe.wait_ge(S("prob_slope1"), H1 * T)
                pe.wait_ge(S("kp_ready"), (T * (h + 1) - 1) // UPJ + 1)
                b = cring.pair(st)[0]
                for m in range(2):
                    for t in range(T):
                        last = pe.matmul(ps[:, b, m * AUG1:(m + 1) * AUG1], kp[:, (T * h + t) % (5 * UPJ), m * 128:(m + 1) * 128],
                                         v1[:, t, h, :], start=t == 0, stop=t == T - 1)
                last.then_inc(S("pe_cjob"), 1)
            elif k == "qexp":
                dash(general1(st), q1T, a[0]).then_inc(S("pe_job1"), 1)
            elif k == "qpT":
                j = a[0]
                emptied1(("qexp", j))
                if j >= 1:
                    pe.wait_ge(S("qpT_ready"), j)
                lo, _ = tring.pair(st)
                for i in range(UPJ):
                    for m in range(2):
                        q_ = 2 * i + m
                        last = pe.transpose(ps[:, lo + q_ // 4, (q_ % 4) * P:(q_ % 4 + 1) * P],
                                            qp[:, (j % 3) * UPJ + i, m * 128:(m + 1) * 128], ident[0:P, 0:P])
                last.then_inc(S("pe_tjob"), 1)
            elif k == "mo":
                j = a[0]
                pe.wait_ge(S("qpT_ready"), j + 1)
                if j == 0:
                    pe.wait_ge(S("ctx_ready"), H1)
                if j >= 2:
                    pe.wait_ge(S("mo_ready"), j - 1)
                b = oring.pair(st)[0]
                for i, (h, t) in enumerate(units(j)):
                    for m in range(2):
                        last = pe.matmul(ps[0:P, b, i * AUG1:(i + 1) * AUG1], qpT[:, j % 2, i, m, :], ctx[:, h, m, :],
                                         start=m == 0, stop=m == 1)
                last.then_inc(S("pe_ojob"), 1)
            elif k == "oT":
                dst = general1(st)
                pe.wait_ge(S("mo_ready"), NJ)
                transposed(dst, mo, a[0]).then_inc(S("pe_job1"), 1)
            elif k == "wo":
                emptied1(("oT", T - 1))
                emptied1(("oT", T - 2))
                project_tok(general1(st), moT, weights1(3), a[0]).then_inc(S("pe_job1"), 1)
        for t in range(T):
            lo = 2 * (t % 2)
            pe.wait_ge(S("xn_tok"), 3 * T + t + 1)
            if t >= 2:
                pe.wait_ge(S("xT4"), t - 1)
            transposed(ps[:, lo:lo + 2, :], xn4, t).then_inc(S("lnT4"), 1)
        pe.wait_ge(S("xT4"), T)
        pe.wait_ge(S("ffn1_in"), 16 * (KT + 2))
        for t in range(T):
            for c in range(KT):
                last = pe.matmul(ps[0:P, 4, t * E1:(t + 1) * E1], xnT[:, c, t * P:(t + 1) * P], r1[:, c, :],
                                 start=c == 0, stop=c == KT - 1)
        last.then_inc(S("router1_job"), 1)

        def hidden(m):
            lo = 2 * (m % 2)
            if m >= 2:
                pe.wait_ge(S("silu"), m - 1)
            for half in range(2):
                for c in range(KT):
                    last = pe.matmul(ps[:, lo + half, 0:HALF], f1[:, c, 2 * m:2 * m + 2, :].rearrange("p e i -> p (e i)"),
                                     xnT[:, c, half * HALF:(half + 1) * HALF], start=c == 0, stop=c == KT - 1)
            last.then_inc(S("hid1_job"), 1)

        hidden(0)
        hidden(1)
        pe.wait_ge(S("mask1"), 1)
        for t in range(T):
            last = pe.transpose(ps[0:E1, 6 + t // 4, (t % 4) * P:(t % 4 + 1) * P], mk[:, t, :], ident[0:P, 0:P])
        last.then_inc(S("mask1T"), 1)
        hidden(2)
        hidden(3)
        pe.wait_ge(S("mask1_rows"), 1)
        for m in range(4):
            lo = 4 + 2 * (m % 2)
            if m >= 2:
                pe.wait_ge(S("hid1"), m - 1)
            for half in range(2):
                last = pe.matmul(ps[:, lo + half, 0:HALF],
                                 sel1[:, m * 128:(m + 1) * 128],
                                 mkT[:, half * HALF:(half + 1) * HALF], start=True, stop=True)
            last.then_inc(S("mask1_bc"), 1)
        pe.wait_ge(S("hid1"), 4)
        for t in range(T):
            lo = 2 * (t % 4)
            if t >= 4:
                pe.wait_ge(S("x_out"), t - 3)
            for half in range(2):
                for m in range(4):
                    last = pe.matmul(ps[0:P, lo + half, 0:DH], hid1[:, m, t * P:(t + 1) * P], f2[:, m, half * DH:(half + 1) * DH],
                                     start=m == 0, stop=m == 3)
            last.then_inc(S("out1_job"), 1)

    block.__exit__(None, None, None)


_INS = ["x", "src", "dst", "L0_gnn_W1", "L0_gnn_a_src1", "L0_gnn_a_dst1", "L0_gnn_b1", "L0_gnn_W2", "L0_gnn_a_src2",
        "L0_gnn_a_dst2", "L0_gnn_b2", "L0_mix_W_qkv", "L0_mix_W_out", "L0_mix_b_out", "L0_ffn_w1", "L0_ffn_w2",
        "L1_gnn_W", "L1_mix_Wq", "L1_mix_Wk", "L1_mix_Wv", "L1_mix_Wo", "L1_ffn_w1"]


def lay_out(inputs):
    arrays = {n: np.asarray(inputs[n]) for n in _INS}
    for n in ("L0_gnn_a_src1", "L0_gnn_a_dst1", "L0_gnn_a_src2", "L0_gnn_a_dst2"):
        arrays[n] = arrays[n].reshape(-1)
    arrays["L0_ffn_router_wT"] = np.asarray(inputs["L0_ffn_router_w"]).T
    arrays["L1_gnn_WT"] = np.asarray(inputs["L1_gnn_W"]).T
    arrays["L1_gnn_W_resT"] = np.asarray(inputs["L1_gnn_W_res"]).T
    arrays["L1_gnn_attnT"] = np.concatenate([np.asarray(inputs["L1_gnn_attn_l"])[0], np.asarray(inputs["L1_gnn_attn_r"])[0]]).T
    arrays["L1_mix_projT"] = np.asarray(inputs["L1_mix_proj"]).T
    arrays["L1_ffn_router_wT"] = np.asarray(inputs["L1_ffn_router_w"]).T
    arrays["L1_ffn_w2"] = np.asarray(inputs["L1_ffn_w2"]).reshape(E1 * I1, D)
    return {n: np.ascontiguousarray(a) for n, a in arrays.items()}


def kernel(**inputs):
    import concourse.bacc as bacc
    from concourse.bass_utils import run_bass_kernel_spmd

    nc = bacc.Bacc("TRN2", target_bir_lowering=False, num_devices=1)
    arrays = lay_out(inputs)
    dram = {n: nc.dram_tensor("in_" + n, a.shape, mybir.dt.from_np(a.dtype), kind="ExternalInput").ap() for n, a in arrays.items()}
    result = nc.dram_tensor("out_x", [N, D], FP32, kind="ExternalOutput").ap()
    build(nc, dram, {"out": result})
    r = run_bass_kernel_spmd(nc, [{"in_" + n: a for n, a in arrays.items()}], core_ids=[0])
    return r.results[0]["out_x"]
```

```python
import numpy as np
import concourse.bass as bass
from concourse import mybir

FP32 = mybir.dt.float32
FP32R = mybir.dt.float32r
FP16 = mybir.dt.float16
BF16 = mybir.dt.bfloat16
I32 = mybir.dt.int32
ALU = mybir.AluOpType
ACT = mybir.ActivationFunctionType
AX = mybir.AxisListType

N = 625
D = 768
P = 125
T = N // P
KT = D // 128
NP = 628
HALF = NP // 2
DH = D // 2
E = 20625
EC = E // P
G_EDGE = 7
CPG = 24
ECP = G_EDGE * CPG
SLOT = 4
NSLOT = 3
SPG = CPG // SLOT
PACK = 4096.0
FAR = -1.0e30
LN_EPS = 1e-5
SLOPE = 0.2
H0 = 4
C0 = D // H0
AUG0 = C0 + 1
MIX_EPS = 1e-6
NEXP0 = 16
TOPK0 = 8
WIDTHS = [512] * 8 + [1024] * 8
CH = 256
NCH = sum(WIDTHS) // CH
H1 = 12
C1 = D // H1
AUG1 = C1 + 1
M1 = 256
K_EPS = 1e-4
E1 = 8
I1 = 64
RPAD = 32

assert CPG * P < PACK and ECP >= EC and SPG % NSLOT == 0
assert E == EC * P and N == T * P and D == KT * 128


class Ring:

    def __init__(self, pairs, jobs):
        self.pairs = pairs
        self.jobs = jobs
        self.index = {name: i for i, (name, _) in enumerate(jobs)}
        assert len(self.index) == len(jobs)

    def pair(self, name):
        return self.pairs[self.index[name] % len(self.pairs)]

    def emptied(self, i):
        engine = self.jobs[i][1]
        return engine, sum(1 for _, e in self.jobs[:i + 1] if e == engine)


def gat_schedule0():
    def prob(l, h, fill, agg):
        return [("bc", l, h, 0), ("lin", l, h)] + fill[:1] + [("bc", l, h, 1), ("prob", l, h)] + fill[1:] + agg

    steps = [("ln", 0)] + [("h", 1, t) for t in range(T)] + [("edges",)] + [("lg", 1, t) for t in range(T)]
    steps += [("q", 0), ("q", 1), ("logit", 1), ("q", 2), ("q", 3)] + [("mask", t) for t in range(T)]
    steps += [("asmax", 1, 0), ("asmax", 1, 1), ("q", 4), ("asmax", 1, 2), ("q", 5), ("asmax", 1, 3), ("k", 0)]
    steps += [("shift", 1), ("k", 1)]
    steps += prob(1, 0, [("k", 2)], [])
    steps += prob(1, 1, [("k", 3), ("k", 4)], [("agg", 1, 0)])
    steps += prob(1, 2, [("v", 0), ("v", 1)], [("agg", 1, 1)])
    steps += prob(1, 3, [("v", 2), ("v", 3)], [("agg", 1, 2)])
    steps += [("v", 4), ("agg", 1, 3)] + [("kv", p) for p in range(KT)] + [("mix", 0), ("relu",), ("mix", 1)]
    for t in range(T):
        steps += [("h", 2, t), ("lg", 2, t)] + [("mix", t + 2)] * (t + 2 < KT)
    steps += [("out", 0), ("logit", 2), ("asmax", 2, 0), ("asmax", 2, 1), ("out", 1), ("asmax", 2, 2), ("asmax", 2, 3),
              ("out", 2), ("shift", 2)]
    for h in range(H0):
        steps += [("bc", 2, h, 0), ("bc", 2, h, 1), ("lin", 2, h), ("prob", 2, h)]
        steps += {0: [("out", 3)], 3: [("out", 4)]}.get(h, [])
        if h:
            steps += [("agg", 2, h - 1)]
    steps += [("agg", 2, H0 - 1)]
    return steps


AGG_GROUPS = [(0, 1, 2, 3), (4,)]

UPJ = 4
NJ = H1 * T // UPJ


def units(j):
    return [divmod(u, T) for u in range(UPJ * j, UPJ * (j + 1))]


def gat_schedule1():
    steps = [("ln",)] + [("ft", t, g) for t in range(T) for g in range(2)] + [("logit",)]
    for m in range(KT):
        steps += [("asmax", 2 * m), ("asmax", 2 * m + 1), ("q", m)]
        if m:
            steps += [("sq", "q", m - 1)]
    steps += [("sq", "q", KT - 1), ("k", 0), ("shift",)]
    fill = [("k", m) for m in range(1, KT)] + [("v", t) for t in range(T)]
    for h in range(H1):
        steps += [("bc", h, 0), ("bc", h, 1), ("lin", h)]
        if h >= 2:
            steps += [("tok", h - 2)]
        steps += [("prob", h)]
        if h:
            steps += [("agg", h - 1)]
        steps += fill[h:h + 1]
        if h < KT:
            steps += [("sq", "k", h)]
    steps += [("tok", H1 - 2), ("agg", H1 - 1)]
    steps += [("kmax", 0), ("tok", H1 - 1)] + [("kmax", j) for j in range(1, NJ)]
    steps += [("qmax", 0), ("kstab",), ("qmax", 1), ("qmax", 2), ("kstabs",), ("qmax", 3)]
    ready = []
    for j in range(NJ + 2):
        if j < NJ:
            steps += [("kexp", j)]
        if j + 4 < NJ:
            steps += [("qmax", j + 4)]
        if j == NJ - 2:
            steps += [("qrow",)]
        steps += [("ctxt", h) for h in ready]
        ready = [h for h in range(H1) if UPJ * (j - 1) < (h + 1) * T <= UPJ * j] if j else []
        steps += [("ctx", h) for h in ready]
    steps += [("ctxt", h) for h in ready]
    for h in range(H1 + 2):
        if h < H1:
            steps += [("dash", h, 0), ("dash", h, 1)]
        if h >= 2:
            steps += [("mo", h - 2)]
            if h % 2:
                steps += [("norm", (h - 3) // 2)]
    steps += [("wo", t) for t in range(T)]
    return steps


def build(nc, dram, out):
    sbase = 16512
    off = {}
    at = sbase
    for name, size in [("x", 15360), ("T1", 15072), ("C", 12576), ("MASK", 6304), ("W0", 18432), ("W1", 18432),
                       ("H", 15616), ("A", 25152), ("E2", 5024), ("Q", 15072), ("K", 15360), ("V", 15616),
                       ("KB", 6144), ("TM", 15360), ("B1", 3072), ("AROW", 6144)]:
        off[name] = at
        assert at % 32 == 0
        at += size
    small = [at]

    def place(name, shape, dtype, region, extra=0):
        return nc.alloc_sbuf_tensor_at(name, shape, dtype, offset=off[region] + extra, align_bytes=16)

    def tiny(name, shape, dtype):
        size = int(np.prod(shape[1:])) * (2 if dtype in (FP16, BF16) else 4)
        t = nc.alloc_sbuf_tensor_at(name, shape, dtype, offset=small[0], align_bytes=4)
        small[0] += (size + 3) // 4 * 4
        assert small[0] <= 229368, small[0]
        return t

    x = place("x_res", [P, T, D], FP32, "x")
    cnt = place("edge_count", [P, T, NP], FP32, "C")
    far = place("far", [P, T, NP], BF16, "MASK")
    ident = tiny("ident", [128, 128], FP32)
    eps_ln = tiny("eps_ln", [128, 1], FP32)
    stats = tiny("ln_stats", [P, T, 2, 6], FP32)
    mv = tiny("ln_mean_var", [P, T, 2], FP32)
    std = tiny("ln_std", [P, T], FP32)
    rstd = tiny("ln_rstd", [P, T], FP32)
    nmr = tiny("ln_shift", [P, T], FP32)
    layer_small = small[0]
    rows = tiny("rows", [2 * RPAD, NP], FP32R)
    logit = tiny("logit_cols", [P, T, RPAD], FP32)
    as02 = place("as_slope", [P, T, H0], FP32, "H", 15440)
    asmax = place("as_max", [P, T, H0], FP32, "H", 15520)
    mcol = place("m_col", [P, T, H0], FP32, "V", 15488)
    recip = place("recip", [P, 8], FP32, "V", 15568)
    pick = {0: place("pick_row0", [2 * RPAD, RPAD], FP32R, "V", 15360), 1: place("pick_row1", [2 * RPAD, RPAD], FP32R, "AROW", 1280)}
    xn = place("xn_tok", [P, T, D], FP32, "TM")
    xnT = place("xn_T", [128, KT, NP], FP32, "T1")
    x1 = place("gat1_tok", [P, T, D], FP32, "TM")
    x1T = place("gat1_T", [128, KT, NP], FP32, "T1")
    wslot = [place("w_slot0", [128, KT, D], FP32, "W0"), place("w_slot1", [128, KT, D], FP32, "W1")]
    haug = place("h_aug", [P, T, H0, AUG0], FP32, "H")
    probs = [place(f"gat_prob{i}", [P, T, NP], FP32, "A", i * 12576) for i in range(2)]
    e2 = [place(f"gat_slope{i}", [P, NP], FP32, "E2", i * 2512) for i in range(2)]
    junk = place("junk", [P, 2 * NP], FP32, "E2")
    qT = place("q_T", [128, KT, NP], FP32, "Q")
    kk = place("k_tok", [P, T, D], FP32, "K")
    vv = place("v_tok", [P, T, D], FP32, "V")
    phie = [place(f"phi_exp{i}", [128, D], FP32, "KB", i * 3072) for i in range(2)]
    kvb = place("kv_blocks", [128, KT, 128], FP32, "KB")
    ksb = place("ksum_blocks", [128, KT, 128], FP32, "KB", 3072)
    den = [place(f"mix_den{i}", [128, NP], FP32, "K", i * 2528) for i in range(2)]
    b1 = place("b1_rows", [P, D], FP32, "B1")
    b2 = place("b2_rows", [P, D], FP32, "A")
    bo = place("bo_rows", [P, D], FP32, "A", 3072)
    arow = place("a_rows", [P, 2, D], FP32, "AROW")
    craw = place("count_raw", [P, T, HALF], FP32, "K")
    chi = place("count_hi", [P, T, HALF], I32, "K", 6304)
    chif = place("count_hi_float", [P, T, HALF], FP32, "TM")
    hot_at = [("Q", 0), ("Q", 7520), ("A", 6144)]
    shot = [place(f"src_onehot{i}", [P, SLOT, 626], FP16, *hot_at[i]) for i in range(NSLOT)]
    dhot = [place(f"dst_onehot{i}", [P, SLOT, HALF], FP16, hot_at[i][0], hot_at[i][1] + 5008) for i in range(NSLOT)]
    iota16 = place("iota16", [P, NP], FP16, "V", 7552)
    ids = place("ids", [P, 2, ECP], I32, "V", 8832)
    sid = place("src_id", [P, ECP], FP32, "V", 10176)
    dlo = place("dst_lo", [P, ECP], FP32, "V", 10848)
    dwt = place("dst_weight", [P, ECP], FP32, "V", 11520)
    did = place("dst_id", [P, ECP], FP32, "V", 12192)

    small[0] = layer_small
    xh = place("x_hi", [128, KT, NP], FP32R, "T1")
    xl = place("x_lo", [128, KT, NP], FP32R, "Q")
    xn2 = place("xn2_tok", [P, T, D], FP32, "TM")
    w1raw = [place(f"w1_raw{i}", [128, KT, CH], FP32, f"W{i}") for i in range(2)]
    w1hi = [place(f"w1_hi{i}", [128, KT, CH], FP32R, f"W{i}", 6144) for i in range(2)]
    w1lo = [place(f"w1_lo{i}", [128, KT, CH], FP32R, f"W{i}", 12288) for i in range(2)]
    w2raw = [place(f"w2_raw{i}", [128, 2, D], FP32, ("A", "K")[i]) for i in range(2)]
    w2hi = [place(f"w2_hi{i}", [128, 2, D], FP32R, ("A", "K")[i], 6144) for i in range(2)]
    w2lo = [place(f"w2_lo{i}", [128, 2, D], FP32R, ("A", "K")[i], 12288) for i in range(2)]
    hid = [place(f"hid{i}", [128, 2, NP], FP32, ("H", "TM")[i]) for i in range(2)]
    hidh = [place(f"hid_hi{i}", [128, 2, NP], FP32R, ("H", "TM")[i], 5024) for i in range(2)]
    hidl = [place(f"hid_lo{i}", [128, 2, NP], FP32R, ("H", "TM")[i], 10048) for i in range(2)]
    rw = place("router0", [128, KT, NEXP0], FP32, "KB")
    rwh = place("router0_hi", [128, KT, NEXP0], FP32R, "KB", 384)
    rwl = place("router0_lo", [128, KT, NEXP0], FP32R, "KB", 768)
    pr = place("router0_prob", [P, T, NEXP0], FP32, "KB", 1152)
    rest = place("router0_rest", [P, T, NEXP0], FP32, "KB", 1472)
    top = place("router0_top", [P, T, 8], FP32, "KB", 1792)
    col = [place(f"router0_col{i}", [P, T], FP32, "KB", 1952 + 32 * i) for i in range(2)]
    comb = place("router0_comb", [P, T, NCH], FP32, "KB", 2048)
    rrow = place("router0_rows", [NEXP0, NP], FP32, "KB", 3072)

    ft = place("ft_aug", [P, T, H1, AUG1], FP32, "H")
    res = place("gat_res", [P, T, D], FP32, "TM")
    xn3 = place("xn3_tok", [P, T, D], FP32, "H")
    q1T = place("q1_T", [128, KT, NP], FP32, "Q")
    k1T = place("k1_T", [128, KT, NP], FP32, "K")
    v1 = place("v1_aug", [P, T, H1, AUG1], FP32, "V")
    sq = [place(f"sq{i}", [128, NP], FP32, "KB", i * 2528) for i in range(2)]
    wblk = place("wt_blocks", [128, 256], FP32, "B1")
    wab = place("logit_weights", [128, KT, RPAD], FP32, "B1", 1024)
    wpair = place("w_pair", [64, 128], FP32, "B1", 1792)
    attn = place("attn_T", [64, 2 * H1], FP32, "B1", 2304)
    halves = place("half_ones", [128, 2], FP32, "B1", 2400)
    projT = place("proj_T", [128, 2, M1], FP32, "MASK")
    acol = place("logit1_cols", [P, T, RPAD], FP32, "AROW", 0)
    as02b = place("as1_slope", [P, T, H1], FP32, "AROW", 1504)
    asmaxb = place("as1_max", [P, T, H1], FP32, "AROW", 1744)
    mcolb = place("m1_col", [P, T, H1], FP32, "AROW", 1984)
    shiftb = place("shift1_cols", [P, T, RPAD], FP32, "AROW", 640)
    diag = {"q": place("diag_q", [P, H1, T], FP32, "AROW", 2704), "k": place("diag_k", [P, H1, T], FP32, "AROW", 2944)}
    kmax = place("k_max", [P, H1, T], FP32, "AROW", 3184)
    kmaxh = place("k_max_head", [P, H1], FP32, "AROW", 3424)
    gmax = place("k_max_all", [H1, 1], FP32, "AROW", 3472)
    nstab = place("k_bias", [P, H1, T], FP32, "AROW", 3488)
    qmax = place("q_max", [P, H1, T], FP32, "AROW", 3728)
    kmaxb = place("k_max_everywhere", [P, H1], FP32, "AROW", 4208)
    aggr = place("agg1_recip", [P, T, 1], FP32, "AROW", 4256)
    aggv = place("agg1_value", [P, T, C1], FP32, "AROW", 4288)
    kp_at = [("W0", 3), ("TM", 3), ("A", 6), ("H", 3)]
    kp = []
    for region, jobs_ in kp_at:
        kp += [place(f"k_prime{len(kp) + i}", [P, UPJ, M1], FP32, region, i * UPJ * M1 * 4) for i in range(jobs_)]
    assert len(kp) == NJ
    qp = [place(f"q_prime{i}", [128, 2, NP], FP32, "TM", i * 5024) for i in range(3)]
    ctx = place("performer_ctx", [128, H1, 2, 2 * C1], FP32, "C")
    ctxT = [place(f"performer_ctx_T{i}", [AUG1, M1], FP32, "MASK", 2048 + i * 1024) for i in range(2)]
    moden = [place(f"performer_den{i}", [128, NP], FP32, "E2", i * 2512) for i in range(2)]
    lrow = place("logit_rows", [RPAD, NP], FP32, "A")
    aggT = place("agg1_T", [AUG1, NP], FP32, "MASK", 2048)
    moT = place("performer_T", [128, KT, NP], FP32, "H")
    xn4 = place("xn4_tok", [P, T, D], FP32, "TM")
    f1 = place("experts1_w1", [128, KT, E1, I1], FP32, "W0")
    f2 = place("experts1_w2", [128, 4, D], FP32, "K")
    r1 = place("router1", [128, KT, E1], FP32, "KB")
    p1 = place("router1_prob", [P, T, E1], FP32, "KB", 192)
    t1 = place("router1_top", [P, T, 8], FP32, "KB", 352)
    i1 = place("router1_index", [P, T, 8], mybir.dt.uint32, "KB", 512)
    f1i = place("router1_index_f", [P, T, 2], FP32, "KB", 672)
    mk = place("router1_mask", [P, T, E1], FP32, "KB", 720)
    c1 = [place(f"router1_col{i}", [P, T], FP32, "KB", 880 + 32 * i) for i in range(3)]
    io8 = place("iota8", [P, E1], FP32, "KB", 976)
    mkT = place("router1_mask_T", [E1, NP], FP32, "KB", 1024)
    sel1 = place("expert_rows", [E1, E1 * I1], FP32, "KB", 3552)
    f1h = place("experts1_w1_hi", [128, KT, E1, I1], FP32R, "A")
    f1l = place("experts1_w1_lo", [128, KT, E1, I1], FP32R, "V")
    r1h = place("router1_hi", [128, KT, E1], FP32R, "KB", 5600)
    r1l = place("router1_lo", [128, KT, E1], FP32R, "KB", 5792)
    rrow1 = place("router1_rows", [E1, NP], FP32, "E2")
    hid1 = place("hid1_T", [128, 4, NP], FP32, "A", 12288)

    ps = nc.alloc_psum_tensor("ps", [128, 8, 512], FP32)

    sems = {}

    def S(name):
        if name not in sems:
            sems[name] = nc.alloc_semaphore("s_" + name)
        return sems[name]

    steps0 = gat_schedule0()
    jobs = []
    bjobs = []
    for st in steps0:
        k, a = st[0], st[1:]
        if k == "ln":
            jobs += [(("lnT", t), "act" if t % 2 else "dve") for t in range(T)]
        elif k == "h":
            jobs += [(("h",) + a, "act")]
        elif k == "mask":
            jobs += [(("mask",) + a, "dve")]
        elif k == "logit":
            jobs += [(("logitT",) + a, "dve")]
        elif k == "asmax":
            bjobs += [(("asmax",) + a, "dve")]
        elif k == "shift":
            jobs += [(("shiftT",) + a, "dve")]
        elif k == "prob":
            bjobs += [(("prob",) + a + (0,), "act"), (("prob",) + a + (1,), "slope")]
        elif k in ("q", "k", "v"):
            jobs += [((k,) + a, "act")]
        elif k == "agg":
            jobs += [(("agg",) + a + (j,), "dve") for j in range(len(AGG_GROUPS))]
        elif k == "relu":
            jobs += [(("x1T", t), "act") for t in range(T)]
        elif k == "kv":
            jobs += [(("kv",) + a, "dve")]
        elif k == "mix":
            jobs += [(("den",) + a, "act"), (("num",) + a, "num")]
        elif k == "out":
            jobs += [(("out",) + a, "dve")]
    ring0 = Ring([(0, 1), (2, 3)], jobs)
    steps1 = gat_schedule1()
    jobs1, bjobs1, cjobs = [], [], []
    for st in steps1:
        k, a = st[0], st[1:]
        if k == "ln":
            jobs1 += [(("lnT", t), "act" if t % 2 else "dve") for t in range(T)]
        elif k == "logit":
            jobs1 += [(("wal",), "dve"), (("logitT",), "dve"), (("logit",), "dve")]
        elif k == "shift":
            jobs1 += [(("shiftT",), "dve")]
        elif k == "asmax":
            bjobs1 += [(st, "dve")]
        elif k == "prob":
            bjobs1 += [(st + (0,), "act"), (st + (1,), "slope")]
        elif k in ("ft", "q", "k", "v", "kmax", "dash", "agg"):
            jobs1 += [(st, "dve" if k == "ft" and a[1] else "act")]
        elif k in ("sq", "tok", "qmax", "kstab", "kstabs", "qrow", "wo"):
            jobs1 += [(st, "dve")]
        elif k in ("ctx", "ctxt"):
            cjobs += [(st, "dve")]
    ring1 = Ring([(0, 1), (2, 3)], jobs1)
    bring1 = Ring([(4, 5), (6, 7)], bjobs1)
    cring = Ring([(6,), (7,)], cjobs)
    bring0 = Ring([(4, 5), (6, 7)], bjobs)

    phis = [st for st in steps0 if st[0] in ("q", "k")]
    prob_steps = [st for st in steps0 if st[0] == "prob"]

    def feat(ap):
        return ap.rearrange("(k p) n -> p k n", p=128)

    W_ORDER = [("W1", dram["L0_gnn_W1"]), ("Wq", dram["L0_mix_W_qkv"][:, 0:D]), ("Wk", dram["L0_mix_W_qkv"][:, D:2 * D]),
               ("Wv", dram["L0_mix_W_qkv"][:, 2 * D:3 * D]), ("W2", dram["L0_gnn_W2"]), ("Wo", dram["L0_mix_W_out"])]
    W_INDEX = {n: i for i, (n, _) in enumerate(W_ORDER)}
    W_LAST = {"W1": ("h", 1, T - 1), "Wq": ("q", KT - 1), "Wk": ("k", T - 1), "Wv": ("v", T - 1), "W2": ("h", 2, T - 1)}

    NORM = float(C1) ** -0.25
    far_t = place("far_diag", [P, 640], FP32, "E2")

    def mo_bank(h):
        return 4 + 2 * (h % 2)

    sq_jobs = [st for st in steps1 if st[0] == "sq"]
    block = nc.Block()
    block.__enter__()

    def bcast_rows(ap):
        return ap.rearrange("(a n) -> a n", a=1).broadcast_to([P, ap.shape[0]])

    @block.sync
    def _(sp):
        for t in range(T):
            sp.dma_start(x[:, t, :], dram["x"][t * P:(t + 1) * P, :]).then_inc(S(f"x_in{t}"), 16)
        for i, (name, src) in enumerate(W_ORDER):
            if i >= 2:
                sp.wait_ge(S("pe_job"), ring0.index[W_LAST[W_ORDER[i - 2][0]]] + 1)
            sp.dma_start(wslot[i % 2][:, :, :], feat(src)).then_inc(S(f"w_in{i % 2}"), 16)
            if name == "W1":
                sp.dma_start(arow[:, 0, :], bcast_rows(dram["L0_gnn_a_src1"])).then_inc(S("arow_in"), 16)
                sp.dma_start(arow[:, 1, :], bcast_rows(dram["L0_gnn_a_dst1"])).then_inc(S("arow_in"), 16)
                sp.dma_start(b1[:, :], bcast_rows(dram["L0_gnn_b1"])).then_inc(S("b1_in"), 16)
                sp.dma_start(b2[:, :], bcast_rows(dram["L0_gnn_b2"])).then_inc(S("bias_in"), 16)
                sp.dma_start(bo[:, :], bcast_rows(dram["L0_mix_b_out"])).then_inc(S("bias_in"), 16)
            if name == "W2":
                sp.wait_ge(S("logit_cols"), 1)
                sp.dma_start(arow[:, 0, :], bcast_rows(dram["L0_gnn_a_src2"])).then_inc(S("arow_in"), 16)
                sp.dma_start(arow[:, 1, :], bcast_rows(dram["L0_gnn_a_dst2"])).then_inc(S("arow_in"), 16)

        def load_w1(c, b):
            sp.dma_start(w1raw[b][:, :, :], feat(dram["L0_ffn_w1"][:, bass.ds(c * CH, CH)])).then_inc(S(f"w1_in{b}"), 16)

        def load_w2(c, b):
            sp.dma_start(w2raw[b][:, :, :], dram["L0_ffn_w2"][bass.ds(c * CH, CH), :].rearrange("(j p) d -> p j d", p=128)
                         ).then_inc(S(f"w2_in{b}"), 16)

        sp.wait_ge(S("pe_job"), ring0.index[("h", 2, T - 1)] + 1)
        load_w1(0, 0)
        sp.wait_ge(S("pe_job"), ring0.index[("num", KT - 1)] + 1)
        sp.dma_start(rw[:, :, :], feat(dram["L0_ffn_router_wT"])).then_inc(S("router_in"), 16)
        sp.wait_ge(S("num_done"), KT)
        load_w2(1, 1)
        sp.wait_ge(S("pe_job"), ring0.index[("out", T - 1)] + 1)
        load_w1(1, 1)
        sp.wait_ge(S("pe_job"), len(ring0.jobs))
        load_w2(0, 0)
        sp.dma_start(wpair[:, 0:64], dram["L1_gnn_W"]).then_inc(S("gat1_in"), 16)
        sp.dma_start(wpair[:, 64:128], dram["L1_gnn_W"]).then_inc(S("gat1_in"), 16)
        sp.dma_start(attn[:, :], dram["L1_gnn_attnT"]).then_inc(S("gat1_in"), 16)
        sp.wait_ge(S("wblk_clear"), 1)
        for i in range(2):
            hs = slice(64 * i, 64 * i + 64)
            sp.dma_start(wblk[hs, 64 * i:64 * i + 64], dram["L1_gnn_WT"]).then_inc(S("gat1_in"), 16)
            sp.dma_start(wblk[hs, 128 + 64 * i:192 + 64 * i], dram["L1_gnn_W_resT"]).then_inc(S("gat1_in"), 16)
        with sp.Fori(1, NCH // 2) as i:
            for b in range(2):
                c = i * 2 + b
                sp.wait_ge(S("w1_lo"), c - 1)
                load_w1(c, b)
                sp.wait_ge(S("w2_lo"), c - 1)
                load_w2(c, b)
        for i, name in enumerate(("Wq", "Wk", "Wv", "Wo")):
            if i < 2:
                sp.wait_ge(S("hid_job"), 2 * (NCH - 1 + i))
            else:
                last = ("q", KT - 1) if i == 2 else ("k", KT - 1)
                sp.wait_ge(S("pe_job1"), ring1.index[last] + 1)
            sp.dma_start(wslot[i % 2][:, :, :], feat(dram["L1_mix_" + name])).then_inc(S(f"w_in{i % 2}"), 16)
            if i == 2:
                sp.wait_ge(S("proj_clear"), 1)
                for half in range(2):
                    sp.dma_start(projT[64 * half:64 * half + 64, half, :], dram["L1_mix_projT"]).then_inc(S("proj_in"), 16)
        sp.wait_ge(S("pe_job1"), ring1.index[("kmax", NJ - 1)] + 1)
        sp.dma_start(f2[:, :, :], dram["L1_ffn_w2"].rearrange("(m p) d -> p m d", p=128)).then_inc(S("ffn1_in"), 16)
        sp.dma_start(r1[:, :, :], feat(dram["L1_ffn_router_wT"])).then_inc(S("ffn1_in"), 16)
        sp.wait_ge(S("pe_cjob"), cring.index[("ctx", (UPJ * 3 - 1) // T)] + 1)
        for c in range(KT):
            sp.dma_start(f1[:, c, :, :], dram["L1_ffn_w1"][:, c * 128:(c + 1) * 128, :].rearrange("e p i -> p e i")
                         ).then_inc(S("ffn1_in"), 16)
        for t in range(T):
            sp.wait_ge(S("x_out"), t + 1)
            sp.dma_start(out["out"][t * P:(t + 1) * P, :], x[:, t, :]).then_inc(S("out"), 16)
        sp.wait_ge(S("out"), 16 * T)

    @block.gpsimd
    def _(pool):
        pool.sem_inc(S("count_added"), 1)
        pool.memset(eps_ln[:, :], LN_EPS).then_inc(S("eps"), 1)
        pool.memset(ident[:, :], 0.0).then_inc(S("pool_chain"), 1)
        pool.memset(ids[:, :, :], -1).then_inc(S("ids_clear"), 1)
        pool.wait_ge(S("ids_clear"), 1)
        pool.dma_start(ids[:, 0, 0:EC], dram["src"].rearrange("(p c) -> p c", p=P)).then_inc(S("ids_in"), 16)
        pool.dma_start(ids[:, 1, 0:EC], dram["dst"].rearrange("(p c) -> p c", p=P)).then_inc(S("ids_in"), 16)
        pool.wait_ge(S("pool_chain"), 1)
        pool.affine_select(out=ident[:, :], in_=ident[:, :], compare_op=ALU.not_equal, fill=1.0, base=0,
                           pattern=[[-1, 128]], channel_multiplier=1).then_inc(S("ident"), 1)
        pool.iota(iota16[:, :], [[1, NP]], base=0, channel_multiplier=0,
                  allow_small_or_imprecise_dtypes=True).then_inc(S("const"), 1)
        pool.memset(xnT[:, :, N:NP], 0.0).then_inc(S("const"), 1)
        pool.memset(cnt[:, :, :], 0.0).then_inc(S("const"), 1)
        pool.memset(far[:, :, :], FAR).then_inc(S("const"), 1)
        pool.memset(haug[:, :, :, C0:AUG0], 1.0).then_inc(S("const"), 1)
        pool.memset(rows[:, :].bitcast(FP32), 0.0).then_inc(S("const"), 1)
        pool.memset(logit[:, :, :], 0.0).then_inc(S("const"), 1)
        pool.wait_ge(S("bias_in"), 32)
        pool.wait_ge(S("xn_tok"), T)
        for t in range(T):
            pool.tensor_tensor(x[:, t, :], x[:, t, :], b2[:, :], ALU.add).then_inc(S("x_bias"), 1)
        pool.wait_ge(S("x_bias"), T)
        for t in range(T):
            pool.tensor_tensor(x[:, t, :], x[:, t, :], bo[:, :], ALU.add).then_inc(S("x_bias"), 1)
        pool.wait_ge(S("const"), 7)
        with pool.Fori(0, G_EDGE) as g:
            pool.wait_ge(S("count_float"), g + 1)
            pool.tensor_tensor(cnt[:, :, HALF:NP], cnt[:, :, HALF:NP], chif[:, :, :], ALU.add)
            pool.wait_ge(S("count_split"), g + 1)
            pool.tensor_tensor(cnt[:, :, 0:HALF], cnt[:, :, 0:HALF], craw[:, :, :], ALU.add).then_inc(S("count_added"), 1)
        pool.wait_ge(S("count_added"), G_EDGE + 1)
        for t in range(T):
            pool.tensor_tensor(cnt[:, t, t * P:(t + 1) * P], cnt[:, t, t * P:(t + 1) * P], ident[0:P, 0:P],
                               ALU.add).then_inc(S("count_ready"), 1)
        pool.wait_ge(S("phi_done"), len(phis))
        pool.memset(kvb[:, :, :], 0.0).then_inc(S("blocks_clear"), 1)
        pool.memset(ksb[:, :, :], 0.0).then_inc(S("blocks_clear"), 1)

        pool.wait_ge(S("pe_job"), ring0.index[("out", T - 1)] + 1)
        pool.memset(xh[:, :, N:NP].bitcast(FP32), 0.0).then_inc(S("pads"), 1)
        pool.memset(xl[:, :, N:NP].bitcast(FP32), 0.0).then_inc(S("pads"), 1)

        pool.wait_ge(S("x_done"), 1)
        pool.memset(wblk[:, :], 0.0).then_inc(S("wblk_clear"), 1)
        pool.memset(halves[:, :], 0.0).then_inc(S("halves0"), 1)
        pool.memset(wab[:, :, :], 0.0).then_inc(S("const1"), 1)
        pool.memset(acol[:, :, :], 0.0).then_inc(S("const1"), 1)
        pool.memset(shiftb[:, :, :], 0.0).then_inc(S("const1"), 1)
        pool.wait_ge(S("halves0"), 1)
        for i in range(2):
            pool.wait_ge(S("const1"), 3 + i)
            pool.memset(halves[64 * i:64 * i + 64, i:i + 1], 1.0).then_inc(S("const1"), 1)
        pool.wait_ge(S("const1"), 5)
        for t in range(T):
            pool.tensor_tensor(cnt[:, t, t * P:(t + 1) * P], cnt[:, t, t * P:(t + 1) * P], ident[0:P, 0:P],
                               ALU.subtract).then_inc(S("count1"), 1)

        def low1(c, b):
            pool.wait_ge(S("w1_hi"), c + 1)
            pool.tensor_tensor(w1lo[b][:, :, :], w1raw[b][:, :, :], w1hi[b][:, :, :].bitcast(FP32),
                               ALU.subtract).then_inc(S("w1_lo"), 1)

        with pool.Fori(0, NCH // 2) as i:
            for b in range(2):
                low1(i * 2 + b, b)

        pool.wait_ge(S("hid_job"), 2 * NCH)
        pool.memset(xnT[:, :, N:NP], 0.0).then_inc(S("pads1"), 1)
        pool.wait_ge(S("out_job"), T + T * NCH)
        pool.memset(v1[:, :, :, C1:AUG1], 1.0).then_inc(S("v_ones"), 1)
        pool.wait_ge(S("pe_job1"), ring1.index[("lnT", T - 1)] + 1)
        pool.memset(ft[:, :, :, C1:AUG1], 1.0).then_inc(S("ft_ones"), 1)
        pool.wait_ge(S("shift1"), 1)
        pool.memset(projT[:, :, :], 0.0).then_inc(S("proj_clear"), 1)
        pool.wait_ge(S("pe_job1"), ring1.index[sq_jobs[-1]] + 1)
        pool.iota(io8[:, :], [[1, E1]], base=0, channel_multiplier=0, allow_small_or_imprecise_dtypes=True).then_inc(S("const2"), 1)
        pool.memset(mkT[:, :], 0.0).then_inc(S("const2"), 1)
        pool.memset(sel1[:, :], 1.0).then_inc(S("const2"), 1)
        pool.wait_ge(S("const2"), 3)
        pool.affine_select(out=sel1[:, :], in_=sel1[:, :], compare_op=ALU.is_ge, fill=0.0, base=0,
                           pattern=[[1, E1 * I1]], channel_multiplier=-I1).then_inc(S("const2"), 1)
        pool.wait_ge(S("const2"), 4)
        pool.affine_select(out=sel1[:, :], in_=sel1[:, :], compare_op=ALU.is_ge, fill=0.0, base=I1 - 1,
                           pattern=[[-1, E1 * I1]], channel_multiplier=I1).then_inc(S("const2"), 1)
        for h in range(H1):
            pool.wait_ge(S("g1_act"), ring1.emptied(ring1.index[("dash", h, 1)])[1])
            pool.tensor_scalar(qp[h % 3][:, 1, :], qp[h % 3][:, 1, :], K_EPS, None, ALU.add).then_inc(S("qp_ready1"), 1)
        pool.wait_ge(S("pe_job1"), ring1.index[("dash", H1 - 1, 1)] + 1)
        pool.memset(xh[:, :, N:NP].bitcast(FP32), 0.0).then_inc(S("pads4"), 1)
        pool.memset(xl[:, :, N:NP].bitcast(FP32), 0.0).then_inc(S("pads4"), 1)
        pool.wait_ge(S("f1_hi"), 2)
        pool.tensor_tensor(f1l[:, :, :, :], f1[:, :, :, :], f1h[:, :, :, :].bitcast(FP32), ALU.subtract).then_inc(S("f1_lo"), 1)
        pool.tensor_tensor(r1l[:, :, :], r1[:, :, :], r1h[:, :, :].bitcast(FP32), ALU.subtract).then_inc(S("f1_lo"), 1)

    @block.scalar
    def _(act):
        def general(name):
            act.wait_ge(S("pe_job"), ring0.index[name] + 1)
            a, b = ring0.pair(name)
            return ps[:, a:b + 1, :]

        def lin(l, h):
            j = prob_steps.index(("prob", l, h))
            if j >= 2:
                act.wait_ge(S("pe_job"), ring0.index[("agg",) + prob_steps[j - 2][1:] + (len(AGG_GROUPS) - 1,)] + 1)
            if (l, h) == (1, 0):
                act.wait_ge(S("x_bias"), 2 * T)
            act.wait_ge(S("shift_cols"), l)
            name = ("prob", l, h, 0)
            act.wait_ge(S("pe_bjob"), bring0.index[name] + 1)
            a, b = bring0.pair(name)
            for t in range(T):
                dst = probs[j % 2][:, t, :]
                act.activation(dst.rearrange("p (a b) -> p a b", a=2), ps[0:P, a:b + 1, 0:HALF], ACT.Exp,
                               bias=logit[:, t, h:h + 1]).then_inc(S("b_act" if t == T - 1 else "prob_lin"), 1)

        def slope(l, h):
            j = prob_steps.index(("prob", l, h))
            name = ("prob", l, h, 1)
            act.wait_ge(S("pe_bjob"), bring0.index[name] + 1)
            a, b = bring0.pair(name)
            for t in range(T):
                n = j * T + t
                if n >= 2:
                    act.wait_ge(S("prob_max"), n - 1)
                dst = e2[n % 2][:, :]
                act.activation(dst.rearrange("p (a b) -> p a b", a=2), ps[0:P, a:b + 1, 0:HALF], ACT.Exp,
                               bias=as02[:, t, h:h + 1]).then_inc(S("prob_slope"), 1)

        def ln_tiles(l, dst, evacuate):
            for i in range(T + 2):
                if i < T:
                    act.wait_ge(S("ln_var"), T * l + i + 1)
                    act.activation(std[:, i:i + 1], mv[:, i, 1:2], ACT.Sqrt, bias=eps_ln[0:P, :]).then_inc(S("ln_std"), 1)
                if 1 <= i <= T:
                    t = i - 1
                    act.wait_ge(S("ln_shift"), T * l + t + 1)
                    act.activation(dst[:, t, :], x[:, t, :], ACT.Identity, bias=nmr[:, t:t + 1],
                                   scale=rstd[:, t:t + 1]).then_inc(S("xn_tok"), 1)
                if i >= 2:
                    evacuate(i - 2)

        act.sem_inc(S("count_copied"), T)
        for st in steps0:
            k, a = st[0], st[1:]
            if k == "ln":
                act.wait_ge(S("eps"), 1)

                def evacuate(t):
                    if t % 2 == 0:
                        return
                    act.wait_ge(S("const"), 7)
                    src = general(("lnT", t))[:, :, 0:3 * P].rearrange("p a (b c) -> p a b c", b=3)
                    act.activation(xnT[:, :, t * P:(t + 1) * P].rearrange("p (a b) c -> p a b c", a=2), src,
                                   ACT.Copy).then_inc(S("g_act"), 1)

                ln_tiles(0, xn, evacuate)
            elif k == "h":
                l, t = a
                if l == 2:
                    act.wait_ge(S("pe_job"), ring0.index[("agg", 1, H0 - 1, len(AGG_GROUPS) - 1)] + 1)
                else:
                    act.wait_ge(S("const"), 7)
                src = general(st)[0:P, :, 0:DH].rearrange("p a (b c) -> p a b c", b=2)
                act.activation(haug[:, t, :, 0:C0].rearrange("p (a b) c -> p a b c", a=2), src, ACT.Copy).then_inc(S("g_act"), 1)
            elif k == "edges":
                with act.Fori(0, G_EDGE) as g:
                    act.wait_ge(S("count_added"), g + 1)
                    for t in range(T):
                        if t < T - 1:
                            act.wait_ge(S("edge_tile"), g * (T - 1) + t + 1)
                        else:
                            act.wait_ge(S("edge_used"), NSLOT + (g + 1) * SPG)
                        act.activation(craw[:, t, :], ps[0:P, t, 0:HALF], ACT.Copy).then_inc(S("count_copied"), 1)
                    act.wait_ge(S("count_high"), g + 1)
                    act.activation(chif[:, :, :], chi[:, :, :], ACT.Copy).then_inc(S("count_float"), 1)
            elif k == "lin":
                lin(*a)
            elif k == "prob":
                slope(*a)
            elif k in ("q", "k"):
                i = phis.index(st)
                if i >= 2:
                    act.wait_ge(S("phi_done"), i - 1)
                if st == ("k", 0):
                    act.wait_ge(S("count_ready"), T)
                if k == "q":
                    src = general(st)[:, :, 0:HALF]
                    dst = qT[:, a[0], :].rearrange("p (a b) -> p a b", a=2)
                    ex = phie[i % 2][:, 0:NP].rearrange("p (a b) -> p a b", a=2)
                else:
                    src = general(st)[0:P, :, 0:DH]
                    dst = kk[:, a[0], :].rearrange("p (a b) -> p a b", a=2)
                    ex = phie[i % 2][0:P, :].rearrange("p (a b) -> p a b", a=2)
                act.activation(ex, src, ACT.Exp).then_inc(S("phi_exp"), 1)
                act.activation(dst, src, ACT.Relu).then_inc(S("g_act"), 1)
            elif k == "v":
                src = general(st)[0:P, :, 0:DH]
                act.activation(vv[:, a[0], :].rearrange("p (a b) -> p a b", a=2), src, ACT.Copy).then_inc(S("g_act"), 1)
            elif k == "relu":
                for t in range(T):
                    src = general(("x1T", t))[:, :, 0:3 * P].rearrange("p a (b c) -> p a b c", b=3)
                    act.activation(x1T[:, :, t * P:(t + 1) * P].rearrange("p (a b) c -> p a b c", a=2), src,
                                   ACT.Relu).then_inc(S("g_act"), 1)
            elif k == "mix":
                p = a[0]
                if p >= 2:
                    act.wait_ge(S("num_done"), p - 1)
                src = general(("den", p))[:, :, 0:HALF]
                act.activation(den[p % 2][:, :].rearrange("p (a b) -> p a b", a=2), src, ACT.Copy,
                               bias=MIX_EPS).then_inc(S("g_act"), 1)

        def high_x(n):
            t = n % T
            a = 4 + 2 * (t % 2)
            act.wait_ge(S("lnT1"), n + 1)
            src = ps[:, a:a + 2, 0:3 * P].rearrange("p a (b c) -> p a b c", b=3)
            act.activation(xh[:, :, t * P:(t + 1) * P].rearrange("p (a b) c -> p a b c", a=2), src,
                           ACT.Copy).then_inc(S("xh1"), 1)

        def high1(c, b):
            act.wait_ge(S(f"w1_in{b}"), 16 * (c // 2 + 1) if isinstance(c, int) else (c - b) * 8 + 16)
            act.activation(w1hi[b][:, :, :], w1raw[b][:, :, :], ACT.Copy).then_inc(S("w1_hi"), 1)

        def high2(c, b):
            act.wait_ge(S(f"w2_in{b}"), 16 * (c // 2 + 1) if isinstance(c, int) else (c - b) * 8 + 16)
            act.activation(w2hi[b][:, :, :], w2raw[b][:, :, :], ACT.Copy).then_inc(S("w2_hi"), 1)

        def gelu(c, b):
            for j in range(2):
                act.wait_ge(S("hid_job"), 2 * c + j + 1)
                act.activation(hid[b][:, j, :].rearrange("p (a b) -> p a b", a=2), ps[:, 2 * j:2 * j + 2, 0:HALF],
                               ACT.Gelu_apprx_tanh).then_inc(S("gelu"), 1)

        def after_o(c):
            act.wait_ge(S("out_job"), T * c + T)

        act.wait_ge(S("router_in"), 16)
        act.activation(rwh[:, :, :], rw[:, :, :], ACT.Copy).then_inc(S("router_hi"), 1)
        high1(0, 0)
        ln_tiles(1, xn2, high_x)
        high1(1, 1)
        high2(0, 0)
        act.wait_ge(S("router_max"), 1)
        act.activation(pr[:, :, :], pr[:, :, :], ACT.Exp).then_inc(S("router_exp"), 1)
        with act.Fori(0, NCH // 2 - 1) as i:
            for b in range(2):
                c = i * 2 + b
                gelu(c, b)
                high1(c + 2, b)
                after_o(c)
                high2(c + 1, 1 - b)
        gelu(NCH - 2, 0)
        after_o(NCH - 2)
        high2(NCH - 1, 1)
        gelu(NCH - 1, 1)
        def general1(name):
            act.wait_ge(S("pe_job1"), ring1.index[name] + 1)
            a, b = ring1.pair(name)
            return ps[:, a:b + 1, :]

        def flat(name):
            act.wait_ge(S("pe_job1"), ring1.index[name] + 1)
            a, b = ring1.pair(name)
            return ps[:, :, :].rearrange("p b n -> p (b n)")[:, a * 512:(b + 1) * 512]

        def two(ap):
            return ap.rearrange("p (a b) -> p a b", a=2)

        nsq = 0
        for st in steps1:
            k, a = st[0], st[1:]
            if k == "ln":
                def evacuate(t):
                    if t % 2 == 0:
                        return
                    act.wait_ge(S("pads1"), 1)
                    src = general1(("lnT", t))[:, :, 0:3 * P].rearrange("p a (b c) -> p a b c", b=3)
                    act.activation(xnT[:, :, t * P:(t + 1) * P].rearrange("p (a b) c -> p a b c", a=2), src,
                                   ACT.Copy).then_inc(S("g1_act"), 1)

                ln_tiles(2, xn3, evacuate)
            elif k == "ft" and a[1] == 0:
                t, g = a
                nk = 4
                act.wait_ge(S("pe_job1"), ring1.index[("lnT", T - 1)] + 1)
                src = flat(st)[0:P, 0:nk * 256].rearrange("p (q z) -> p q z", q=nk)
                act.activation(res[:, t, g * 512:g * 512 + nk * 128].rearrange("p (q z) -> p q z", q=nk),
                               src[:, :, 128:256], ACT.Copy).then_inc(S("res_done"), 1)
                act.activation(ft[:, t, g * 8:g * 8 + 2 * nk, 0:C1].rearrange("p (q i) c -> p q i c", q=nk),
                               src[:, :, 0:128].rearrange("p q (i c) -> p q i c", i=2), ACT.Copy).then_inc(S("g1_act"), 1)
            elif k in ("q", "k"):
                m = a[0]
                src = general1(st)[:, :, 0:HALF]
                dst = (q1T if k == "q" else k1T)[:, m, :]
                if nsq >= 2:
                    act.wait_ge(S("pe_job1"), ring1.index[sq_jobs[nsq - 2]] + 1)
                act.activation(two(dst), src, ACT.Copy).then_inc(S("qk1"), 1)
                act.activation(two(sq[nsq % 2][:, :]), src, ACT.Square).then_inc(S("g1_act"), 1)
                nsq += 1
            elif k == "v":
                t = a[0]
                act.wait_ge(S("v_ones"), 1)
                src = general1(st)[0:P, :, 0:DH].rearrange("p a (b c) -> p a b c", b=6)
                act.activation(v1[:, t, :, 0:C1].rearrange("p (a b) c -> p a b c", a=2), src, ACT.Copy).then_inc(S("g1_act"), 1)
            elif k == "lin":
                h = a[0]
                if h >= 2:
                    act.wait_ge(S("pe_job1"), ring1.index[("agg", h - 2)] + 1)
                act.wait_ge(S("shift1"), 1)
                name = ("prob", h, 0)
                act.wait_ge(S("pe_bjob1"), bring1.index[name] + 1)
                lo, hi = bring1.pair(name)
                for t in range(T):
                    act.activation(two(probs[h % 2][:, t, :]), ps[0:P, lo:hi + 1, 0:HALF], ACT.Exp,
                                   bias=acol[:, t, h:h + 1]).then_inc(S("b1_act" if t == T - 1 else "prob_lin1"), 1)
            elif k == "prob":
                h = a[0]
                name = ("prob", h, 1)
                act.wait_ge(S("pe_bjob1"), bring1.index[name] + 1)
                lo, hi = bring1.pair(name)
                for t in range(T):
                    n = h * T + t
                    if n >= 2:
                        act.wait_ge(S("prob_max1"), n - 1)
                    act.activation(two(e2[n % 2][:, :]), ps[0:P, lo:hi + 1, 0:HALF], ACT.Exp,
                                   bias=as02b[:, t, h:h + 1]).then_inc(S("prob_slope1"), 1)
            elif k == "kmax":
                j = a[0]
                if j == 3:
                    act.wait_ge(S("g1_dve"), ring1.emptied(ring1.index[("tok", H1 - 1)])[1])
                if j == 0:
                    act.wait_ge(S("pe_job1"), ring1.index[("agg", H1 - 1)] + 1)
                act.activation(kp[j][:, :, :].rearrange("p u m -> p (u m)"), flat(st)[0:P, :], ACT.Copy).then_inc(S("g1_act"), 1)
            elif k == "kexp":
                j = a[0]
                act.wait_ge(S("nstab"), 1)
                for i, (h, t) in enumerate(units(j)):
                    ins = act.activation(kp[j][:, i, :], kp[j][:, i, :], ACT.Exp, bias=nstab[:, h, t:t + 1], scale=NORM)
                ins.then_inc(S("k_exp"), 1)
            elif k == "agg":
                h = a[0]
                if h:
                    act.wait_ge(S("pe_job1"), ring1.index[("tok", h - 1)] + 1)
                act.activation(two(aggT[:, :]), general1(st)[0:AUG1, :, 0:HALF], ACT.Copy).then_inc(S("g1_act"), 1)
            elif k == "dash":
                h, m = a
                if h == 0:
                    act.wait_ge(S("pe_cjob"), cring.index[("ctx", (UPJ * 6 - 1) // T)] + 1)
                if h >= 3:
                    act.wait_ge(S("pe_ojob"), h - 2)
                act.activation(two(qp[h % 3][:, m, :]), general1(st)[:, :, 0:HALF], ACT.Exp, scale=NORM).then_inc(S("g1_act"), 1)
            elif k == "mo":
                h = a[0]
                c, i = divmod(h, 2)
                if c >= 2:
                    act.wait_ge(S("mo_ready"), c - 1)
                act.wait_ge(S("pe_ojob"), h + 1)
                src = ps[64 * (1 - i):64 * (2 - i), mo_bank(h):mo_bank(h) + 2, 0:HALF]
                act.activation(two(moden[c % 2][64 * i:64 * i + 64, :]), src, ACT.Copy).then_inc(S("den_copied"), 1)
        act.wait_ge(S("ffn1_in"), 16 * (KT + 2))
        act.wait_ge(S("pe_cjob"), len(cring.jobs))
        act.activation(f1h[:, :, :, :], f1[:, :, :, :], ACT.Copy).then_inc(S("f1_hi"), 1)
        act.activation(r1h[:, :, :], r1[:, :, :], ACT.Copy).then_inc(S("f1_hi"), 1)
        ln_tiles(3, xn4, lambda t: high_x(T + t))
        act.wait_ge(S("router1_max"), 1)
        act.activation(p1[:, :, :], p1[:, :, :], ACT.Exp).then_inc(S("router1_exp"), 1)
        for m in range(4):
            act.wait_ge(S("hid1_job"), m + 1)
            lo = 2 * (m % 2)
            act.activation(two(hid1[:, m, :]), ps[:, lo:lo + 2, 0:HALF], ACT.Silu).then_inc(S("silu"), 1)

    @block.vector
    def _(dve):
        chain = [0]

        def link(ins):
            chain[0] += 1
            ins.then_inc(S("dve_chain"), 1)
            dve.wait_ge(S("dve_chain"), chain[0])

        def general(name):
            dve.wait_ge(S("pe_job"), ring0.index[name] + 1)
            a, b = ring0.pair(name)
            return ps[:, a:b + 1, :]

        def split_rows(src):
            high, low = slice(0, RPAD), slice(RPAD, 2 * RPAD)
            for cols, piece in src:
                last = dve.tensor_copy(rows[high, cols], piece)
            link(last)
            for cols, piece in src:
                last = dve.tensor_tensor(rows[low, cols], piece, rows[high, cols].bitcast(FP32), ALU.subtract)
            return last

        def by_tiles(src):
            return [(slice(0, 4 * P), src[0:RPAD, 0, 0:4 * P]), (slice(4 * P, N), src[0:RPAD, 1, 0:P])]

        def row_picker(layer):
            return dve.tensor_tensor(pick[layer][:, :], ident[0:2 * RPAD, 0:RPAD], ident[0:2 * RPAD, RPAD:2 * RPAD], ALU.add)

        scrap = [0, 0]

        def scrapped(slots):
            n = scrap[0]
            if scrap[1] != slots:
                if n:
                    dve.wait_ge(S("scrap"), n)
                scrap[1], scrap[0] = slots, n
                scrap.append(n)
            elif n - scrap[-1] >= slots:
                dve.wait_ge(S("scrap"), n - slots + 1)
            scrap[0] += 1
            return (n - scrap[-1]) % slots

        def ln_tiles(l, ready, evacuate):
            for i in range(T + 3):
                if i < T:
                    ready(i)
                    for half in range(2):
                        last = dve.bn_stats(stats[:, i, half, :], x[:, i, half * DH:(half + 1) * DH])
                    link(last)
                    dve.bn_aggr(mv[:, i, :], stats[:, i, :, :]).then_inc(S("ln_var"), 1)
                if 1 <= i <= T:
                    t = i - 1
                    dve.wait_ge(S("ln_std"), T * l + t + 1)
                    link(dve.reciprocal(rstd[:, t:t + 1], std[:, t:t + 1]))
                    dve.scalar_tensor_tensor(nmr[:, t:t + 1], mv[:, t, 0:1], -1.0, rstd[:, t:t + 1], ALU.mult,
                                             ALU.mult).then_inc(S("ln_shift"), 1)
                if i >= 3:
                    evacuate(i - 3)

        def average(l, h, t):
            j = [t in group for group in AGG_GROUPS].index(True)
            i = AGG_GROUPS[j].index(t)
            src = general(("agg", l, h, j))[0:P]
            r = recip[:, t:t + 1]
            value = src[:, i // 2, (i % 2) * AUG0:(i % 2 + 1) * AUG0]
            link(dve.reciprocal(r, value[:, C0:AUG0]))
            cols = slice(h * C0, (h + 1) * C0)
            dst = x1[:, t, cols] if l == 1 else x[:, t, cols]
            add = b1[:, cols] if l == 1 else x[:, t, cols]
            ins = dve.scalar_tensor_tensor(dst, value[:, 0:C0], r, add, ALU.mult, ALU.add)
            if t == AGG_GROUPS[j][-1]:
                ins.then_inc(S("g_dve"), 1)
            return ins

        for st in steps0:
            k, a = st[0], st[1:]
            if k == "ln":
                def evacuate(t):
                    if t % 2:
                        return
                    dve.wait_ge(S("const"), 7)
                    src = general(("lnT", t))[:, :, 0:3 * P].rearrange("p a (b c) -> p a b c", b=3)
                    dve.tensor_copy(xnT[:, :, t * P:(t + 1) * P].rearrange("p (a b) c -> p a b c", a=2),
                                    src).then_inc(S("g_dve"), 1)

                ln_tiles(0, lambda t: dve.wait_ge(S(f"x_in{t}"), 16), evacuate)
                link(row_picker(0))
                dve.wait_ge(S("ids_in"), 32)
                dve.tensor_copy(sid[:, :], ids[:, 0, :])
                link(dve.tensor_copy(did[:, :], ids[:, 1, :]))
                link(dve.tensor_scalar(dwt[:, :], did[:, :], float(HALF), None, ALU.is_ge))
                link(dve.scalar_tensor_tensor(dlo[:, :], dwt[:, :], -float(HALF), did[:, :], ALU.mult, ALU.add))
                link(dve.tensor_scalar(dwt[:, :], dwt[:, :], PACK - 1.0, 1.0, ALU.mult, ALU.add))
            elif k == "edges":
                def onehot(n, b):
                    dve.wait_ge(S("edge_used"), n + 1)
                    for r in range(SLOT):
                        c = n * SLOT + r
                        dve.tensor_scalar(shot[b][:, r, 0:N], iota16[:, 0:N], sid[:, bass.ds(c, 1)], None, ALU.is_equal)
                        last = dve.tensor_scalar(dhot[b][:, r, :], iota16[:, 0:HALF], dlo[:, bass.ds(c, 1)],
                                                 dwt[:, bass.ds(c, 1)], ALU.is_equal, ALU.mult)
                    last.then_inc(S("edge_hot"), 1)

                def onehots(g, lo, hi):
                    for i in range(lo, hi):
                        onehot(g * SPG + i, i % NSLOT)

                def split_high(g):
                    dve.wait_ge(S("count_copied"), g * T + 2 * T)
                    dve.tensor_scalar(chi[:, :, :], craw[:, :, :], 1.0 / PACK, -0.5 + 0.5 / PACK, ALU.mult,
                                      ALU.add).then_inc(S("count_high"), 1)

                def split_low(g):
                    dve.wait_ge(S("count_high"), g + 1)
                    dve.scalar_tensor_tensor(craw[:, :, :], chi[:, :, :], -PACK, craw[:, :, :], ALU.mult,
                                             ALU.add).then_inc(S("count_split"), 1)

                onehots(0, 0, SPG)
                with dve.Fori(1, G_EDGE) as g:
                    onehots(g, 0, 2)
                    split_high(g - 1)
                    onehots(g, 2, 3)
                    split_low(g - 1)
                    onehots(g, 3, SPG)
                split_high(G_EDGE - 1)
                split_low(G_EDGE - 1)
            elif k == "mask":
                t = a[0]
                src = general(st)[0:P]
                dve.tensor_scalar(far[:, t, 0:3 * P], src[:, 0, 0:3 * P], 0.5, FAR, ALU.is_lt, ALU.mult)
                dve.tensor_scalar(far[:, t, 3 * P:N], src[:, 1, 0:2 * P], 0.5, FAR, ALU.is_lt, ALU.mult).then_inc(S("g_dve"), 1)
            elif k == "lg":
                l, t = a
                dve.wait_ge(S("arow_in"), 32 * l)
                eng, n = ring0.emptied(ring0.index[("h", l, t)])
                dve.wait_ge(S("g_act"), n)
                for s in range(2):
                    for h in range(H0):
                        z = scrapped(6) * C0
                        dve.tensor_tensor_reduce(
                            out=junk[:, z:z + C0], in0=haug[:, t, h, 0:C0], in1=arow[:, s, h * C0:(h + 1) * C0],
                            scale=1.0, scalar=0.0, op0=ALU.mult, op1=ALU.add,
                            accum_out=logit[:, t, s * H0 + h:s * H0 + h + 1]).then_inc(S("scrap"), 1)
            elif k == "logit":
                l = a[0]
                dve.wait_ge(S("scrap"), scrap[0])
                dve.sem_inc(S("logit_cols"), 1)
                link(dve.tensor_scalar(as02[:, :, :], logit[:, :, 0:H0], SLOPE, None, ALU.mult))
                split_rows(by_tiles(general(("logitT", l)))).then_inc(S("g_dve"), 1)
            elif k == "asmax":
                l, h = a
                dve.wait_ge(S("pe_bjob"), bring0.index[st] + 1)
                pa, pb = bring0.pair(st)
                src = ps[0:P, pa:pb + 1, 0:HALF]
                for t in range(T):
                    z = scrapped(2) * NP
                    last = dve.tensor_tensor_reduce(
                        out=junk[:, z:z + NP].rearrange("p (a b) -> p a b", a=2), in0=far[:, t, :].rearrange("p (a b) -> p a b", a=2),
                        in1=src, scale=1.0, scalar=-3.0e38, op0=ALU.add, op1=ALU.max, accum_out=asmax[:, t, h:h + 1]).then_inc(S("scrap"), 1)
                dve.wait_ge(S("scrap"), scrap[0])
                dve.sem_inc(S("b_dve"), 1)
            elif k == "shift":
                l = a[0]
                dve.wait_ge(S("b_dve"), H0 * l)
                ad = logit[:, :, H0:2 * H0]
                link(dve.tensor_tensor(mcol[:, :, :], asmax[:, :, :], ad, ALU.add))
                link(dve.scalar_tensor_tensor(mcol[:, :, :], mcol[:, :, :], SLOPE, mcol[:, :, :], ALU.mult, ALU.max))
                dve.tensor_tensor(logit[:, :, 2 * H0:3 * H0], ad, mcol[:, :, :], ALU.subtract)
                dve.scalar_tensor_tensor(logit[:, :, 3 * H0:4 * H0], ad, SLOPE, mcol[:, :, :], ALU.mult,
                                         ALU.subtract).then_inc(S("shift_cols"), 1)
                split_rows(by_tiles(general(("shiftT", l)))).then_inc(S("g_dve"), 1)
            elif k == "prob":
                j = prob_steps.index(st)
                for t in range(T):
                    n = j * T + t
                    dve.wait_ge(S("prob_slope"), n + 1)
                    dst = probs[j % 2][:, t, :]
                    dve.tensor_tensor(dst, dst, e2[n % 2][:, :], ALU.max).then_inc(S("prob_max"), 1)
                    dve.wait_ge(S("prob_max"), n + 1)
                    dve.scalar_tensor_tensor(dst, dst, 1.0, cnt[:, t, :], ALU.min, ALU.mult).then_inc(S("prob_ready"), 1)
            elif k in ("q", "k"):
                i = phis.index(st)
                eng, n = ring0.emptied(ring0.index[st])
                dve.wait_ge(S("g_act"), n)
                if k == "q":
                    dst, ex = qT[:, a[0], :], phie[i % 2][:, 0:NP]
                else:
                    dst, ex = kk[:, a[0], :], phie[i % 2][0:P, :]
                dve.scalar_tensor_tensor(dst, ex, 1.0, dst, ALU.min, ALU.add).then_inc(S("phi_done"), 1)
            elif k == "agg":
                l, h = a
                if (l, h) == (1, 0):
                    dve.wait_ge(S("b1_in"), 16)
                if (l, h) == (2, 0):
                    dve.wait_ge(S("x_bias"), 2 * T)
                if (l, h) != (2, H0 - 1):
                    for t in range(T):
                        average(l, h, t)
            elif k == "kv":
                p = a[0]
                dve.wait_ge(S("blocks_clear"), 2)
                src = general(st)
                for i in range(2):
                    hs = slice(i * 64, (i + 1) * 64)
                    dve.tensor_copy(kvb[hs, p, hs], src[hs, 0, i * 64:(i + 1) * 64])
                    ins = dve.tensor_scalar(ksb[hs, p, hs], src[hs, 1, i * 64:(i + 1) * 64], 1.0, None, ALU.add)
                ins.then_inc(S("g_dve"), 1)
            elif k == "mix":
                p = a[0]
                eng, n = ring0.emptied(ring0.index[("den", p)])
                dve.wait_ge(S("g_act"), n)
                link(dve.reciprocal(den[p % 2][:, :], den[p % 2][:, :]))
                src = general(("num", p))[:, :, 0:HALF]
                dve.tensor_tensor(qT[:, p, :].rearrange("p (a b) -> p a b", a=2), src,
                                  den[p % 2][:, :].rearrange("p (a b) -> p a b", a=2), ALU.mult).then_inc(S("num_done"), 1)
            elif k == "out":
                t = a[0]
                src = general(st)[0:P, :, 0:DH]
                dst = x[:, t, :].rearrange("p (a b) -> p a b", a=2)
                dve.wait_ge(S("x_bias"), 2 * T)
                dve.tensor_tensor(dst, dst, src, ALU.add).then_inc(S("g_dve"), 1)

        def last_head(t):
            ins = average(2, H0 - 1, t)
            ends = [group[-1] for group in AGG_GROUPS]
            if t in ends:
                job = ("agg", 2, H0 - 1, ends.index(t))
                dve.wait_ge(S("g_dve"), ring0.emptied(ring0.index[job])[1])
            else:
                link(ins)
            if t == T - 1:
                dve.sem_inc(S("x_done"), 1)

        def low_x(n):
            t = n % T
            a = 4 + 2 * (t % 2)
            dve.wait_ge(S("xh1"), n + 1)
            src = ps[:, a:a + 2, 0:3 * P].rearrange("p a (b c) -> p a b c", b=3)
            cols = slice(t * P, (t + 1) * P)
            dve.tensor_tensor(xl[:, :, cols].rearrange("p (a b) c -> p a b c", a=2), src,
                              xh[:, :, cols].bitcast(FP32).rearrange("p (a b) c -> p a b c", a=2), ALU.subtract
                              ).then_inc(S("xl1"), 1)

        ln_tiles(1, last_head, low_x)
        dve.wait_ge(S("router_hi"), 1)
        dve.tensor_tensor(rwl[:, :, :], rw[:, :, :], rwh[:, :, :].bitcast(FP32), ALU.subtract).then_inc(S("router_lo"), 1)

        def low2(c, b):
            dve.wait_ge(S("w2_hi"), c + 1)
            dve.tensor_tensor(w2lo[b][:, :, :], w2raw[b][:, :, :], w2hi[b][:, :, :].bitcast(FP32),
                              ALU.subtract).then_inc(S("w2_lo"), 1)

        def split(c, b):
            for j in range(2):
                dve.wait_ge(S("gelu"), 2 * c + j + 1)
                dve.tensor_copy(hidh[b][:, j, :], hid[b][:, j, :]).then_inc(S("hid_hi"), 1)
                dve.wait_ge(S("hid_hi"), 2 * c + j + 1)
                dve.tensor_tensor(hidl[b][:, j, :], hid[b][:, j, :], hidh[b][:, j, :].bitcast(FP32),
                                  ALU.subtract).then_inc(S("hid_lo"), 1)

        def gather(c, b, tiles=range(T)):
            for t in tiles:
                a = 4 + 2 * ((T * b + t) % 2)
                dve.wait_ge(S("out_job"), T * c + t + 1 + T)
                dst = x[:, t, :].rearrange("p (a b) -> p a b", a=2)
                dve.scalar_tensor_tensor(dst, ps[0:P, a:a + 2, 0:DH], comb[:, t, bass.ds(c, 1)], dst, ALU.mult,
                                         ALU.add).then_inc(S("out_added"), 1)

        low2(0, 0)
        dve.wait_ge(S("router_job"), 1)
        dve.tensor_copy(rrow[:, :].rearrange("p (a b) -> p a b", a=2), ps[0:NEXP0, 4:6, 0:HALF]).then_inc(S("router_rows"), 1)
        dve.wait_ge(S("router_job"), 2)
        lg = ps[0:P, 6, 0:T * NEXP0].rearrange("p (t e) -> p t e", t=T)
        link(dve.tensor_reduce(col[0][:, :], lg, AX.X, ALU.max))
        dve.tensor_tensor(pr[:, :, :], lg, col[0][:, :].unsqueeze(2).broadcast_to([P, T, NEXP0]),
                          ALU.subtract).then_inc(S("router_max"), 1)
        dve.wait_ge(S("router_exp"), 1)
        link(dve.tensor_reduce(col[0][:, :], pr[:, :, :], AX.X, ALU.add))
        link(dve.reciprocal(col[1][:, :], col[0][:, :]))
        link(dve.tensor_tensor(pr[:, :, :], pr[:, :, :], col[1][:, :].unsqueeze(2).broadcast_to([P, T, NEXP0]), ALU.mult))
        for t in range(T):
            last = dve.max(top[:, t, :], pr[:, t, :])
        link(last)
        for t in range(T):
            last = dve.match_replace(rest[:, t, :], top[:, t, :], pr[:, t, :], 0.0)
        dve.tensor_reduce(col[0][:, :], top[:, :, :], AX.X, ALU.add)
        link(last)
        link(dve.tensor_tensor(pr[:, :, :], pr[:, :, :], rest[:, :, :], ALU.subtract))
        link(dve.reciprocal(col[1][:, :], col[0][:, :]))
        link(dve.tensor_tensor(pr[:, :, :], pr[:, :, :], col[1][:, :].unsqueeze(2).broadcast_to([P, T, NEXP0]), ALU.mult))
        at, e0 = 0, 0
        for width in sorted(set(WIDTHS)):
            ne, nch = WIDTHS.count(width), width // CH
            for t in range(T):
                last = dve.tensor_copy(comb[:, t, at:at + ne * nch].rearrange("p (e c) -> p e c", c=nch),
                                       pr[:, t, e0:e0 + ne].unsqueeze(2).broadcast_to([P, ne, nch]))
            at, e0 = at + ne * nch, e0 + ne
        link(last)
        dve.sem_inc(S("out_added"), 2)
        split(0, 0)
        low2(1, 1)
        with dve.Fori(0, NCH // 2 - 1) as i:
            for b in (1, 0):
                c = i * 2 + (2 - b)
                split(c, b)
                gather(c - 1, 1 - b)
                low2(c + 1, 1 - b)
        split(NCH - 1, 1)
        gather(NCH - 2, 0)

        def last_chunk(t):
            gather(NCH - 1, 1, [t])
            dve.wait_ge(S("out_added"), 2 + T * (NCH - 1) + t + 1)


        def general1(name):
            dve.wait_ge(S("pe_job1"), ring1.index[name] + 1)
            a, b = ring1.pair(name)
            return ps[:, a:b + 1, :]

        def two(ap):
            return ap.rearrange("p (a b) -> p a b", a=2)

        for st in steps1:
            k, a = st[0], st[1:]
            if k == "ln":
                def evacuate(t):
                    if t % 2:
                        return
                    dve.wait_ge(S("pads1"), 1)
                    src = general1(("lnT", t))[:, :, 0:3 * P].rearrange("p a (b c) -> p a b c", b=3)
                    dve.tensor_copy(xnT[:, :, t * P:(t + 1) * P].rearrange("p (a b) c -> p a b c", a=2),
                                    src).then_inc(S("g1_dve"), 1)

                ln_tiles(2, last_chunk, evacuate)
                dve.wait_ge(S("const1"), 5)
                link(row_picker(1))
                dve.wait_ge(S("diag_job"), 1)
                dve.tensor_scalar(far_t[:, 0:4 * P], ps[0:P, 4, 0:4 * P], 0.5, FAR, ALU.is_lt, ALU.mult)
                link(dve.tensor_scalar(far_t[:, 4 * P:N], ps[0:P, 5, 0:P], 0.5, FAR, ALU.is_lt, ALU.mult))
                for t in range(T):
                    last = dve.tensor_copy(far[:, t, t * P:(t + 1) * P], far_t[:, t * P:(t + 1) * P])
                last.then_inc(S("far1"), 1)
            elif k == "ft" and a[1] == 1:
                t = a[0]
                src = general1(st)[0:P, 0, :].rearrange("p (q z) -> p q z", q=2)
                dve.tensor_copy(res[:, t, 512:768].rearrange("p (q z) -> p q z", q=2), src[:, :, 128:256]).then_inc(S("res_done"), 1)
                dve.tensor_copy(ft[:, t, 8:12, 0:C1].rearrange("p (q i) c -> p q i c", q=2),
                                src[:, :, 0:128].rearrange("p q (i c) -> p q i c", i=2)).then_inc(S("g1_dve"), 1)
            elif k == "logit":
                src = general1(("wal",))
                for i in range(2):
                    hs = slice(64 * i, 64 * i + 64)
                    for c in range(KT):
                        h = 2 * c + i
                        last = dve.tensor_copy(wab[hs, c, h:h + H1 + 1:H1], src[hs, 0, h:h + H1 + 1:H1])
                last.then_inc(S("g1_dve"), 1)
                src = general1(("logitT",))[0:RPAD, :, 0:HALF]
                dve.tensor_copy(two(lrow[:, :]), src).then_inc(S("logit_rows"), 1)
                split_rows([(slice(i * HALF, (i + 1) * HALF), src[:, i, :]) for i in range(2)]).then_inc(S("g1_dve"), 1)
                src = general1(("logit",))[0:P, 0, 0:T * RPAD].rearrange("p (t h) -> p t h", t=T)
                dve.tensor_copy(acol[:, :, :], src)
                link(dve.tensor_scalar(as02b[:, :, :], src[:, :, 0:H1], SLOPE, None, ALU.mult))
                dve.sem_inc(S("g1_dve"), 1)
            elif k == "asmax":
                h = a[0]
                dve.wait_ge(S("far1"), 1)
                dve.wait_ge(S("pe_bjob1"), bring1.index[st] + 1)
                lo, hi = bring1.pair(st)
                for t in range(T):
                    z = scrapped(2) * NP
                    dve.tensor_tensor_reduce(out=two(junk[:, z:z + NP]), in0=two(far[:, t, :]), in1=ps[0:P, lo:hi + 1, 0:HALF],
                                             scale=1.0, scalar=-3.0e38, op0=ALU.add, op1=ALU.max,
                                             accum_out=asmaxb[:, t, h:h + 1]).then_inc(S("scrap"), 1)
                dve.wait_ge(S("scrap"), scrap[0])
                dve.sem_inc(S("b1_dve"), 1)
            elif k == "shift":
                ad = acol[:, :, H1:2 * H1]
                link(dve.tensor_tensor(mcolb[:, :, :], asmaxb[:, :, :], ad, ALU.add))
                link(dve.scalar_tensor_tensor(mcolb[:, :, :], mcolb[:, :, :], SLOPE, mcolb[:, :, :], ALU.mult, ALU.max))
                link(dve.tensor_scalar(asmaxb[:, :, :], asmaxb[:, :, :], 0.5 * FAR, None, ALU.is_gt))
                link(dve.tensor_tensor(mcolb[:, :, :], mcolb[:, :, :], asmaxb[:, :, :], ALU.mult))
                dve.tensor_tensor(shiftb[:, :, 0:H1], ad, mcolb[:, :, :], ALU.subtract)
                link(dve.scalar_tensor_tensor(shiftb[:, :, H1:2 * H1], ad, SLOPE, mcolb[:, :, :], ALU.mult, ALU.subtract))
                dve.sem_inc(S("shift1"), 1)
                split_rows(by_tiles(general1(("shiftT",)))).then_inc(S("g1_dve"), 1)
            elif k == "sq":
                src = general1(st)[0:P, 0, 0:2 * T].rearrange("p (t i) -> p t i", t=T)
                m = a[1]
                dve.tensor_scalar(diag[a[0]][:, 2 * m:2 * m + 2, :].rearrange("p i t -> p t i"), src, 0.5 * NORM * NORM, None,
                                  ALU.mult).then_inc(S("g1_dve"), 1)
            elif k == "prob":
                h = a[0]
                if h == 0:
                    dve.wait_ge(S("count1"), T)
                for t in range(T):
                    n = h * T + t
                    dve.wait_ge(S("prob_slope1"), n + 1)
                    dst = probs[h % 2][:, t, :]
                    dve.tensor_tensor(dst, dst, e2[n % 2][:, :], ALU.max).then_inc(S("prob_max1"), 1)
                    dve.wait_ge(S("prob_max1"), n + 1)
                    dve.scalar_tensor_tensor(dst, dst, 1.0, cnt[:, t, :], ALU.min, ALU.mult).then_inc(S("prob_ready1"), 1)
            elif k == "tok":
                h = a[0]
                dve.wait_ge(S("res_done"), 2 * T)
                src = general1(st)[0:P, 0, 0:T * AUG1].rearrange("p (t c) -> p t c", t=T)
                cols = slice(h * C1, (h + 1) * C1)
                link(dve.tensor_scalar(aggr[:, :, :], src[:, :, C1:AUG1], 1e-16, None, ALU.max))
                link(dve.reciprocal(aggr[:, :, :], aggr[:, :, :]))
                link(dve.tensor_tensor(aggv[:, :, :], src[:, :, 0:C1], aggr[:, :, :].broadcast_to([P, T, C1]), ALU.mult))
                link(dve.tensor_tensor(aggv[:, :, :], aggv[:, :, :], res[:, :, cols], ALU.add))
                dve.scalar_tensor_tensor(x[:, :, cols], aggv[:, :, :], 0.0, x[:, :, cols], ALU.max, ALU.add
                                         ).then_inc(S("g1_dve"), 1)
            elif k == "kmax":
                j = a[0]
                dve.wait_ge(S("g1_act"), ring1.emptied(ring1.index[st])[1])
                dst = kmax[:, :, :].rearrange("p h t -> p (h t)")[:, UPJ * j:UPJ * (j + 1)]
                dve.tensor_reduce(dst, kp[j][:, :, :], AX.X, ALU.max).then_inc(S("k_max"), 1)
            elif k == "qmax":
                j = a[0]
                dve.wait_ge(S("pe_job1"), ring1.index[st] + 1)
                lo, hi = ring1.pair(st)
                src = ps[0:P, lo:hi + 1, :].rearrange("p a (u m) -> p (a u) m", u=2)
                dst = qmax[:, :, :].rearrange("p h t -> p (h t)")[:, UPJ * j:UPJ * (j + 1)]
                dve.tensor_reduce(dst, src, AX.X, ALU.max).then_inc(S("g1_dve"), 1)
            elif k == "kstab":
                dve.wait_ge(S("k_max"), NJ)
                dve.tensor_reduce(kmaxh[:, :], kmax[:, :, :], AX.X, ALU.max).then_inc(S("kmax_head"), 1)
                src = general1(st)[0:H1, 0, 0:P]
                dve.tensor_reduce(gmax[:, :], src, AX.X, ALU.max).then_inc(S("g1_dve"), 1)
            elif k == "kstabs":
                src = general1(st)[0:P, 0, 0:H1]
                link(dve.tensor_copy(kmaxb[:, :], src))
                link(dve.scalar_tensor_tensor(nstab[:, :, :], kmaxb[:, :].unsqueeze(2).broadcast_to([P, H1, T]), -NORM,
                                              diag["k"][:, :, :], ALU.mult, ALU.subtract))
                dve.sem_inc(S("nstab"), 1)
                dve.sem_inc(S("g1_dve"), 1)
            elif k == "kexp":
                j = a[0]
                dve.wait_ge(S("k_exp"), j + 1)
                dve.tensor_scalar(kp[j][:, :, :], kp[j][:, :, :], K_EPS, None, ALU.add).then_inc(S("kp_ready"), 1)
            elif k == "ctx":
                dve.wait_ge(S("pe_cjob"), cring.index[st] + 1)
                dve.tensor_copy(ctxT[a[0] % 2][:, :], ps[0:AUG1, cring.pair(st)[0], 0:M1]).then_inc(S("ctx_ready"), 1)
            elif k == "ctxt":
                h = a[0]
                dve.wait_ge(S("pe_cjob"), cring.index[st] + 1)
                src = ps[:, cring.pair(st)[0], 0:2 * AUG1].rearrange("p (m c) -> p m c", m=2)
                i = h % 2
                dve.tensor_copy(ctx[:, h, :, i * C1:(i + 1) * C1], src[:, :, 0:C1])
                dve.tensor_copy(ctx[:, h, :, (1 - i) * C1:(2 - i) * C1],
                                src[:, :, C1:AUG1].broadcast_to([128, 2, C1])).then_inc(S("ctx_ready"), 1)
            elif k == "qrow":
                link(dve.scalar_tensor_tensor(acol[:, :, 0:H1].rearrange("p t h -> p h t"), diag["q"][:, :, :], -1.0 / NORM,
                                              qmax[:, :, :], ALU.mult, ALU.subtract))
                dve.sem_inc(S("q_cols"), 1)
                split_rows(by_tiles(general1(st))).then_inc(S("g1_dve"), 1)
            elif k == "dash":
                h, m = a
                if m == 0:
                    dve.wait_ge(S("g1_act"), ring1.emptied(ring1.index[st])[1])
                    dve.tensor_scalar(qp[h % 3][:, 0, :], qp[h % 3][:, 0, :], K_EPS, None, ALU.add).then_inc(S("qp_ready0"), 1)
            elif k == "mo":
                h = a[0]
                hs = slice(64 * (h % 2), 64 * (h % 2) + 64)
                dve.wait_ge(S("pe_ojob"), h + 1)
                dve.tensor_copy(two(moT[hs, h // 2, :]), ps[hs, mo_bank(h):mo_bank(h) + 2, 0:HALF]).then_inc(S("num_copied"), 1)
            elif k == "norm":
                c = a[0]
                dve.wait_ge(S("den_copied"), 2 * c + 2)
                dve.wait_ge(S("num_copied"), 2 * c + 2)
                link(dve.reciprocal(moden[c % 2][:, :], moden[c % 2][:, :]))
                dve.tensor_tensor(moT[:, c, :], moT[:, c, :], moden[c % 2][:, :], ALU.mult).then_inc(S("mo_ready"), 1)

        def project(t):
            src = general1(("wo", t))[0:P, :, 0:DH]
            dst = two(x[:, t, :])
            dve.tensor_tensor(dst, dst, src, ALU.add).then_inc(S("g1_dve"), 1)
            dve.wait_ge(S("g1_dve"), ring1.emptied(ring1.index[("wo", t)])[1])

        ln_tiles(3, project, lambda t: low_x(T + t))
        dve.wait_ge(S("router1_job"), 1)
        dve.tensor_copy(two(rrow1[:, :]), ps[0:E1, 4:6, 0:HALF]).then_inc(S("router1_rows"), 1)
        dve.wait_ge(S("router1_job"), 2)
        lg = ps[0:P, 6, 0:T * E1].rearrange("p (t e) -> p t e", t=T)
        link(dve.tensor_reduce(c1[0][:, :], lg, AX.X, ALU.max))
        dve.tensor_tensor(p1[:, :, :], lg, c1[0][:, :].unsqueeze(2).broadcast_to([P, T, E1]), ALU.subtract).then_inc(S("router1_max"), 1)
        dve.wait_ge(S("router1_exp"), 1)
        link(dve.tensor_reduce(c1[1][:, :], p1[:, :, :], AX.X, ALU.add))
        link(dve.reciprocal(c1[2][:, :], c1[1][:, :]))
        link(dve.tensor_tensor(p1[:, :, :], p1[:, :, :], c1[2][:, :].unsqueeze(2).broadcast_to([P, T, E1]), ALU.mult))
        for t in range(T):
            last = dve.max(t1[:, t, :], p1[:, t, :])
        link(last)
        for t in range(T):
            last = dve.max_index(i1[:, t, :], t1[:, t, :], p1[:, t, :])
        link(last)
        link(dve.tensor_copy(f1i[:, :, :], i1[:, :, 0:2]))
        link(dve.tensor_tensor(f1i[:, :, 0:1], f1i[:, :, 0:1], f1i[:, :, 1:2], ALU.max))
        dve.wait_ge(S("const2"), 5)
        for t in range(T):
            last = dve.tensor_scalar(mk[:, t, :], io8[:, :], f1i[:, t, 0:1], None, ALU.is_equal)
        last.then_inc(S("mask1"), 1)
        dve.wait_ge(S("mask1T"), 1)
        dve.tensor_copy(mkT[:, 0:4 * P], ps[0:E1, 6, 0:4 * P])
        dve.tensor_copy(mkT[:, 4 * P:N], ps[0:E1, 7, 0:P]).then_inc(S("mask1_rows"), 1)
        for m in range(4):
            dve.wait_ge(S("silu"), m + 1)
            dve.wait_ge(S("mask1_bc"), m + 1)
            lo = 4 + 2 * (m % 2)
            dve.tensor_tensor(two(hid1[:, m, :]), two(hid1[:, m, :]), ps[:, lo:lo + 2, 0:HALF], ALU.mult).then_inc(S("hid1"), 1)
        for t in range(T):
            lo = 2 * (t % 4)
            dve.wait_ge(S("out1_job"), t + 1)
            dve.tensor_tensor(two(x[:, t, :]), two(x[:, t, :]), ps[0:P, lo:lo + 2, 0:DH], ALU.add).then_inc(S("x_out"), 1)

    @block.tensor
    def _(pe):
        def emptied(name):
            eng, n = ring0.emptied(ring0.index[name])
            pe.wait_ge(S("num_done" if eng == "num" else "g_" + eng), n)

        def general(name):
            i = ring0.index[name]
            if i >= 2:
                eng, n = ring0.emptied(i - 2)
                pe.wait_ge(S("num_done" if eng == "num" else "g_" + eng), n)
            a, b = ring0.pair(name)
            return ps[:, a:b + 1, :]

        def bring(name):
            i = bring0.index[name]
            if i >= 2:
                eng, n = bring0.emptied(i - 2)
                if eng == "slope":
                    pe.wait_ge(S("prob_slope"), n * T)
                else:
                    pe.wait_ge(S("b_" + eng), n)
            a, b = bring0.pair(name)
            return ps[0:P, a:b + 1, 0:HALF]

        def as_rows(dst, cols, t):
            return pe.transpose(dst[0:RPAD, t // 4, (t % 4) * P:(t % 4 + 1) * P], cols[:, t, :], ident[0:P, 0:P])

        def spread(dst, pick, r):
            for half in range(2):
                last = pe.matmul(dst[:, half, :], pick[:, r:r + 1].broadcast_to([2 * RPAD, P]),
                                 rows[:, half * HALF:(half + 1) * HALF], start=True, stop=True)
            return last

        def project_tok(dst, actT, w, t):
            for half in range(2):
                for k in range(KT):
                    last = pe.matmul(dst[0:P, half, 0:DH], actT[:, k, t * P:(t + 1) * P], w[:, k, half * DH:(half + 1) * DH],
                                     start=k == 0, stop=k == KT - 1)
            return last

        def weights(name):
            i = W_INDEX[name]
            pe.wait_ge(S(f"w_in{i % 2}"), 16 * (i // 2 + 1))
            return wslot[i % 2]

        pe.sem_inc(S("edge_used"), NSLOT)
        pe.wait_ge(S("ident"), 1)
        for st in steps0:
            k, a = st[0], st[1:]
            if k == "ln":
                for t in range(T):
                    dst = general(("lnT", t))
                    pe.wait_ge(S("xn_tok"), t + 1)
                    for j in range(KT):
                        last = pe.transpose(dst[:, j // 3, (j % 3) * P:(j % 3 + 1) * P], xn[:, t, j * 128:(j + 1) * 128],
                                            ident[0:P, 0:P])
                    last.then_inc(S("pe_job"), 1)
            elif k == "h":
                l, t = a
                dst = general(st)
                emptied(("lnT", t) if l == 1 else ("x1T", t))
                if l == 1:
                    emptied(("lnT", max(t - 1, 0)))
                project_tok(dst, xnT if l == 1 else x1T, weights(f"W{l}"), t).then_inc(S("pe_job"), 1)
            elif k == "edges":
                emptied(("h", 1, T - 1))
                emptied(("h", 1, T - 2))

                def count(n, b, g, first=False, last=False):
                    pe.wait_ge(S("edge_hot"), n + 1)
                    for t in range(T):
                        if first:
                            pe.wait_ge(S("count_copied"), g * T + t + 1)
                        for r in range(SLOT):
                            ins = pe.matmul(ps[0:P, t, 0:HALF], shot[b][:, r, t * P:(t + 1) * P], dhot[b][:, r, :],
                                            start=first and r == 0, stop=last and r == SLOT - 1)
                        if t == T - 1:
                            ins.then_inc(S("edge_used"), 1)
                        elif last:
                            ins.then_inc(S("edge_tile"), 1)

                with pe.Fori(0, G_EDGE) as g:
                    for i in range(SPG):
                        count(g * SPG + i, i % NSLOT, g, first=i == 0, last=i == SPG - 1)
                pe.wait_ge(S("count_copied"), (G_EDGE + 1) * T)
            elif k == "mask":
                t = a[0]
                if t == 0:
                    pe.wait_ge(S("count_ready"), T)
                dst = general(st)
                for s in range(T):
                    last = pe.transpose(dst[0:P, s // 3, (s % 3) * P:(s % 3 + 1) * P], cnt[:, s, t * P:(t + 1) * P],
                                        ident[0:P, 0:P])
                last.then_inc(S("pe_job"), 1)
            elif k in ("logit", "shift"):
                l = a[0]
                name = (k + "T", l)
                dst = general(name)
                pe.wait_ge(S(k + "_cols"), l)
                for t in range(T):
                    last = as_rows(dst, logit, t)
                last.then_inc(S("pe_job"), 1)
            elif k == "asmax":
                l, h = a
                dst = bring(st)
                emptied(("logitT", l))
                spread(dst, pick[0], h).then_inc(S("pe_bjob"), 1)
            elif k == "bc":
                l, h, part = a
                emptied(("shiftT", l))
                dst = bring(("prob", l, h, part))
                spread(dst, pick[0], (2 + part) * H0 + h).then_inc(S("pe_bjob"), 1)
            elif k == "q":
                w = weights("Wq")
                dst = general(st)
                for half in range(2):
                    for c in range(KT):
                        last = pe.matmul(dst[:, half, 0:HALF], w[:, c, a[0] * 128:(a[0] + 1) * 128],
                                         xnT[:, c, half * HALF:(half + 1) * HALF], start=c == 0, stop=c == KT - 1)
                last.then_inc(S("pe_job"), 1)
            elif k in ("k", "v"):
                project_tok(general(st), xnT, weights("W" + k), a[0]).then_inc(S("pe_job"), 1)
            elif k == "agg":
                l, h = a
                j = prob_steps.index(("prob", l, h))
                pe.wait_ge(S("prob_ready"), (j + 1) * T)
                if h == 0:
                    emptied(("h", l, T - 1))
                for g, group in enumerate(AGG_GROUPS):
                    dst = general(("agg", l, h, g))
                    for i, t in enumerate(group):
                        for s in range(T):
                            last = pe.matmul(dst[0:P, i // 2, (i % 2) * AUG0:(i % 2 + 1) * AUG0], probs[j % 2][:, s, t * P:(t + 1) * P], haug[:, s, h, :],
                                             start=s == 0, stop=s == T - 1)
                    last.then_inc(S("pe_job"), 1)
            elif k == "relu":
                emptied(("agg", 1, H0 - 1, len(AGG_GROUPS) - 1))
                for t in range(T):
                    dst = general(("x1T", t))
                    for j in range(KT):
                        last = pe.transpose(dst[:, j // 3, (j % 3) * P:(j % 3 + 1) * P], x1[:, t, j * 128:(j + 1) * 128],
                                            ident[0:P, 0:P])
                    last.then_inc(S("pe_job"), 1)
            elif k == "kv":
                p = a[0]
                if p == 0:
                    pe.wait_ge(S("phi_done"), len(phis))
                    emptied(("v", T - 1))
                dst = general(st)
                pair = slice(p * 128, (p + 1) * 128)
                for t in range(T):
                    pe.matmul(dst[:, 0, 0:128], kk[:, t, pair], vv[:, t, pair], start=t == 0, stop=t == T - 1)
                for t in range(T):
                    last = pe.matmul(dst[:, 1, 0:128], kk[:, t, pair], haug[:, 0, 0, C0:AUG0].broadcast_to([P, 128]),
                                     start=t == 0, stop=t == T - 1)
                last.then_inc(S("pe_job"), 1)
            elif k == "mix":
                p = a[0]
                if p == 0:
                    emptied(("kv", KT - 1))
                for name, w in (("den", ksb), ("num", kvb)):
                    dst = general((name, p))
                    for half in range(2):
                        last = pe.matmul(dst[:, half, 0:HALF], w[:, p, :], qT[:, p, half * HALF:(half + 1) * HALF],
                                         start=True, stop=True)
                    last.then_inc(S("pe_job"), 1)
            elif k == "out":
                emptied(("num", KT - 1))
                project_tok(general(st), qT, weights("Wo"), a[0]).then_inc(S("pe_job"), 1)

        for t in range(T):
            a = 4 + 2 * (t % 2)
            pe.wait_ge(S("xn_tok"), T + t + 1)
            if t >= 2:
                pe.wait_ge(S("xl1"), t - 1)
            for j in range(KT):
                last = pe.transpose(ps[:, a + j // 3, (j % 3) * P:(j % 3 + 1) * P], xn2[:, t, j * 128:(j + 1) * 128],
                                    ident[0:P, 0:P])
            last.then_inc(S("lnT1"), 1)
        pe.wait_ge(S("xl1"), T)
        pe.wait_ge(S("router_lo"), 1)
        pe.wait_ge(S("pads"), 2)
        for k in range(KT):
            for n, (w, xx) in enumerate([(rwh, xh), (rwh, xl), (rwl, xh)]):
                for half in range(2):
                    last = pe.matmul(ps[0:NEXP0, 4 + half, 0:HALF], w[:, k, :], xx[:, k, half * HALF:(half + 1) * HALF],
                                     start=(k == 0 and n == 0), stop=(k == KT - 1 and n == 2))
        last.then_inc(S("router_job"), 1)

        def router_tokens():
            pe.wait_ge(S("router_rows"), 1)
            for t in range(T):
                last = pe.transpose(ps[0:P, 6, t * NEXP0:(t + 1) * NEXP0], rrow[:, t * P:(t + 1) * P], ident[0:NEXP0, 0:NEXP0])
            last.then_inc(S("router_job"), 1)

        def up(c, b, first=False):
            pe.wait_ge(S("w1_lo"), c + 1)
            for j in range(2):
                if first and j:
                    router_tokens()
                if not first:
                    pe.wait_ge(S("gelu"), 2 * c + j - 1)
                m = slice(j * 128, (j + 1) * 128)
                for k in range(KT):
                    for w, xs in ((w1hi[b], (xh, xl)), (w1lo[b], (xh,))):
                        for xx in xs:
                            for half in range(2):
                                last = pe.matmul(ps[:, 2 * j + half, 0:HALF], w[:, k, m], xx[:, k, half * HALF:(half + 1) * HALF],
                                                 start=(k == 0 and w is w1hi[b] and xx is xh),
                                                 stop=(k == KT - 1 and w is w1lo[b]))
                last.then_inc(S("hid_job"), 1)

        def down(c, b):
            pe.wait_ge(S("hid_lo"), 2 * c + 2)
            pe.wait_ge(S("w2_lo"), c + 1)
            for t in range(T):
                a = 4 + 2 * ((T * b + t) % 2)
                pe.wait_ge(S("out_added"), T * c + t + 1)
                cols = slice(t * P, (t + 1) * P)
                for j in range(2):
                    for hh, ws in ((hidh[b], (w2hi[b], w2lo[b])), (hidl[b], (w2hi[b],))):
                        for w in ws:
                            for half in range(2):
                                last = pe.matmul(ps[0:P, a + half, 0:DH], hh[:, j, cols], w[:, j, half * DH:(half + 1) * DH],
                                                 start=(j == 0 and hh is hidh[b] and w is w2hi[b]),
                                                 stop=(j == 1 and hh is hidl[b]))
                last.then_inc(S("out_job"), 1)

        pe.sem_inc(S("out_job"), T)
        up(0, 0, first=True)
        with pe.Fori(0, NCH // 2 - 1) as i:
            for b in range(2):
                c = i * 2 + b
                up(c + 1, 1 - b)
                down(c, b)
        up(NCH - 1, 1)
        down(NCH - 2, 0)
        down(NCH - 1, 1)

        def emptied1(name):
            eng, n = ring1.emptied(ring1.index[name])
            pe.wait_ge(S("g1_" + eng), n)

        def general1(name):
            i = ring1.index[name]
            if i >= 2:
                eng, n = ring1.emptied(i - 2)
                pe.wait_ge(S("g1_" + eng), n)
            a, b = ring1.pair(name)
            return ps[:, a:b + 1, :]

        def bring_1(name):
            i = bring1.index[name]
            if i >= 2:
                eng, n = bring1.emptied(i - 2)
                if eng == "slope":
                    pe.wait_ge(S("prob_slope1"), n * T)
                else:
                    pe.wait_ge(S("b1_" + eng), n)
            a, b = bring1.pair(name)
            return ps[0:P, a:b + 1, 0:HALF]

        def weights1(i):
            pe.wait_ge(S(f"w_in{i % 2}"), 16 * (3 + i // 2 + 1))
            return wslot[i % 2]

        def transposed(dst, src, t):
            for j in range(KT):
                last = pe.transpose(dst[:, j // 3, (j % 3) * P:(j % 3 + 1) * P], src[:, t, j * 128:(j + 1) * 128],
                                    ident[0:P, 0:P])
            return last

        def dash(dst, srcT, j):
            for i, (h, t) in enumerate(units(j)):
                last = pe.matmul(dst[0:P, i // 2, (i % 2) * M1:(i % 2 + 1) * M1], srcT[:, h // 2, t * P:(t + 1) * P],
                                 projT[:, h % 2, :], start=True, stop=True)
            return last

        for st in steps1:
            k, a = st[0], st[1:]
            if k == "ln":
                for t in range(T):
                    dst = general1(("lnT", t))
                    pe.wait_ge(S("xn_tok"), 2 * T + t + 1)
                    transposed(dst, xn3, t).then_inc(S("pe_job1"), 1)
                pe.wait_ge(S("count1"), T)
                for t in range(T):
                    last = pe.transpose(ps[0:P, 4 + t // 4, (t % 4) * P:(t % 4 + 1) * P], cnt[:, t, t * P:(t + 1) * P],
                                        ident[0:P, 0:P])
                last.then_inc(S("diag_job"), 1)
            elif k == "ft":
                t, g = a
                if t == 0:
                    pe.wait_ge(S("gat1_in"), 16 * 7)
                    emptied1(("lnT", T - 1))
                    emptied1(("lnT", T - 2))
                dst = general1(st)
                for q_ in range((4, 2)[g]):
                    c = 4 * g + q_
                    last = pe.matmul(dst[0:P, q_ // 2, (q_ % 2) * 256:(q_ % 2 + 1) * 256], xnT[:, c, t * P:(t + 1) * P],
                                     wblk[:, :], start=True, stop=True)
                last.then_inc(S("pe_job1"), 1)
            elif k == "logit":
                dst = general1(("wal",))
                pe.matmul(dst[:, 0, 0:2 * H1], wpair[:, :], attn[:, :], start=True, stop=True).then_inc(S("pe_job1"), 1)
                dst = general1(("logitT",))
                emptied1(("wal",))
                for half in range(2):
                    for c in range(KT):
                        last = pe.matmul(dst[0:RPAD, half, 0:HALF], wab[:, c, :], xnT[:, c, half * HALF:(half + 1) * HALF],
                                         start=c == 0, stop=c == KT - 1)
                last.then_inc(S("pe_job1"), 1)
                dst = general1(("logit",))
                pe.wait_ge(S("logit_rows"), 1)
                for t in range(T):
                    last = pe.transpose(dst[0:P, 0, t * RPAD:(t + 1) * RPAD], lrow[:, t * P:(t + 1) * P], ident[0:RPAD, 0:RPAD])
                last.then_inc(S("pe_job1"), 1)
            elif k == "shift":
                dst = general1(("shiftT",))
                pe.wait_ge(S("shift1"), 1)
                for t in range(T):
                    last = as_rows(dst, shiftb, t)
                last.then_inc(S("pe_job1"), 1)
            elif k in ("asmax", "bc"):
                h = a[0]
                emptied1(("logitT",) if k == "asmax" else ("shiftT",))
                if k == "asmax" and h == 0:
                    pe.wait_ge(S("far1"), 1)
                name, r = (st, h) if k == "asmax" else (("prob", h, a[1]), H1 * a[1] + h)
                dst = bring_1(name)
                spread(dst, pick[1], r).then_inc(S("pe_bjob1"), 1)
            elif k in ("q", "k"):
                m = a[0]
                w = weights1(0 if k == "q" else 1)
                dst = general1(st)
                for half in range(2):
                    for c in range(KT):
                        last = pe.matmul(dst[:, half, 0:HALF], w[:, c, m * 128:(m + 1) * 128],
                                         xnT[:, c, half * HALF:(half + 1) * HALF], start=c == 0, stop=c == KT - 1)
                last.then_inc(S("pe_job1"), 1)
            elif k == "sq":
                dst = general1(st)
                emptied1(a)
                n = sq_jobs.index(st)
                for t in range(T):
                    last = pe.matmul(dst[0:P, 0, 2 * t:2 * t + 2], sq[n % 2][:, t * P:(t + 1) * P], halves[:, :], start=True, stop=True)
                last.then_inc(S("pe_job1"), 1)
            elif k == "v":
                project_tok(general1(st), xnT, weights1(2), a[0]).then_inc(S("pe_job1"), 1)
            elif k == "agg":
                h = a[0]
                pe.wait_ge(S("prob_ready1"), (h + 1) * T)
                pe.wait_ge(S("ft_ones"), 1)
                dst = general1(st)
                for half in range(2):
                    for s in range(T):
                        last = pe.matmul(dst[0:AUG1, half, 0:HALF], ft[:, s, h, :], probs[h % 2][:, s, half * HALF:(half + 1) * HALF],
                                         start=s == 0, stop=s == T - 1)
                last.then_inc(S("pe_job1"), 1)
            elif k == "tok":
                dst = general1(st)
                emptied1(("agg", a[0]))
                for t in range(T):
                    last = pe.transpose(dst[0:P, 0, t * AUG1:(t + 1) * AUG1], aggT[:, t * P:(t + 1) * P], ident[0:AUG1, 0:AUG1])
                last.then_inc(S("pe_job1"), 1)
            elif k in ("kmax", "qmax"):
                pe.wait_ge(S("proj_in"), 32)
                dash(general1(st), k1T if k == "kmax" else q1T, a[0]).then_inc(S("pe_job1"), 1)
            elif k == "kstab":
                dst = general1(st)
                pe.wait_ge(S("kmax_head"), 1)
                pe.transpose(dst[0:H1, 0, 0:P], kmaxh[:, :], ident[0:P, 0:P]).then_inc(S("pe_job1"), 1)
            elif k == "kstabs":
                dst = general1(st)
                emptied1(("kstab",))
                pe.matmul(dst[0:P, 0, 0:H1], gmax[:, :].broadcast_to([H1, P]), ident[0:H1, 0:H1], start=True,
                          stop=True).then_inc(S("pe_job1"), 1)
            elif k == "ctx":
                h = a[0]
                i = cring.index[st]
                if i >= 2:
                    pe.wait_ge(S("ctx_ready"), i - 1)
                else:
                    pe.wait_ge(S("prob_slope1"), H1 * T)
                pe.wait_ge(S("kp_ready"), (T * (h + 1) - 1) // UPJ + 1)
                for t in range(T):
                    last = pe.matmul(ps[0:AUG1, cring.pair(st)[0], 0:M1], v1[:, t, h, :], kp[(T * h + t) // UPJ][:, (T * h + t) % UPJ, :],
                                     start=t == 0, stop=t == T - 1)
                last.then_inc(S("pe_cjob"), 1)
            elif k == "ctxt":
                h = a[0]
                pe.wait_ge(S("ctx_ready"), max(cring.index[st] - 1, cring.index[("ctx", h)] + 1))
                for m in range(2):
                    last = pe.transpose(ps[:, cring.pair(st)[0], m * AUG1:(m + 1) * AUG1], ctxT[h % 2][:, m * 128:(m + 1) * 128],
                                        ident[0:AUG1, 0:AUG1])
                last.then_inc(S("pe_cjob"), 1)
            elif k == "qrow":
                dst = general1(st)
                pe.wait_ge(S("q_cols"), 1)
                for t in range(T):
                    last = as_rows(dst, acol, t)
                last.then_inc(S("pe_job1"), 1)
            elif k == "dash":
                h, m = a
                dst = general1(st)
                emptied1(("qrow",))
                for half in range(2):
                    cols = slice(half * HALF, (half + 1) * HALF)
                    pe.matmul(dst[:, half, 0:HALF], projT[:, h % 2, m * 128:(m + 1) * 128], q1T[:, h // 2, cols], start=True, stop=False)
                    last = pe.matmul(dst[:, half, 0:HALF], pick[1][:, h:h + 1].broadcast_to([2 * RPAD, 128]), rows[:, cols],
                                     start=False, stop=True)
                last.then_inc(S("pe_job1"), 1)
            elif k == "mo":
                h = a[0]
                pe.wait_ge(S("qp_ready0"), h + 1)
                pe.wait_ge(S("qp_ready1"), h + 1)
                pe.wait_ge(S("ctx_ready"), 2 * H1)
                if h >= 2:
                    pe.wait_ge(S("den_copied"), h - 1)
                    pe.wait_ge(S("num_copied"), h - 1)
                for half in range(2):
                    for m in range(2):
                        last = pe.matmul(ps[:, mo_bank(h) + half, 0:HALF], ctx[:, h, m, :],
                                         qp[h % 3][:, m, half * HALF:(half + 1) * HALF], start=m == 0, stop=m == 1)
                last.then_inc(S("pe_ojob"), 1)
            elif k == "wo":
                t = a[0]
                dst = general1(st)
                w = weights1(3)
                for c in range(KT):
                    pe.wait_ge(S("mo_ready"), c + 1)
                    for half in range(2):
                        last = pe.matmul(dst[0:P, half, 0:DH], moT[:, c, t * P:(t + 1) * P], w[:, c, half * DH:(half + 1) * DH],
                                         start=c == 0, stop=c == KT - 1)
                last.then_inc(S("pe_job1"), 1)
        for t in range(T):
            lo = 4 + 2 * (t % 2)
            pe.wait_ge(S("xn_tok"), 3 * T + t + 1)
            if t >= 2:
                pe.wait_ge(S("xl1"), T + t - 1)
            transposed(ps[:, lo:lo + 2, :], xn4, t).then_inc(S("lnT1"), 1)
        pe.wait_ge(S("xl1"), 2 * T)
        pe.wait_ge(S("pads4"), 2)
        pe.wait_ge(S("f1_lo"), 2)
        for c in range(KT):
            for n, (w, xx) in enumerate([(r1h, xh), (r1h, xl), (r1l, xh)]):
                for half in range(2):
                    last = pe.matmul(ps[0:E1, 4 + half, 0:HALF], w[:, c, :], xx[:, c, half * HALF:(half + 1) * HALF],
                                     start=(c == 0 and n == 0), stop=(c == KT - 1 and n == 2))
        last.then_inc(S("router1_job"), 1)

        def hidden(m):
            lo = 2 * (m % 2)
            if m >= 2:
                pe.wait_ge(S("silu"), m - 1)
            for c in range(KT):
                for n, (w, xx) in enumerate([(f1h, xh), (f1h, xl), (f1l, xh)]):
                    for half in range(2):
                        last = pe.matmul(ps[:, lo + half, 0:HALF], w[:, c, 2 * m:2 * m + 2, :].rearrange("p e i -> p (e i)"),
                                         xx[:, c, half * HALF:(half + 1) * HALF],
                                         start=(c == 0 and n == 0), stop=(c == KT - 1 and n == 2))
            last.then_inc(S("hid1_job"), 1)

        hidden(0)
        pe.wait_ge(S("router1_rows"), 1)
        for t in range(T):
            last = pe.transpose(ps[0:P, 6, t * E1:(t + 1) * E1], rrow1[:, t * P:(t + 1) * P], ident[0:E1, 0:E1])
        last.then_inc(S("router1_job"), 1)
        hidden(1)
        hidden(2)
        pe.wait_ge(S("mask1"), 1)
        for t in range(T):
            last = pe.transpose(ps[0:E1, 6 + t // 4, (t % 4) * P:(t % 4 + 1) * P], mk[:, t, :], ident[0:P, 0:P])
        last.then_inc(S("mask1T"), 1)
        hidden(3)
        pe.wait_ge(S("mask1_rows"), 1)
        for m in range(4):
            lo = 4 + 2 * (m % 2)
            if m >= 2:
                pe.wait_ge(S("hid1"), m - 1)
            for half in range(2):
                last = pe.matmul(ps[:, lo + half, 0:HALF],
                                 sel1[:, m * 128:(m + 1) * 128],
                                 mkT[:, half * HALF:(half + 1) * HALF], start=True, stop=True)
            last.then_inc(S("mask1_bc"), 1)
        pe.wait_ge(S("hid1"), 4)
        for t in range(T):
            lo = 2 * (t % 4)
            if t >= 4:
                pe.wait_ge(S("x_out"), t - 3)
            for half in range(2):
                for m in range(4):
                    last = pe.matmul(ps[0:P, lo + half, 0:DH], hid1[:, m, t * P:(t + 1) * P], f2[:, m, half * DH:(half + 1) * DH],
                                     start=m == 0, stop=m == 3)
            last.then_inc(S("out1_job"), 1)

    block.__exit__(None, None, None)


_INS = ["x", "src", "dst", "L0_gnn_W1", "L0_gnn_a_src1", "L0_gnn_a_dst1", "L0_gnn_b1", "L0_gnn_W2", "L0_gnn_a_src2",
        "L0_gnn_a_dst2", "L0_gnn_b2", "L0_mix_W_qkv", "L0_mix_W_out", "L0_mix_b_out", "L0_ffn_w1", "L0_ffn_w2",
        "L1_gnn_W", "L1_mix_Wq", "L1_mix_Wk", "L1_mix_Wv", "L1_mix_Wo", "L1_ffn_w1"]


def lay_out(inputs):
    arrays = {n: np.asarray(inputs[n]) for n in _INS}
    for n in ("L0_gnn_a_src1", "L0_gnn_a_dst1", "L0_gnn_a_src2", "L0_gnn_a_dst2"):
        arrays[n] = arrays[n].reshape(-1)
    arrays["L0_ffn_router_wT"] = np.asarray(inputs["L0_ffn_router_w"]).T
    arrays["L1_gnn_WT"] = np.asarray(inputs["L1_gnn_W"]).T
    arrays["L1_gnn_W_resT"] = np.asarray(inputs["L1_gnn_W_res"]).T
    arrays["L1_gnn_attnT"] = np.concatenate([np.asarray(inputs["L1_gnn_attn_l"])[0], np.asarray(inputs["L1_gnn_attn_r"])[0]]).T
    arrays["L1_mix_projT"] = np.asarray(inputs["L1_mix_proj"]).T
    arrays["L1_ffn_router_wT"] = np.asarray(inputs["L1_ffn_router_w"]).T
    arrays["L1_ffn_w2"] = np.asarray(inputs["L1_ffn_w2"]).reshape(E1 * I1, D)
    return {n: np.ascontiguousarray(a) for n, a in arrays.items()}


def kernel(**inputs):
    import concourse.bacc as bacc
    from concourse.bass_utils import run_bass_kernel_spmd

    nc = bacc.Bacc("TRN2", target_bir_lowering=False, num_devices=1)
    arrays = lay_out(inputs)
    dram = {n: nc.dram_tensor("in_" + n, a.shape, mybir.dt.from_np(a.dtype), kind="ExternalInput").ap() for n, a in arrays.items()}
    result = nc.dram_tensor("out_x", [N, D], FP32, kind="ExternalOutput").ap()
    build(nc, dram, {"out": result})
    r = run_bass_kernel_spmd(nc, [{"in_" + n: a for n, a in arrays.items()}], core_ids=[0])
    return r.results[0]["out_x"]
```
